# Optimizing a Trainium2 kernel written in Bass

```python
import numpy as np
import jax
import jax.numpy as jnp

def _softmax(x, axis=-1):
    return jax.nn.softmax(x, axis=axis)

def _gelu(x):
    return jax.nn.gelu(x, approximate=True)

def _silu(x):
    return jax.nn.silu(x)

def _sigmoid(x):
    return jax.nn.sigmoid(x)

def _layernorm(x, axis=-1, eps=1e-05):
    m = jnp.mean(x, axis=axis, keepdims=True)
    v = jnp.var(x, axis=axis, keepdims=True)
    return (x - m) / jnp.sqrt(v + eps)

def _scatter_add(tgt, idx, src, axis=0):
    return tgt.at[idx].add(src)

def _segment_sum(src, seg, n):
    return jax.ops.segment_sum(src, seg, n)
kernel_name = 'mk_decoder_postln_d1_seqx_r8_776ae2'

def setup_inputs(seed: int=0):
    np.random.seed(seed)
    _w = jnp.asarray

    def _rec_inputs():
        import jax
        import jax.numpy as jnp
        _rk = jax.random.key(seed)
        x = 7.22e-05 + 1 * jax.random.normal(jax.random.fold_in(_rk, 1), (4, 256, 128), jnp.float32)
        _lenS = 256 - jax.random.randint(jax.random.fold_in(_rk, 7), (4,), 0, max(1, 256 // 4) + 1, jnp.int32)
        _lenS2 = 1601 - jax.random.randint(jax.random.fold_in(_rk, 8), (4,), 0, max(1, 1601 // 4) + 1, jnp.int32)
        _ctx_768P = jax.random.normal(jax.random.fold_in(_rk, 11), (4, 16, 96), jnp.float32)
        _ctx_768c = jax.random.dirichlet(jax.random.fold_in(_rk, 511), 0.3 * jnp.ones((16,), jnp.float32), (4, 1601))
        _ctx_768t = jnp.einsum('bsk,bkd->bsd', _ctx_768c, _ctx_768P)
        _ctx_768t = _ctx_768t * jax.lax.rsqrt(jnp.mean(jnp.square(_ctx_768t)) + 1e-12) * 0.953939
        ctx_768 = 3.88148e-05 + 0.999967 * (_ctx_768t + 0.3 * jax.random.normal(jax.random.fold_in(_rk, 611), (4, 1601, 96), jnp.float32))
        _validS = jnp.arange(256)[None, :] < _lenS[:, None]
        _validS2 = jnp.arange(1601)[None, :] < _lenS2[:, None]
        _causal = jnp.tril(jnp.ones((256, 256), dtype=bool))
        mask_BxS_bf1 = jnp.ones((4, 256), dtype=bool)
        mask_BxS2_bf1 = jnp.ones((4, 1601), dtype=bool)
        return (x, ctx_768, mask_BxS_bf1, mask_BxS2_bf1)
    x, ctx_768, mask_BxS_bf1, mask_BxS2_bf1 = _rec_inputs()

    def _L0_attn_setup():
        import jax, jax.numpy as jnp
        import numpy as np
        D_MODEL, D_INNER, D_STATE, D_CONV = (128, 256, 16, 4)
        LN_EPS = 1e-05

        def _mamba_forward(x, ln_gamma, ln_beta, W_in, conv_w, conv_b, W_x, w_dt, b_dt, A_log, D_param, W_out):
            residual = x
            B, T, _ = x.shape
            mu = x.mean(-1, keepdims=True)
            var = ((x - mu) ** 2).mean(-1, keepdims=True)
            xn = (x - mu) / jnp.sqrt(var + LN_EPS) * ln_gamma + ln_beta
            xz = xn @ W_in.T
            xb, z = jnp.split(xz, 2, axis=-1)
            xp = jnp.pad(xb, ((0, 0), (D_CONV - 1, 0), (0, 0)))
            xc = conv_b + sum((xp[:, k:k + T, :] * conv_w[:, k] for k in range(D_CONV)))
            xc = jax.nn.silu(xc)
            ssm_p = xc @ W_x.T
            dt_raw = ssm_p[..., :1]
            Bp = ssm_p[..., 1:1 + D_STATE]
            Cp = ssm_p[..., 1 + D_STATE:]
            dt = jax.nn.softplus(dt_raw @ w_dt.T + b_dt)
            A = -jnp.exp(A_log)

            def step(h, inp):
                dt_t, x_t, B_t, C_t = inp
                A_bar = jnp.exp(dt_t[:, :, None] * A[None])
                h = A_bar * h + (dt_t * x_t)[:, :, None] * B_t[:, None, :]
                y_t = jnp.einsum('bdn,bn->bd', h, C_t)
                return (h, y_t)
            h0 = jnp.zeros((B, D_INNER, D_STATE), x.dtype)
            xs = (jnp.swapaxes(dt, 0, 1), jnp.swapaxes(xc, 0, 1), jnp.swapaxes(Bp, 0, 1), jnp.swapaxes(Cp, 0, 1))
            _, ys = jax.lax.scan(step, h0, xs)
            y = jnp.swapaxes(ys, 0, 1)
            y = y + D_param * xc
            y = y * jax.nn.silu(z)
            return residual + y @ W_out.T
        key = jax.random.key(seed)
        ks = jax.random.split(key, 8)
        B, T = (2, 128)
        s = 0.02
        A = jnp.broadcast_to(jnp.arange(1, D_STATE + 1, dtype=jnp.float32), (D_INNER, D_STATE))
        return {'x': jax.random.normal(ks[0], (B, T, D_MODEL), jnp.float32), 'ln_gamma': jnp.ones((D_MODEL,), jnp.float32), 'ln_beta': jnp.zeros((D_MODEL,), jnp.float32), 'W_in': jax.random.normal(ks[1], (2 * D_INNER, D_MODEL), jnp.float32) * s, 'conv_w': jax.random.normal(ks[2], (D_INNER, D_CONV), jnp.float32) * s, 'conv_b': jnp.zeros((D_INNER,), jnp.float32), 'W_x': jax.random.normal(ks[3], (2 * D_STATE + 1, D_INNER), jnp.float32) * s, 'w_dt': jax.random.normal(ks[4], (D_INNER, 1), jnp.float32) * s, 'b_dt': jnp.zeros((D_INNER,), jnp.float32), 'A_log': jnp.log(A), 'D_param': jnp.ones((D_INNER,), jnp.float32), 'W_out': jax.random.normal(ks[5], (D_MODEL, D_INNER), jnp.float32) * s}
    _L0_attn_all = _L0_attn_setup()
    _L0_attn_in = {k: v for k, v in _L0_attn_all.items() if k in ('ln_gamma', 'ln_beta', 'W_in', 'conv_w', 'conv_b', 'W_x', 'w_dt', 'b_dt', 'A_log', 'D_param', 'W_out')}
    del _L0_attn_all

    def _L0_xattn_setup():
        import jax, jax.numpy as jnp
        import numpy as np
        B, T, DT, G, DV = (16, 64, 128, 72, 96)
        H, DH = (4, 32)
        INNER = H * DH
        HID = 4 * DT
        N_STATE = 64
        K_TOP = 32

        def layernorm(x, g, b, eps=1e-05):
            m = x.mean(-1, keepdims=True)
            v = x.var(-1, keepdims=True)
            return (x - m) * jax.lax.rsqrt(v + eps) * g + b

        def s4d(x, log_dt, A_re, A_im, C_re, C_im, D_skip):
            Bb, L, D = x.shape
            dt = jnp.exp(log_dt)
            A = A_re + 1j * A_im
            C = C_re + 1j * C_im
            dtA = dt[:, None] * A
            dC = C * (jnp.exp(dtA) - 1.0) / A
            powers = jnp.exp(dtA[:, :, None] * jnp.arange(L))
            K = 2.0 * jnp.einsum('dn,dnl->dl', dC, powers).real
            n = 2 * L
            Kf = jnp.fft.rfft(K, n=n, axis=-1)
            xf = jnp.fft.rfft(x, n=n, axis=1)
            y = jnp.fft.irfft(xf * Kf.T[None], n=n, axis=1)[:, :L]
            return y + x * D_skip
        key = jax.random.key(seed)
        ks = jax.random.split(key, 16)
        s = 0.02
        inp = {'x_text': jax.random.normal(ks[0], (B, T, DT), jnp.float32), 'x_vision': jax.random.normal(ks[1], (B, G, DV), jnp.float32), 'text_mask': jnp.ones((B, T), bool), 'vision_mask': jnp.ones((B, G), bool), 'Wq': jax.random.normal(ks[2], (DT, INNER), jnp.float32) * s, 'Wk': jax.random.normal(ks[3], (DV, INNER), jnp.float32) * s, 'Wv': jax.random.normal(ks[4], (DV, DT), jnp.float32) * s, 'W_film_in': jax.random.normal(ks[5], (DT, 2 * DT), jnp.float32) * s, 'b_film_in': jnp.zeros((2 * DT,), jnp.float32), 'W_film_out': jax.random.normal(ks[6], (DT, 2 * DT), jnp.float32) * s, 'b_film_out': jnp.zeros((2 * DT,), jnp.float32), 'g_norm_in': jnp.ones((DT,), jnp.float32), 'b_norm_in': jnp.zeros((DT,), jnp.float32), 'g_norm_out': jnp.ones((DT,), jnp.float32), 'b_norm_out': jnp.zeros((DT,), jnp.float32), 'g_ffn': jnp.ones((DT,), jnp.float32), 'b_ffn': jnp.zeros((DT,), jnp.float32), 'W1': jax.random.normal(ks[7], (DT, HID), jnp.float32) * s, 'b1': jnp.zeros((HID,), jnp.float32), 'W2': jax.random.normal(ks[8], (HID, DT), jnp.float32) * s, 'b2': jnp.zeros((DT,), jnp.float32), 'log_dt': jnp.log(0.001) + jax.random.uniform(ks[9], (DT,), jnp.float32) * (jnp.log(0.1) - jnp.log(0.001)), 'A_re': -0.5 * jnp.ones((DT, N_STATE), jnp.float32), 'A_im': jnp.tile(jnp.pi * jnp.arange(N_STATE, dtype=jnp.float32), (DT, 1)), 'C_re': jax.random.normal(ks[10], (DT, N_STATE), jnp.float32) * 0.5 ** 0.5, 'C_im': jax.random.normal(ks[11], (DT, N_STATE), jnp.float32) * 0.5 ** 0.5, 'D_skip': jax.random.normal(ks[12], (DT,), jnp.float32), 'mod_gate': jnp.array(0.5, jnp.float32)}
        return inp
    _L0_xattn_all = _L0_xattn_setup()
    _L0_xattn_in = {k: v for k, v in _L0_xattn_all.items() if k in ('Wq', 'Wk', 'Wv', 'W_film_in', 'b_film_in', 'W_film_out', 'b_film_out', 'g_norm_in', 'b_norm_in', 'g_norm_out', 'b_norm_out', 'g_ffn', 'b_ffn', 'W1', 'b1', 'W2', 'b2', 'log_dt', 'A_re', 'A_im', 'C_re', 'C_im', 'D_skip', 'mod_gate')}
    del _L0_xattn_all

    def _L0_ffn_setup():
        import jax, jax.numpy as jnp
        import numpy as np
        D_MODEL = 128
        D_FF = 512
        N_EXPERTS = 8
        TOP_K = 2
        B, S = (4, 256)
        key = jax.random.key(seed)
        ks = jax.random.split(key, 8)
        std = 0.02
        x = jax.random.normal(ks[0], (B, S, D_MODEL), dtype=jnp.float32)
        router_w = jax.random.normal(ks[1], (N_EXPERTS, D_MODEL), dtype=jnp.float32) * std
        router_b = jnp.zeros((N_EXPERTS,), dtype=jnp.float32)
        w1 = jax.random.normal(ks[2], (N_EXPERTS, D_FF, D_MODEL), dtype=jnp.float32) * std
        b1 = jnp.zeros((N_EXPERTS, D_FF), dtype=jnp.float32)
        w2 = jax.random.normal(ks[3], (N_EXPERTS, D_MODEL, D_FF), dtype=jnp.float32) * std
        b2 = jnp.zeros((N_EXPERTS, D_MODEL), dtype=jnp.float32)
        return {'x': x, 'router_w': router_w, 'router_b': router_b, 'w1': w1, 'b1': b1, 'w2': w2, 'b2': b2}
    _L0_ffn_all = _L0_ffn_setup()
    _L0_ffn_in = {k: v for k, v in _L0_ffn_all.items() if k in ('router_w', 'router_b', 'w1', 'b1', 'w2', 'b2')}
    del _L0_ffn_all
    return {'x': x, 'ctx_768': ctx_768, 'mask_BxS_bf1': mask_BxS_bf1, 'mask_BxS2_bf1': mask_BxS2_bf1, 'L0_attn_ln_gamma': _L0_attn_in['ln_gamma'], 'L0_attn_ln_beta': _L0_attn_in['ln_beta'], 'L0_attn_W_in': _L0_attn_in['W_in'], 'L0_attn_conv_w': _L0_attn_in['conv_w'], 'L0_attn_conv_b': _L0_attn_in['conv_b'], 'L0_attn_W_x': _L0_attn_in['W_x'], 'L0_attn_w_dt': _L0_attn_in['w_dt'], 'L0_attn_b_dt': _L0_attn_in['b_dt'], 'L0_attn_A_log': _L0_attn_in['A_log'], 'L0_attn_D_param': _L0_attn_in['D_param'], 'L0_attn_W_out': _L0_attn_in['W_out'], 'L0_xattn_Wq': _L0_xattn_in['Wq'], 'L0_xattn_Wk': _L0_xattn_in['Wk'], 'L0_xattn_Wv': _L0_xattn_in['Wv'], 'L0_xattn_W_film_in': _L0_xattn_in['W_film_in'], 'L0_xattn_b_film_in': _L0_xattn_in['b_film_in'], 'L0_xattn_W_film_out': _L0_xattn_in['W_film_out'], 'L0_xattn_b_film_out': _L0_xattn_in['b_film_out'], 'L0_xattn_g_norm_in': _L0_xattn_in['g_norm_in'], 'L0_xattn_b_norm_in': _L0_xattn_in['b_norm_in'], 'L0_xattn_g_norm_out': _L0_xattn_in['g_norm_out'], 'L0_xattn_b_norm_out': _L0_xattn_in['b_norm_out'], 'L0_xattn_g_ffn': _L0_xattn_in['g_ffn'], 'L0_xattn_b_ffn': _L0_xattn_in['b_ffn'], 'L0_xattn_W1': _L0_xattn_in['W1'], 'L0_xattn_b1': _L0_xattn_in['b1'], 'L0_xattn_W2': _L0_xattn_in['W2'], 'L0_xattn_b2': _L0_xattn_in['b2'], 'L0_xattn_log_dt': _L0_xattn_in['log_dt'], 'L0_xattn_A_re': _L0_xattn_in['A_re'], 'L0_xattn_A_im': _L0_xattn_in['A_im'], 'L0_xattn_C_re': _L0_xattn_in['C_re'], 'L0_xattn_C_im': _L0_xattn_in['C_im'], 'L0_xattn_D_skip': _L0_xattn_in['D_skip'], 'L0_xattn_mod_gate': _L0_xattn_in['mod_gate'], 'L0_ffn_router_w': _L0_ffn_in['router_w'], 'L0_ffn_router_b': _L0_ffn_in['router_b'], 'L0_ffn_w1': _L0_ffn_in['w1'], 'L0_ffn_b1': _L0_ffn_in['b1'], 'L0_ffn_w2': _L0_ffn_in['w2'], 'L0_ffn_b2': _L0_ffn_in['b2']}

def reference(x, ctx_768, mask_BxS_bf1, mask_BxS2_bf1, L0_attn_ln_gamma, L0_attn_ln_beta, L0_attn_W_in, L0_attn_conv_w, L0_attn_conv_b, L0_attn_W_x, L0_attn_w_dt, L0_attn_b_dt, L0_attn_A_log, L0_attn_D_param, L0_attn_W_out, L0_xattn_Wq, L0_xattn_Wk, L0_xattn_Wv, L0_xattn_W_film_in, L0_xattn_b_film_in, L0_xattn_W_film_out, L0_xattn_b_film_out, L0_xattn_g_norm_in, L0_xattn_b_norm_in, L0_xattn_g_norm_out, L0_xattn_b_norm_out, L0_xattn_g_ffn, L0_xattn_b_ffn, L0_xattn_W1, L0_xattn_b1, L0_xattn_W2, L0_xattn_b2, L0_xattn_log_dt, L0_xattn_A_re, L0_xattn_A_im, L0_xattn_C_re, L0_xattn_C_im, L0_xattn_D_skip, L0_xattn_mod_gate, L0_ffn_router_w, L0_ffn_router_b, L0_ffn_w1, L0_ffn_b1, L0_ffn_w2, L0_ffn_b2):
    import jax
    import jax.numpy as jnp

    def _L0_attn_ref(x, ln_gamma, ln_beta, W_in, conv_w, conv_b, W_x, w_dt, b_dt, A_log, D_param, W_out):
        import jax, jax.numpy as jnp
        import numpy as np
        D_MODEL, D_INNER, D_STATE, D_CONV = (128, 256, 16, 4)
        LN_EPS = 1e-05

        def _mamba_forward(x, ln_gamma, ln_beta, W_in, conv_w, conv_b, W_x, w_dt, b_dt, A_log, D_param, W_out):
            residual = x
            B, T, _ = x.shape
            mu = x.mean(-1, keepdims=True)
            var = ((x - mu) ** 2).mean(-1, keepdims=True)
            xn = (x - mu) / jnp.sqrt(var + LN_EPS) * ln_gamma + ln_beta
            xz = xn @ W_in.T
            xb, z = jnp.split(xz, 2, axis=-1)
            xp = jnp.pad(xb, ((0, 0), (D_CONV - 1, 0), (0, 0)))
            xc = conv_b + sum((xp[:, k:k + T, :] * conv_w[:, k] for k in range(D_CONV)))
            xc = jax.nn.silu(xc)
            ssm_p = xc @ W_x.T
            dt_raw = ssm_p[..., :1]
            Bp = ssm_p[..., 1:1 + D_STATE]
            Cp = ssm_p[..., 1 + D_STATE:]
            dt = jax.nn.softplus(dt_raw @ w_dt.T + b_dt)
            A = -jnp.exp(A_log)

            def step(h, inp):
                dt_t, x_t, B_t, C_t = inp
                A_bar = jnp.exp(dt_t[:, :, None] * A[None])
                h = A_bar * h + (dt_t * x_t)[:, :, None] * B_t[:, None, :]
                y_t = jnp.einsum('bdn,bn->bd', h, C_t)
                return (h, y_t)
            h0 = jnp.zeros((B, D_INNER, D_STATE), x.dtype)
            xs = (jnp.swapaxes(dt, 0, 1), jnp.swapaxes(xc, 0, 1), jnp.swapaxes(Bp, 0, 1), jnp.swapaxes(Cp, 0, 1))
            _, ys = jax.lax.scan(step, h0, xs)
            y = jnp.swapaxes(ys, 0, 1)
            y = y + D_param * xc
            y = y * jax.nn.silu(z)
            return residual + y @ W_out.T
        return _mamba_forward(x, ln_gamma, ln_beta, W_in, conv_w, conv_b, W_x, w_dt, b_dt, A_log, D_param, W_out)

    def _L0_xattn_ref(x_text, x_vision, text_mask, vision_mask, Wq, Wk, Wv, W_film_in, b_film_in, W_film_out, b_film_out, g_norm_in, b_norm_in, g_norm_out, b_norm_out, g_ffn, b_ffn, W1, b1, W2, b2, log_dt, A_re, A_im, C_re, C_im, D_skip, mod_gate):
        import jax, jax.numpy as jnp
        import numpy as np
        B, T, DT, G, DV = (16, 64, 128, 72, 96)
        H, DH = (4, 32)
        INNER = H * DH
        HID = 4 * DT
        N_STATE = 64
        K_TOP = 32

        def layernorm(x, g, b, eps=1e-05):
            m = x.mean(-1, keepdims=True)
            v = x.var(-1, keepdims=True)
            return (x - m) * jax.lax.rsqrt(v + eps) * g + b

        def s4d(x, log_dt, A_re, A_im, C_re, C_im, D_skip):
            Bb, L, D = x.shape
            dt = jnp.exp(log_dt)
            A = A_re + 1j * A_im
            C = C_re + 1j * C_im
            dtA = dt[:, None] * A
            dC = C * (jnp.exp(dtA) - 1.0) / A
            powers = jnp.exp(dtA[:, :, None] * jnp.arange(L))
            K = 2.0 * jnp.einsum('dn,dnl->dl', dC, powers).real
            n = 2 * L
            Kf = jnp.fft.rfft(K, n=n, axis=-1)
            xf = jnp.fft.rfft(x, n=n, axis=1)
            y = jnp.fft.irfft(xf * Kf.T[None], n=n, axis=1)[:, :L]
            return y + x * D_skip
        Bb, Tt, D = x_text.shape
        Gg = x_vision.shape[1]
        Q = (x_text @ Wq).reshape(Bb, Tt, H, DH)
        K = (x_vision @ Wk).reshape(Bb, Gg, H, DH)
        scores = jnp.einsum('bthd,bghd->bhtg', Q, K) / np.sqrt(DH).astype(np.float32)
        scores = jnp.where(vision_mask[:, None, None, :], scores, -jnp.inf)
        topv, topi = jax.lax.top_k(scores, K_TOP)
        probs = jax.nn.softmax(topv, axis=-1)
        bi = jnp.arange(Bb)[:, None, None, None]
        hi = jnp.arange(H)[None, :, None, None]
        ti = jnp.arange(Tt)[None, None, :, None]
        attn = jnp.zeros_like(scores).at[bi, hi, ti, topi].set(probs)
        attn_mean = attn.mean(axis=1)
        V = x_vision @ Wv
        c_t = jnp.einsum('btg,bgd->btd', attn_mean, V)
        c_t = c_t * text_mask[..., None]
        x = layernorm(x_text, g_norm_in, b_norm_in)
        scale_in, shift_in = jnp.split(c_t @ W_film_in + b_film_in, 2, axis=-1)
        x = x * (1.0 + mod_gate * scale_in) + mod_gate * shift_in
        y = s4d(x, log_dt, A_re, A_im, C_re, C_im, D_skip)
        scale_out, shift_out = jnp.split(c_t @ W_film_out + b_film_out, 2, axis=-1)
        y = y * (1.0 + mod_gate * scale_out) + mod_gate * shift_out
        xt = x_text + y
        h = layernorm(xt, g_ffn, b_ffn)
        h = jax.nn.gelu(h @ W1 + b1, approximate=False) @ W2 + b2
        xt = xt + h
        return layernorm(xt, g_norm_out, b_norm_out)

    def _L0_ffn_ref(x, router_w, router_b, w1, b1, w2, b2):
        import jax, jax.numpy as jnp
        import numpy as np
        D_MODEL = 128
        D_FF = 512
        N_EXPERTS = 8
        TOP_K = 2
        B, S = (4, 256)
        Bx, Sx, D = x.shape
        E = router_b.shape[0]
        xf = x.reshape(-1, D)
        logits = xf @ router_w.T + router_b
        probs = jax.nn.softmax(logits, axis=-1)
        topk_w, topk_idx = jax.lax.top_k(probs, TOP_K)
        topk_w = topk_w / jnp.sum(topk_w, axis=-1, keepdims=True)
        onehot = jax.nn.one_hot(topk_idx, E, dtype=xf.dtype)
        w_dense = jnp.einsum('tke,tk->te', onehot, topk_w)
        out = jnp.zeros_like(xf)
        for e in range(E):
            h = jax.nn.gelu(xf @ w1[e].T + b1[e], approximate=False)
            out = out + w_dense[:, e:e + 1] * (h @ w2[e].T + b2[e])
        return out.reshape(Bx, Sx, D)
    x = _layernorm(x + _L0_attn_ref(x, L0_attn_ln_gamma, L0_attn_ln_beta, L0_attn_W_in, L0_attn_conv_w, L0_attn_conv_b, L0_attn_W_x, L0_attn_w_dt, L0_attn_b_dt, L0_attn_A_log, L0_attn_D_param, L0_attn_W_out), axis=-1)
    x = _layernorm(x + _L0_xattn_ref(x, ctx_768, mask_BxS_bf1, mask_BxS2_bf1, L0_xattn_Wq, L0_xattn_Wk, L0_xattn_Wv, L0_xattn_W_film_in, L0_xattn_b_film_in, L0_xattn_W_film_out, L0_xattn_b_film_out, L0_xattn_g_norm_in, L0_xattn_b_norm_in, L0_xattn_g_norm_out, L0_xattn_b_norm_out, L0_xattn_g_ffn, L0_xattn_b_ffn, L0_xattn_W1, L0_xattn_b1, L0_xattn_W2, L0_xattn_b2, L0_xattn_log_dt, L0_xattn_A_re, L0_xattn_A_im, L0_xattn_C_re, L0_xattn_C_im, L0_xattn_D_skip, L0_xattn_mod_gate), axis=-1)
    x = _layernorm(x + _L0_ffn_ref(x, L0_ffn_router_w, L0_ffn_router_b, L0_ffn_w1, L0_ffn_b1, L0_ffn_w2, L0_ffn_b2), axis=-1)
    return x

_drawn_inputs = setup_inputs


def setup_inputs(seed=0):
    import zlib

    import numpy as np

    out = dict(_drawn_inputs(seed))
    spreads = {'L0_attn_ln_gamma': (1.0, 0.6),
     'L0_attn_ln_beta': (0.0, 0.8),
     'L0_attn_conv_b': (0.0, 0.8),
     'L0_attn_b_dt': (0.0, 0.8),
     'L0_attn_D_param': (1.0, 0.6),
     'L0_xattn_b_film_in': (0.0, 0.382),
     'L0_xattn_b_film_out': (0.0, 0.355),
     'L0_xattn_g_norm_in': (1.0, 0.2),
     'L0_xattn_b_norm_in': (0.0, 0.1),
     'L0_xattn_g_norm_out': (1.0, 0.2),
     'L0_xattn_b_norm_out': (0.0, 0.1),
     'L0_xattn_g_ffn': (1.0, 0.6),
     'L0_xattn_b_ffn': (0.0, 2.0),
     'L0_xattn_b1': (0.0, 0.753),
     'L0_xattn_b2': (0.0, 0.8),
     'L0_xattn_A_re': (-0.5, 0.2),
     'L0_ffn_router_b': (0.0, 0.1),
     'L0_ffn_b1': (0.0, 0.464),
     'L0_ffn_b2': (0.0, 0.1)}
    factors = {'ctx_768': 4.953,
     'L0_attn_W_in': 8.0,
     'L0_attn_conv_w': 8.0,
     'L0_attn_W_x': 8.0,
     'L0_attn_w_dt': 8.0,
     'L0_attn_A_log': 8.0,
     'L0_attn_W_out': 8.0,
     'L0_xattn_Wq': 7.592,
     'L0_xattn_Wk': 8.0,
     'L0_xattn_Wv': 4.558,
     'L0_xattn_W_film_in': 5.199,
     'L0_xattn_W_film_out': 6.823,
     'L0_xattn_W1': 3.089,
     'L0_xattn_W2': 2.775}
    for name, (base, spread) in spreads.items():
        noise = np.random.default_rng([zlib.crc32(name.encode()), seed]).standard_normal(out[name].shape)
        drawn = base * np.exp(spread * noise) if base else spread * noise
        out[name] = jnp.asarray(drawn.astype(out[name].dtype))
    for name, factor in factors.items():
        out[name] = (out[name] * factor).astype(out[name].dtype)
    return out
```

```python
from contextlib import ExitStack

import numpy as np

import concourse.bass as bass
from concourse import mybir

ALU = mybir.AluOpType
ACT = mybir.ActivationFunctionType
F32 = mybir.dt.float32
BF16 = mybir.dt.bfloat16
I32 = mybir.dt.int32
U32 = mybir.dt.uint32
U8 = mybir.dt.uint8
AX = mybir.AxisListType.X

P = 128
B, T, D = 4, 256, 128
R = T // P
CH = 2
NS = 16
NU = 4
UN = NS // NU
KC = 4
G, DV = 1601, 96
GC = (G + P - 1) // P
GL = G - (GC - 1) * P
NH, DH = 4, 32
SEG = 64
NSEG = G // SEG
TOPK = 32
FT = 4
NE = 8
NST = 64
L16 = 16
NFFT = 2 * T
EPS = 1e-5
SCALE = float(np.float32(1.0) / np.sqrt(np.float32(DH)))
PENALTY = 3.0e38
LOWEST = -3.4e38

LOG1P = [2.000000000, 0.666666660, 0.400001500, 0.285600500, 0.228000000]


def log1p_coefficients():
    n = 64
    q = (np.cos(np.pi * (np.arange(n) + 0.5) / n) + 1) / 2 / 9
    s = np.sqrt(q)
    return [float(v) for v in np.polynomial.polynomial.polyfit(q, 2 * np.arctanh(s) / s, 5)]


def column_layout():
    at, n = {}, 0
    for name, width in (("ln_g", 1), ("ln_b", 1), ("conv_w", CH * KC), ("conv_b", CH), ("w_dt", CH), ("b_dt", CH),
                        ("d_param", CH), ("a_log", CH * NS), ("ffn_g", 1), ("ffn_b", 1), ("ffn_b1", FT),
                        ("moe_b1", NE * FT)):
        at[name] = (n, n + width)
        n += width
    return at, n


def row_layout():
    at, n = {}, 0
    for name, width in (("in_g", D), ("in_b", D), ("out_g", D), ("out_b", D), ("ffn_b2", D), ("film_in_b", 2 * D),
                        ("film_out_b", 2 * D), ("router_b", NE), ("gate", 1), ("log_dt", D)):
        at[name] = (n, n + width)
        n += width
    return at, n


def weight_layout():
    at, n = {}, 0
    for name, width in (("w_in", 4 * P), ("wx_bc", CH * 96), ("wx_raw", CH * P), ("w_out", CH * D), ("wq", D),
                        ("film_in", 2 * D), ("film_out", 2 * D), ("w1", FT * P), ("w2", FT * D), ("router", NE)):
        at[name] = (n, n + width)
        n += width
    return at, n


COLS, NCOLS = column_layout()
ROWS, NROWS = row_layout()
WTS, NWTS = weight_layout()
LNS = 7


def build(nc, a):
    ctx = ExitStack()
    with ctx:
        def sb(name, shape, dt=F32):
            return ctx.enter_context(nc.sbuf_tensor(name, shape, dt))

        def sem(name):
            return ctx.enter_context(nc.semaphore(name))

        cols = sb("cols", [P, NCOLS])
        rows = sb("rows", [P, NROWS])
        wts = sb("wts", [P, NWTS])
        wkv = sb("wkv", [DV, 2 * D])
        ident = sb("ident", [P, P])
        sel_c = sb("sel_c", [96, 32])
        sel = sb("sel", [96, 32], BF16)
        dft = sb("dft", [P, R, 6, P])
        idft = sb("idft", [P, 4, T])
        moe_w = sb("moe_w", [P, 2 * NE * FT * P])
        moe_w1, moe_w2 = (moe_w[:, i * NE * FT * P:(i + 1) * NE * FT * P].rearrange("p (e f m) -> p e f m", e=NE, f=FT)
                          for i in range(2))
        moe_b2 = sb("moe_b2", [NE, D])
        tmask8 = sb("tmask8", [P, B * R], U8)
        tmask = sb("tmask", [P, B, R])
        half = sb("half", [P, R])
        onesb = sb("onesb", [P, P], BF16)
        ones = sb("ones", [P, 1])
        iota8 = sb("iota8", [P, NE])
        a_neg = sb("a_neg", [P, CH * NS])
        kf = sb("kf", [P, 4, 2, D])

        x_in = sb("x_in", [P, R, D])
        stat = sb("stat", [P, LNS, R, 6])
        mv = sb("mv", [P, LNS, R, 2])
        rstd = sb("rstd", [P, LNS, R])
        xn = sb("xn", [P, R, D])
        xnT = sb("xnT", [P, T])
        cv = sb("cv", [P, CH, T])
        xc = sb("xc", [P, CH, T])
        sz = sb("sz", [P, CH, T])
        shared = sb("shared", [P, 2 * FT * T])
        sp_a, sp_p, sp_r, sp_q = (shared[:, i * CH * T:(i + 1) * CH * T].rearrange("p (c t) -> p c t", c=CH) for i in range(4))
        dt_ = sb("dt_", [P, CH, T])
        ux = sb("ux", [P, CH, T])
        parts = sb("parts", [96, T], BF16)
        bc_r = sb("bc_r", [96, T])
        bc_m = sb("bc_m", [96, T], BF16)
        area = sb("area", [P, 2 * 2 * CH * UN * T])
        abar, hst = (area[:, i * 2 * CH * UN * T:(i + 1) * 2 * CH * UN * T]
                     .rearrange("p (u c n t) -> p u c n t", u=2, c=CH, n=UN) for i in range(2))
        yv = sb("yv", [P, CH, T])
        res = sb("res", [P, R, D])
        x1 = sb("x1", [P, R, D])

        ctxT = sb("ctxT", [DV, G])
        gmask8 = sb("gmask8", [P, G], U8)
        pen = sb("pen", [P, G], BF16)
        KT = sb("KT", [P, G])
        V = sb("V", [P, GC, D])
        x1T = sb("x1T", [P, T])
        QT = sb("QT", [P, T])
        s = sb("s", [P, NH, G])
        prob = area[:, 0:NH * G].rearrange("p (k g) -> p k g", k=NH)
        cand = sb("cand", [P, NSEG, 8])
        cand2 = sb("cand2", [P, NSEG * 8])
        scratch = shared[:, 0:G]
        top = sb("top", [P, NH, TOPK])
        etop = sb("etop", [P, TOPK])
        ngmax = sb("ngmax", [P, NH])
        ssum = sb("ssum", [P, NH])
        lnsum = sb("lnsum", [P, NH])
        ebias = sb("ebias", [P, NH])
        seg8 = sb("seg8", [P, NH])
        nabove = sb("nabove", [P, NH])
        above = sb("above", [P, NSEG * 8])
        flag = sb("flag", [P, NH])
        anyf = sb("anyf", [1, 1])
        anyi = sb("anyi", [1, 1], I32)
        aT = sb("aT", [P, GC, T])
        cT = sb("cT", [P, T])

        n2 = sb("n2", [P, R, D])
        fi, fo = (area[:, NH * G + i * 512:NH * G + (i + 1) * 512].rearrange("p (r d) -> p r d", r=R) for i in range(2))
        xf_a = sb("xf_a", [P, 2, D])
        xf_b = sb("xf_b", [P, 2, D])
        Y = sb("Y", [P, 4, D])
        xt = sb("xt", [P, R, D])
        hT = sb("hT", [P, T])
        s_flat = s[:, :, :].rearrange("p k g -> p (k g)")
        gT = s_flat[:, 0:FT * T].rearrange("p (f t) -> p f t", f=FT)
        x2 = sb("x2", [P, R, D])
        x2T = sb("x2T", [P, T])
        lg = sb("lg", [P, R, NE])
        lmax = sb("lmax", [P, R, 8])
        lidx = sb("lidx", [P, R, 8], U32)
        lidf = sb("lidf", [P, R, 2])
        wtop = sb("wtop", [P, R, 4])
        oh = sb("oh", [P, R, 2, NE])
        wd = sb("wd", [P, R, NE])
        wdT = sb("wdT", [NE, T])
        gm = shared[:, :].rearrange("p (e f t) -> p e f t", e=2, f=FT)
        acc = sb("acc", [P, R, D])
        outt = sb("outt", [P, R, D])

        LD = L16 * D
        u_ph, u_ph2, u_exp, w_rnd = (moe_w[:, i * LD:(i + 1) * LD].rearrange("p (l d) -> p l d", l=L16) for i in range(4))
        w_ph, w_exp = (s_flat[:, i * LD:(i + 1) * LD].rearrange("p (l d) -> p l d", l=L16) for i in range(2))
        a_re, a_im, c_1, c_2, *sv = [s_flat[:, 2 * LD + i * D:2 * LD + (i + 1) * D] for i in range(16)]
        k16 = s_flat[0:L16, 0:LD].rearrange("p (l d) -> p l d", l=L16)
        dskip = sb("dskip", [1, D])
        steps = sb("steps", [P, 2, L16])
        ki = sb("ki", [P, D], I32)
        phase = sb("phase", [P, 2])
        kT = sb("kT", [P, R, D])

        S = ctx.enter_context(nc.psum_tensor("S", [P, 4 * 512], F32))
        M = ctx.enter_context(nc.psum_tensor("M", [P, 2, 512], F32))
        TT = ctx.enter_context(nc.psum_tensor("TT", [P, 2, 512], F32))

        def col(name, i=0):
            return cols[:, COLS[name][0] + i:COLS[name][0] + i + 1]

        def row(name):
            return rows[:, ROWS[name][0]:ROWS[name][1]]

        def wt(name, i, n):
            return wts[:, WTS[name][0] + i * n:WTS[name][0] + (i + 1) * n]

        ld_x = sem("ld_x"); ld_ctx = sem("ld_ctx"); ld_cols = sem("ld_cols"); ld_rows = sem("ld_rows")
        ld_w = sem("ld_w"); ld_small = sem("ld_small"); ld_s4 = sem("ld_s4"); ld_dft = sem("ld_dft")
        ld_moe = sem("ld_moe"); k16_moved = sem("k16_moved"); out_stored = sem("out_stored")
        pool_step = sem("pool_step"); dve_step = sem("dve_step"); act_step = sem("act_step")
        consts_set = sem("consts_set"); a_exp = sem("a_exp"); params_ready = sem("params_ready")
        s4_small = sem("s4_small"); s4_sin_in = sem("s4_sin_in"); s4_sin = sem("s4_sin")
        s4_th_in = sem("s4_th_in"); s4_gain = sem("s4_gain")
        s4_arg = sem("s4_arg"); s4_fun = sem("s4_fun"); s4_mats = sem("s4_mats"); k16_ps = sem("k16_ps")
        k16_sb = sem("k16_sb"); kT_ready = sem("kT_ready"); kf_ps = sem("kf_ps"); kf_ready = sem("kf_ready")
        var_ready = sem("var_ready"); rstd_ready = sem("rstd_ready")
        xn_ready = sem("xn_ready"); xnT_ps = sem("xnT_ps"); xnT_ready = sem("xnT_ready"); xz_ps = sem("xz_ps")
        conv_ready = sem("conv_ready"); xc_ready = sem("xc_ready"); sz_ready = sem("sz_ready"); ssm_ps = sem("ssm_ps")
        bc_hi = sem("bc_hi"); sp_ready = sem("sp_ready"); sq_in = sem("sq_in"); sq_out = sem("sq_out")
        parts_ready = sem("parts_ready"); dt_ready = sem("dt_ready"); abar_ready = sem("abar_ready")
        bc_ps = sem("bc_ps"); b_used = sem("b_used"); c_used = sem("c_used"); scan_done = sem("scan_done"); hc_ready = sem("hc_ready"); y_sum = sem("y_sum")
        yv_ready = sem("yv_ready"); op_ps = sem("op_ps"); x1_ready = sem("x1_ready"); abar_zero = sem("abar_zero"); x_used = sem("x_used")
        pen_ready = sem("pen_ready"); k_ps = sem("k_ps"); k_ready = sem("k_ready"); v_ps = sem("v_ps")
        v_ready = sem("v_ready"); x1T_ps = sem("x1T_ps"); x1T_ready = sem("x1T_ready"); q_ps = sem("q_ps")
        q_ready = sem("q_ready"); s_ps = sem("s_ps"); s_ready = sem("s_ready"); flags_ready = sem("flags_ready")
        flags_sum = sem("flags_sum"); top_ready = sem("top_ready"); esum_ready = sem("esum_ready")
        ebias_ready = sem("ebias_ready"); prob_ready = sem("prob_ready"); masked_ready = sem("masked_ready")
        avg_ready = sem("avg_ready"); aT_ps = sem("aT_ps"); aT_ready = sem("aT_ready"); c_ps = sem("c_ps")
        c_ready = sem("c_ready")
        film_ps = sem("film_ps"); xs_ready = sem("xs_ready"); xf_ps = sem("xf_ps"); Y_ready = sem("Y_ready")
        y_ps = sem("y_ps"); n3_ready = sem("n3_ready"); n3T_ps = sem("n3T_ps"); hT_ready = sem("hT_ready")
        h1_ps = sem("h1_ps"); gT_ready = sem("gT_ready"); h2_ps = sem("h2_ps"); x2_ready = sem("x2_ready")
        x2T_ps = sem("x2T_ps"); x2T_ready = sem("x2T_ready"); lg_ps = sem("lg_ps"); wd_ready = sem("wd_ready")
        wdT_ps = sem("wdT_ps"); wdT_ready = sem("wdT_ready"); mb_ps = sem("mb_ps"); acc_set = sem("acc_set")
        eh_ps = sem("eh_ps"); eg_ready = sem("eg_ready"); eo_ps = sem("eo_ps"); wexp_in = sem("wexp_in"); wexp_out = sem("wexp_out"); eo_used = sem("eo_used")
        out_ready = sem("out_ready")

        block = ctx.enter_context(nc.Block())
        C1 = log1p_coefficients()
        MAGIC = 1.5 * 2.0 ** 23
        TWO_PI = float(2 * np.pi)

        @block.sync
        def _(sp):
            sp.dma_start(cols[:, :], a["cols"]).then_inc(ld_cols, 16)
            sp.dma_start(x_in[:, :, :], a["x"][0].rearrange("(r p) d -> p r d", p=P)).then_inc(ld_x, 16)
            sp.dma_start(rows[:, :], a["rows"].to_broadcast([P, NROWS])).then_inc(ld_rows, 16)
            sp.dma_start(ident[:, :], a["ident"]).then_inc(ld_small, 16)
            sp.dma_start(sel_c[:, :], a["sel"]).then_inc(ld_small, 16)
            sp.dma_start(wkv[:, :], a["wkv"]).then_inc(ld_small, 16)
            sp.dma_start(tmask8[:, :], a["tmask"]).then_inc(ld_small, 16)
            sp.dma_start(iota8[:, :], a["iota8"].to_broadcast([P, NE])).then_inc(ld_small, 16)
            sp.dma_start(wts[:, :], a["wts"]).then_inc(ld_w, 16)
            for dst, name in ((a_re, "a_re"), (a_im, "a_im"), (c_1, "c_1"), (c_2, "c_2"), (dskip, "dskip")):
                sp.dma_start(dst[:, :], a[name]).then_inc(ld_s4, 16)
            sp.dma_start(steps[:, :, :].rearrange("p a b -> p (a b)"), a["steps"].to_broadcast([P, 2 * L16])).then_inc(ld_s4, 16)
            sp.dma_start(ctxT[:, :], a["ctxT"][0]).then_inc(ld_ctx, 16)
            sp.dma_start(gmask8[:, :], a["gmask"][0:1, :].to_broadcast([P, G])).then_inc(ld_ctx, 16)
            sp.dma_start(dft[:, :, :, :], a["dft"]).then_inc(ld_dft, 16)
            sp.dma_start(idft[:, :, :], a["idft"]).then_inc(ld_dft, 16)
            sp.wait_ge(k16_sb, 1)
            for r in range(R):
                sp.dma_start(kT[:, r, :], k16[r * 8:(r + 1) * 8, :, :]).then_inc(k16_moved, 16)
            sp.dma_start(moe_w1[:, :, :, :], a["moe_w1"]).then_inc(ld_moe, 16)
            sp.dma_start(moe_w2[:, :, :, :], a["moe_w2"]).then_inc(ld_moe, 16)
            sp.dma_start(moe_b2[:, :], a["moe_b2"]).then_inc(ld_moe, 16)
            for b in range(B):
                if b + 1 < B:
                    sp.wait_ge(x_used, b + 1)
                    sp.dma_start(x_in[:, :, :], a["x"][b + 1].rearrange("(r p) d -> p r d", p=P)).then_inc(ld_x, 16)
                    sp.wait_ge(k_ps, 4 * (b + 1))
                    sp.wait_ge(v_ps, 4 * (b + 1))
                    sp.wait_ge(pen_ready, b + 1)
                    sp.dma_start(ctxT[:, :], a["ctxT"][b + 1]).then_inc(ld_ctx, 16)
                    sp.dma_start(gmask8[:, :], a["gmask"][b + 1:b + 2, :].to_broadcast([P, G])).then_inc(ld_ctx, 16)
                sp.wait_ge(out_ready, b + 1)
                sp.dma_start(a["out"][b].rearrange("(r p) d -> p r d", p=P), outt[:, :, :]).then_inc(out_stored, 16)
            sp.wait_ge(out_stored, 16 * B)

        @block.gpsimd
        def _(pool):
            n = [0]

            def link(ins):
                n[0] += 1
                ins.then_inc(pool_step, 1)
                pool.wait_ge(pool_step, n[0])

            pool.memset(half[:, :], -0.5)
            link(pool.memset(ones[:, :], 1.0))
            link(pool.memset(onesb[:, :], 1.0))
            link(pool.memset(phase[0:64, 0:1], 0.25))
            link(pool.memset(phase[64:128, 0:1], 0.5))
            link(pool.tensor_copy(phase[:, 1:2], phase[:, 0:1]))
            pool.sem_inc(consts_set, 1)

            pool.wait_ge(s4_small, 1)
            pool.wait_ge(ld_s4, 96)
            turn, are = sv[0], sv[1]
            bc = lambda v: v.unsqueeze(1).to_broadcast([P, L16, D])
            st = lambda i: steps[:, i, :].unsqueeze(2).to_broadcast([P, L16, D])
            for ph, ex, i in ((w_ph, w_exp, 0), (u_ph, u_exp, 1)):
                pool.tensor_tensor(ex, bc(are[:, :]), st(i), ALU.mult)
                pool.tensor_tensor(ph, bc(turn[:, :]), st(i), ALU.mult).then_inc(s4_arg, 1)
            pool.wait_ge(s4_fun, 5)
            link(pool.tensor_tensor(w_ph, w_exp, w_ph, ALU.mult))
            pool.wait_ge(s4_gain, 1)
            link(pool.tensor_tensor(u_ph, u_ph, bc(sv[10][:, :]), ALU.mult))
            link(pool.tensor_tensor(u_ph2, u_ph2, bc(sv[11][:, :]), ALU.mult))
            link(pool.tensor_tensor(u_ph, u_ph, u_ph2, ALU.add))
            link(pool.tensor_tensor(u_ph, u_ph, u_exp, ALU.mult))
            pool.sem_inc(s4_mats, 1)
            def layernorm(b, k):
                pool.wait_ge(var_ready, LNS * b + k + 1)
                link(pool.tensor_scalar(rstd[:, k, :], mv[:, k, :, 1], EPS, None, ALU.add))
                pool.tensor_tensor(rstd[:, k, :], rstd[:, k, :], half[:, :], ALU.pow).then_inc(rstd_ready, 1)

            for b in range(B):
                if b >= 1:
                    pool.wait_ge(aT_ps, 4 * R * b)
                pool.memset(abar[:, :, :, :, 0:1].rearrange("p u c n t -> p (u c n) t"), 0.0).then_inc(abar_zero, 1)
                layernorm(b, 0)
                pool.wait_ge(ld_ctx, 32 * (b + 1))
                if b >= 1:
                    pool.wait_ge(s_ps, 16 * b)
                pool.tensor_scalar(pen[:, :], gmask8[:, :], PENALTY, -PENALTY, ALU.mult, ALU.add).then_inc(pen_ready, 1)
                layernorm(b, 1)
                for r in range(R):
                    pool.wait_ge(masked_ready, NH * (R * b + r) + 2)
                    link(pool.tensor_tensor(prob[:, 0, :], prob[:, 0, :], prob[:, 1, :], ALU.add))
                    pool.wait_ge(masked_ready, NH * (R * b + r) + 4)
                    link(pool.tensor_tensor(prob[:, 2, :], prob[:, 2, :], prob[:, 3, :], ALU.add))
                    pool.tensor_tensor(prob[:, 0, :], prob[:, 0, :], prob[:, 2, :], ALU.add).then_inc(avg_ready, 1)
                for k in range(2, LNS):
                    layernorm(b, k)

        @block.scalar
        def _(act):
            A = nc.scalar.activation
            n = [0]

            def link(ins):
                n[0] += 1
                ins.then_inc(act_step, 1)
                act.wait_ge(act_step, n[0])

            act.wait_ge(ld_cols, 16)
            A(a_neg[:, :], cols[:, COLS["a_log"][0]:COLS["a_log"][1]], ACT.Exp).then_inc(a_exp, 1)
            act.wait_ge(s4_sin_in, 1)
            A(sv[4][:, :], sv[4][:, :], ACT.Sin, scale=TWO_PI)
            A(sv[5][:, :], sv[5][:, :], ACT.Sin, scale=TWO_PI)
            A(sv[6][:, :], sv[6][:, :], ACT.Sin, scale=TWO_PI / 2)
            A(sv[7][:, :], sv[1][:, :], ACT.Tanh, scale=0.5).then_inc(s4_sin, 1)
            act.wait_ge(s4_th_in, 2)
            A(w_ph, w_ph, ACT.Sin, scale=TWO_PI).then_inc(s4_fun, 1)
            act.wait_ge(s4_th_in, 4)
            A(u_ph, u_ph, ACT.Sin, scale=TWO_PI).then_inc(s4_fun, 1)
            A(u_ph2, u_ph2, ACT.Sin, scale=TWO_PI).then_inc(s4_fun, 1)
            A(w_exp, w_exp, ACT.Exp).then_inc(s4_fun, 1)
            A(u_exp, u_exp, ACT.Exp).then_inc(s4_fun, 1)
            act.wait_ge(k16_ps, 1)
            A(k16[:, :, :], S[0:L16, :].rearrange("p (d j) -> p j d", j=L16), ACT.Copy).then_inc(k16_sb, 1)
            act.wait_ge(ld_small, 80)
            A(sel[:, :], sel_c[:, :], ACT.Copy).then_inc(params_ready, 1)

            def front(b):
                act.wait_ge(xnT_ps, b + 1)
                A(xnT[:, :], M[:, 0, 0:T], ACT.Identity, scale=col("ln_g"), bias=col("ln_b")).then_inc(xnT_ready, 1)
                act.wait_ge(xz_ps, 2 * b + 2)
                act.wait_ge(conv_ready, b + 1)
                A(xc[:, :, :], cv[:, :, :], ACT.Silu).then_inc(xc_ready, 1)
                A(sz[:, :, :], M[:, 1, :].rearrange("p (c t) -> p c t", c=CH), ACT.Silu).then_inc(sz_ready, 1)
                act.wait_ge(ssm_ps, 2 * b + 1)
                for c in range(CH):
                    A(sp_a[:, c, :], M[:, 0, T:2 * T], ACT.Abs, scale=col("w_dt", c), bias=col("b_dt", c))
                    link(A(sp_p[:, c, :], M[:, 0, T:2 * T], ACT.Relu, scale=col("w_dt", c), bias=col("b_dt", c)))
                A(sp_a[:, :, :], sp_a[:, :, :], ACT.Exp, scale=-1.0).then_inc(sp_ready, 1)
                act.wait_ge(ssm_ps, 2 * b + 2)
                A(parts[:, :], M[0:96, 1, 0:T], ACT.Copy).then_inc(bc_hi, 1)
                act.wait_ge(sq_in, b + 1)
                A(sp_q[:, :, :], sp_r[:, :, :], ACT.Square).then_inc(sq_out, 1)
                act.wait_ge(dt_ready, b + 1)
                act.wait_ge(abar_zero, b + 1)
                for u in range(NU):
                    for c in range(CH):
                        if u >= 2:
                            act.wait_ge(scan_done, CH * (NU * b + u - 2) + c + 1)
                        for j in range(UN):
                            i = UN * u + j
                            ins = A(abar[:, u % 2, c, j, 1:T], dt_[:, c, 1:T], ACT.Exp, scale=a_neg[:, c * NS + i:c * NS + i + 1])
                        ins.then_inc(abar_ready, 1)

            def attention(b):
                act.wait_ge(k_ps, 4 * b + 4)
                A(KT[:, :], S[:, 0:G], ACT.Copy).then_inc(k_ready, 1)
                for g in range(4):
                    act.wait_ge(v_ps, 4 * b + g + 1)
                    w = min(4, GC - 4 * g)
                    rows_ = P if w == 4 else GL
                    A(V[0:rows_, 4 * g:4 * g + w, :], M[0:rows_, g % 2, 0:w * D].rearrange("p (g d) -> p g d", d=D),
                      ACT.Copy).then_inc(v_ready, 1)
                act.wait_ge(x1T_ps, b + 1)
                A(x1T[:, :], M[:, 0, 0:T], ACT.Copy).then_inc(x1T_ready, 1)
                act.wait_ge(q_ps, b + 1)
                A(QT[:, :], M[:, 1, 0:T], ACT.Copy, scale=SCALE).then_inc(q_ready, 1)
                for r in range(R):
                    t = R * b + r
                    for k in range(NH):
                        act.wait_ge(s_ps, 2 * (NH * t + k) + 1)
                        A(s[:, k, 0:1024], S[:, 0:1024], ACT.Copy).then_inc(s_ready, 1)
                        act.wait_ge(s_ps, 2 * (NH * t + k) + 2)
                        A(s[:, k, 1024:G], S[:, 1024:G], ACT.Copy).then_inc(s_ready, 1)
                    act.wait_ge(top_ready, t + 1)
                    for k in range(NH):
                        link(A(etop[:, :], top[:, k, :], ACT.Exp, bias=ngmax[:, k:k + 1], accum_out=ssum[:, k:k + 1]))
                    A(lnsum[:, :], ssum[:, :], ACT.Ln, scale=float(NH)).then_inc(esum_ready, 1)
                    act.wait_ge(ebias_ready, t + 1)
                    if t >= 1:
                        act.wait_ge(aT_ps, 4 * t)
                    for k in range(NH):
                        A(prob[:, k, :], s[:, k, :], ACT.Exp, bias=ebias[:, k:k + 1]).then_inc(prob_ready, 1)
                    for g in range(4):
                        act.wait_ge(aT_ps, 4 * t + g + 1)
                        w = min(4, GC - 4 * g)
                        rows_ = P if w == 4 else GL
                        A(aT[0:rows_, 4 * g:4 * g + w, r * P:(r + 1) * P],
                          M[0:rows_, g % 2, 0:w * P].rearrange("p (g d) -> p g d", d=P), ACT.Copy).then_inc(aT_ready, 1)
                act.wait_ge(c_ps, b + 1)
                A(cT[:, :], M[:, 0, 0:T], ACT.Copy).then_inc(c_ready, 1)

            def tail(b):
                act.wait_ge(n3T_ps, b + 1)
                A(hT[:, :], TT[:, 0, 0:T], ACT.Identity, scale=col("ffn_g"), bias=col("ffn_b")).then_inc(hT_ready, 1)
                for f in range(FT):
                    act.wait_ge(h1_ps, FT // 2 * b + f // 2 + 1)
                    A(gT[:, f, :], TT[:, 1 - f // 2, (f % 2) * T:(f % 2 + 1) * T], ACT.Gelu,
                      bias=col("ffn_b1", f)).then_inc(gT_ready, 1)
                act.wait_ge(x2T_ps, b + 1)
                A(x2T[:, :], TT[:, 0, 0:T], ACT.Copy).then_inc(x2T_ready, 1)
                act.wait_ge(wexp_in, b + 1)
                A(wtop[:, :, 1], wtop[:, :, 0], ACT.Exp).then_inc(wexp_out, 1)
                act.wait_ge(wdT_ps, b + 1)
                A(wdT[:, :], TT[0:NE, 1, 128:128 + T], ACT.Copy).then_inc(wdT_ready, 1)
                for e in range(NE):
                    if e >= 2:
                        act.wait_ge(eo_ps, NE * b + e - 1)
                    for f in range(FT):
                        act.wait_ge(eh_ps, FT // 2 * (NE * b + e) + f // 2 + 1)
                        A(gm[:, e % 2, f, :], TT[:, f // 2, (f % 2) * T:(f % 2 + 1) * T], ACT.Gelu,
                          bias=col("moe_b1", FT * e + f)).then_inc(eg_ready, 1)

            for b in range(B):
                front(b)
                attention(b)
                tail(b)

        @block.tensor
        def _(pe):
            mm = nc.tensor.matmul

            pe.wait_ge(s4_mats, 1)
            for d in range(D):
                ins = mm(S[0:L16, d * L16:(d + 1) * L16], u_ph[:, :, d], w_ph[:, :, d], start=True, stop=True)
            ins.then_inc(k16_ps, 1)
            pe.wait_ge(kT_ready, 1)
            pe.wait_ge(ld_dft, 32)
            for j, cols_ in enumerate(((0, 1), (4, 3), (5, 1))):
                for q in range(2):
                    for r in range(R):
                        ins = mm(TT[:, j // 2, (j % 2) * 256 + q * D:(j % 2) * 256 + (q + 1) * D],
                                 dft[:, r, cols_[q], :], kT[:, r, :], start=(r == 0), stop=(r == R - 1))
            ins.then_inc(kf_ps, 1)

            def front(b):
                pe.wait_ge(xn_ready, b + 1)
                if b == 0:
                    pe.wait_ge(ld_small, 80)
                    pe.wait_ge(ld_w, 16)
                for r in range(R):
                    ins = nc.tensor.transpose(M[:, 0, r * P:(r + 1) * P], xn[:, r, :], ident[:, :])
                ins.then_inc(xnT_ps, 1)
                pe.wait_ge(xnT_ready, b + 1)
                for j in range(4):
                    ins = mm(M[:, j // 2, (j % 2) * T:(j % 2 + 1) * T], wt("w_in", j, P), xnT[:, :], start=True, stop=True)
                    if j % 2:
                        ins.then_inc(xz_ps, 1)
                pe.wait_ge(xc_ready, b + 1)
                for c in range(CH):
                    ins = mm(M[:, 0, T:2 * T], wt("wx_raw", c, P), xc[:, c, :], start=(c == 0), stop=(c == CH - 1))
                ins.then_inc(ssm_ps, 1)
                pe.wait_ge(sz_ready, b + 1)
                for c in range(CH):
                    ins = mm(M[0:96, 1, 0:T], wt("wx_bc", c, 96), xc[:, c, :], start=(c == 0), stop=(c == CH - 1))
                ins.then_inc(ssm_ps, 1)
                pe.wait_ge(parts_ready, b + 1)
                pe.wait_ge(params_ready, 1)
                if b == 0:
                    pe.wait_ge(k16_sb, 1)
                pe.wait_ge(dt_ready, b + 1)

                def spread(i):
                    u, which = i // 2, i % 2
                    if u >= 1:
                        pe.wait_ge(c_used if which else b_used, NU * b + u)
                    for j in range(UN):
                        ins = mm(S[:, which * 1024 + j * T:which * 1024 + (j + 1) * T],
                                 sel[:, which * NS + UN * u + j:which * NS + UN * u + j + 1].to_broadcast([96, P]), parts[:, :],
                                 start=True, stop=True)
                    ins.then_inc(bc_ps, 1)

                spread(0)
                spread(1)
                for u in range(NU):
                    if u + 1 < NU:
                        spread(2 * u + 2)
                        spread(2 * u + 3)
                    for c in range(CH):
                        pe.wait_ge(hc_ready, CH * (NU * b + u) + c + 1)
                        for j in range(UN):
                            ins = mm(M[:, c, 0:T], ident[:, :], hst[:, u % 2, c, j, :], start=(u + j == 0),
                                     stop=(u == NU - 1 and j == UN - 1))
                        ins.then_inc(y_sum, 1)
                pe.wait_ge(yv_ready, b + 1)
                for r in range(R):
                    for c in range(CH):
                        ins = mm(M[:, 0, T + r * D:T + (r + 1) * D], yv[:, c, r * P:(r + 1) * P], wt("w_out", c, D),
                                 start=(c == 0), stop=(c == CH - 1))
                ins.then_inc(op_ps, 1)

            def attention(b):
                pe.wait_ge(ld_ctx, 32 * (b + 1))
                pe.wait_ge(c_used, NU * (b + 1))
                for g in range(4):
                    w = min(512, G - 512 * g)
                    mm(S[:, 512 * g:512 * g + w], wkv[:, 0:D], ctxT[:, 512 * g:512 * g + w], start=True, stop=True
                       ).then_inc(k_ps, 1)
                pe.wait_ge(x1_ready, b + 1)
                for g in range(4):
                    if g >= 2:
                        pe.wait_ge(v_ready, 4 * b + g - 1)
                    for i in range(4 * g, min(4 * g + 4, GC)):
                        w = P if i < GC - 1 else GL
                        ins = mm(M[0:w, g % 2, (i % 4) * D:(i % 4 + 1) * D], ctxT[:, i * P:i * P + w], wkv[:, D:2 * D],
                                 start=True, stop=True)
                    ins.then_inc(v_ps, 1)
                pe.wait_ge(v_ready, 4 * b + 4)
                for r in range(R):
                    ins = nc.tensor.transpose(M[:, 0, r * P:(r + 1) * P], x1[:, r, :], ident[:, :])
                ins.then_inc(x1T_ps, 1)
                pe.wait_ge(x1T_ready, b + 1)
                mm(M[:, 1, 0:T], wt("wq", 0, D), x1T[:, :], start=True, stop=True).then_inc(q_ps, 1)
                pe.wait_ge(q_ready, b + 1)
                pe.wait_ge(k_ready, b + 1)
                pe.wait_ge(pen_ready, b + 1)
                for r in range(R):
                    t = R * b + r
                    for k in range(NH):
                        for g in range(4):
                            w = min(512, G - 512 * g)
                            if t or k:
                                pe.wait_ge(s_ready, 2 * (NH * t + k) - (1 if g < 2 else 0))
                            mm(S[:, 512 * g:512 * g + w], onesb[k * DH:k * DH + 1, :], pen[k * DH:k * DH + 1, 512 * g:512 * g + w], start=True, stop=False)
                            ins = mm(S[:, 512 * g:512 * g + w], QT[k * DH:(k + 1) * DH, r * P:(r + 1) * P],
                                     KT[k * DH:(k + 1) * DH, 512 * g:512 * g + w], start=False, stop=True)
                            if g % 2:
                                ins.then_inc(s_ps, 1)
                    pe.wait_ge(flags_ready, t + 1)
                    mm(M[0:1, 1, 0:NH], ones[:, :], flag[:, :], start=True, stop=True).then_inc(flags_sum, 1)
                    pe.wait_ge(avg_ready, t + 1)
                    for g in range(4):
                        if g >= 2:
                            pe.wait_ge(aT_ready, 4 * t + g - 1)
                        for i in range(4 * g, min(4 * g + 4, GC)):
                            w = P if i < GC - 1 else GL
                            ins = nc.tensor.transpose(M[0:w, g % 2, (i % 4) * P:(i % 4 + 1) * P],
                                                      prob[:, 0, i * P:i * P + w], ident[:, :])
                        ins.then_inc(aT_ps, 1)
                pe.wait_ge(aT_ready, 4 * R * (b + 1))
                for i in range(GC):
                    w = P if i < GC - 1 else GL
                    ins = mm(M[:, 0, 0:T], V[0:w, i, :], aT[0:w, i, :], start=(i == 0), stop=(i == GC - 1))
                ins.then_inc(c_ps, 1)

            def tail(b):
                pe.wait_ge(c_ready, b + 1)
                if b == 0:
                    pe.wait_ge(kf_ready, 1)
                    pe.wait_ge(ld_moe, 48)
                if b >= 1:
                    pe.wait_ge(eg_ready, FT * NE * b)
                    pe.wait_ge(eo_used, NE * b)
                for j, name in enumerate(("film_in", "film_out")):
                    for r in range(R):
                        ins = mm(TT[:, j, r * T:(r + 1) * T], cT[:, r * P:(r + 1) * P], wt(name, 0, 2 * D), start=True, stop=True)
                ins.then_inc(film_ps, 1)
                pe.wait_ge(xs_ready, b + 1)
                for q in range(4):
                    for r in range(R):
                        ins = mm(TT[:, 0, q * D:(q + 1) * D], dft[:, r, q, :], n2[:, r, :], start=(r == 0), stop=(r == R - 1))
                ins.then_inc(xf_ps, 1)
                pe.wait_ge(Y_ready, b + 1)
                for r in range(R):
                    for q in range(4):
                        ins = mm(TT[:, 1, r * D:(r + 1) * D], idft[:, q, r * P:(r + 1) * P], Y[:, q, :],
                                 start=(q == 0), stop=(q == 3))
                ins.then_inc(y_ps, 1)
                pe.wait_ge(n3_ready, b + 1)
                for r in range(R):
                    ins = nc.tensor.transpose(TT[:, 0, r * P:(r + 1) * P], n2[:, r, :], ident[:, :])
                ins.then_inc(n3T_ps, 1)
                pe.wait_ge(hT_ready, b + 1)
                for f in range(FT):
                    ins = mm(TT[:, 1 - f // 2, (f % 2) * T:(f % 2 + 1) * T], wt("w1", f, P), hT[:, :], start=True, stop=True)
                    if f % 2:
                        ins.then_inc(h1_ps, 1)
                pe.wait_ge(gT_ready, FT * (b + 1))
                for r in range(R):
                    for f in range(FT):
                        ins = mm(TT[:, 1, r * D:(r + 1) * D], gT[:, f, r * P:(r + 1) * P], wt("w2", f, D),
                                 start=(f == 0), stop=(f == FT - 1))
                ins.then_inc(h2_ps, 1)
                pe.wait_ge(x2_ready, b + 1)
                for r in range(R):
                    ins = nc.tensor.transpose(TT[:, 0, r * P:(r + 1) * P], x2[:, r, :], ident[:, :])
                ins.then_inc(x2T_ps, 1)
                pe.wait_ge(x2T_ready, b + 1)
                for r in range(R):
                    ins = mm(TT[:, 1, r * NE:(r + 1) * NE], x2T[:, r * P:(r + 1) * P], wt("router", 0, NE), start=True, stop=True)
                ins.then_inc(lg_ps, 1)
                pe.wait_ge(wd_ready, b + 1)
                for r in range(R):
                    ins = nc.tensor.transpose(TT[0:NE, 1, 128 + r * P:128 + (r + 1) * P], wd[:, r, :], ident[:, :])
                ins.then_inc(wdT_ps, 1)
                pe.wait_ge(wdT_ready, b + 1)
                for r in range(R):
                    ins = mm(M[:, 0, r * D:(r + 1) * D], wdT[:, r * P:(r + 1) * P], moe_b2[:, :], start=True, stop=True)
                ins.then_inc(mb_ps, 1)
                pe.wait_ge(acc_set, b + 1)

                def expert_out(e):
                    pe.wait_ge(eg_ready, FT * NE * b + FT * (e + 1))
                    if e >= 2:
                        pe.wait_ge(eo_used, NE * b + e - 1)
                    for r in range(R):
                        for f in range(FT):
                            ins = mm(M[:, e % 2, r * D:(r + 1) * D], gm[:, e % 2, f, r * P:(r + 1) * P],
                                     moe_w2[:, e, f, :], start=(f == 0), stop=(f == FT - 1))
                    ins.then_inc(eo_ps, 1)

                for e in range(NE):
                    for f in range(FT):
                        if e >= 1 and f % 2 == 0:
                            pe.wait_ge(eg_ready, FT * (NE * b + e - 1) + f + 2)
                        ins = mm(TT[:, f // 2, (f % 2) * T:(f % 2 + 1) * T], moe_w1[:, e, f, :], x2T[:, :],
                                 start=True, stop=True)
                        if f % 2:
                            ins.then_inc(eh_ps, 1)
                    if e >= 1:
                        expert_out(e - 1)
                expert_out(NE - 1)

            for b in range(B):
                front(b)
                attention(b)
                tail(b)

        @block.vector
        def _(dve):
            n = [0]

            def link(ins, wait=True):
                n[0] += 1
                ins.then_inc(dve_step, 1)
                if wait:
                    dve.wait_ge(dve_step, n[0])

            TS, TTN, STT = nc.vector.tensor_scalar, nc.vector.tensor_tensor, nc.vector.scalar_tensor_tensor

            dve.wait_ge(a_exp, 1)
            link(TS(a_neg[:, :], a_neg[:, :], -1.0, None, ALU.mult), False)
            dve.wait_ge(ld_rows, 16)
            dve.wait_ge(ld_w, 16)
            dve.wait_ge(ld_small, 80)
            gate = rows[:, ROWS["gate"][0]:ROWS["gate"][1]]
            for name in ("film_in", "film_out"):
                link(TS(wt(name, 0, 2 * D), wt(name, 0, 2 * D), gate, None, ALU.mult), False)
                rb = row(name + "_b")
                link(TS(rb, rb, gate, None, ALU.mult))
                link(TS(rb[:, 0:D], rb[:, 0:D], 1.0, None, ALU.add), False)
            link(nc.vector.tensor_copy(tmask[:, :, :].rearrange("p b r -> p (b r)"), tmask8[:, :]))
            dve.sem_inc(consts_set, 1)

            turn, are, dts, r_, sinb, cosb, sinh, th, k_, g_, gx, gy = sv
            v = lambda t_: t_[:, :]
            LN2H = float(np.float32(0.693359375))
            LN2L = float(np.float32(np.log(2.0) - 0.693359375))
            ldt = row("log_dt")
            dve.wait_ge(ld_s4, 96)
            link(TS(v(k_), ldt, float(np.log2(np.e)), MAGIC, ALU.mult, ALU.add))
            link(TS(v(k_), v(k_), MAGIC, None, ALU.subtract))
            link(STT(out=v(r_), in0=v(k_), scalar=-LN2H, in1=ldt, op0=ALU.mult, op1=ALU.add))
            link(STT(out=v(r_), in0=v(k_), scalar=-LN2L, in1=v(r_), op0=ALU.mult, op1=ALU.add))
            fact = [1.0 / 5040, 1.0 / 720, 1.0 / 120, 1.0 / 24, 1.0 / 6, 0.5, 1.0]
            link(TS(v(g_), v(r_), fact[0], None, ALU.mult))
            for c_ in fact[1:]:
                link(STT(out=v(g_), in0=v(g_), scalar=c_, in1=v(r_), op0=ALU.add, op1=ALU.mult))
            link(TS(v(g_), v(g_), 1.0, None, ALU.add))
            link(TS(v(k_), v(k_), 127.0, 0.0, ALU.add, ALU.max))
            link(TS(ki[:, :], v(k_), 254.0, 2.0 ** 23, ALU.min, ALU.mult))
            link(TTN(v(dts), v(g_), ki[:, :].bitcast(F32), ALU.mult))
            link(TTN(v(are), v(dts), v(a_re), ALU.mult), False)
            link(TTN(v(turn), v(dts), v(a_im), ALU.mult))
            link(TS(v(turn), v(turn), float(1.0 / (2 * np.pi)), None, ALU.mult))

            def less_whole(dst, src, tmp, add=None):
                if add is not None:
                    link(TS(dst, src, add, None, ALU.add))
                    src = dst
                link(TS(tmp, src, MAGIC, None, ALU.add))
                link(TS(tmp, tmp, MAGIC, None, ALU.subtract))
                link(TTN(dst, src, tmp, ALU.subtract))

            less_whole(v(turn), v(turn), v(k_))
            dve.sem_inc(s4_small, 1)
            link(nc.vector.tensor_copy(v(sinb), v(turn)), False)
            link(nc.vector.tensor_copy(v(sinh), v(turn)), False)
            less_whole(v(cosb), v(turn), v(k_), 0.25)
            dve.sem_inc(s4_sin_in, 1)
            link(TS(c_2[64:128, :], c_2[64:128, :], -1.0, None, ALU.mult), False)
            dve.wait_ge(s4_sin, 1)
            link(TS(v(k_), v(th), -1.0, 1.0, ALU.mult, ALU.add))
            link(nc.vector.reciprocal(v(k_), v(k_)))
            link(STT(out=v(th), in0=v(th), scalar=2.0, in1=v(k_), op0=ALU.mult, op1=ALU.mult))
            link(TTN(v(cosb), v(th), v(cosb), ALU.mult), False)
            link(TTN(v(sinh), v(sinh), v(sinh), ALU.mult))
            link(STT(out=v(gx), in0=v(sinh), scalar=-2.0, in1=v(cosb), op0=ALU.mult, op1=ALU.add))
            link(STT(out=v(gy), in0=v(th), scalar=1.0, in1=v(sinb), op0=ALU.add, op1=ALU.mult))
            link(TTN(v(k_), v(a_re), v(a_re), ALU.mult), False)
            link(TTN(v(dts), v(a_im), v(a_im), ALU.mult))
            link(TTN(v(k_), v(k_), v(dts), ALU.add))
            link(nc.vector.reciprocal(v(k_), v(k_)))
            link(TTN(v(r_), v(gx), v(a_re), ALU.mult), False)
            link(TTN(v(dts), v(gy), v(a_im), ALU.mult))
            link(TTN(v(r_), v(r_), v(dts), ALU.add))
            link(STT(out=v(r_), in0=v(r_), scalar=2.0, in1=v(k_), op0=ALU.mult, op1=ALU.mult))
            link(TTN(v(g_), v(gy), v(a_re), ALU.mult), False)
            link(TTN(v(dts), v(gx), v(a_im), ALU.mult))
            link(TTN(v(g_), v(g_), v(dts), ALU.subtract))
            link(STT(out=v(g_), in0=v(g_), scalar=2.0, in1=v(k_), op0=ALU.mult, op1=ALU.mult))
            link(TTN(v(gx), v(c_1), v(r_), ALU.mult), False)
            link(TTN(v(dts), v(c_2), v(g_), ALU.mult))
            link(TTN(v(gx), v(gx), v(dts), ALU.subtract))
            link(TTN(v(gy), v(c_1), v(g_), ALU.mult), False)
            link(TTN(v(dts), v(c_2), v(r_), ALU.mult))
            link(TTN(v(gy), v(gy), v(dts), ALU.add))
            dve.sem_inc(s4_gain, 1)
            dve.wait_ge(s4_arg, 1)
            link(TS(w_ph, w_ph, phase[:, 0:1], None, ALU.add))
            link(TS(w_rnd, w_ph, MAGIC, None, ALU.add))
            link(TS(w_rnd, w_rnd, MAGIC, None, ALU.subtract))
            link(TTN(w_ph, w_ph, w_rnd, ALU.subtract))
            dve.sem_inc(s4_th_in, 2)
            dve.wait_ge(s4_arg, 2)
            link(TS(u_ph2, u_ph, 0.5, None, ALU.add), False)
            link(TS(u_ph, u_ph, 0.25, None, ALU.add))
            for ph in (u_ph, u_ph2):
                link(TS(w_rnd, ph, MAGIC, None, ALU.add))
                link(TS(w_rnd, w_rnd, MAGIC, None, ALU.subtract))
                link(TTN(ph, ph, w_rnd, ALU.subtract))
            dve.sem_inc(s4_th_in, 2)
            dve.wait_ge(k16_moved, 32)
            link(TTN(kT[0:1, 0, :], kT[0:1, 0, :], dskip[:, :], ALU.add))
            dve.sem_inc(kT_ready, 1)
            dve.wait_ge(kf_ps, 1)
            for j in range(3):
                link(nc.vector.tensor_copy(kf[:, j, :, :], TT[:, j // 2, (j % 2) * 256:(j % 2) * 256 + 256]
                                           .rearrange("p (q d) -> p q d", q=2)))
            dve.sem_inc(kf_ready, 1)

            def layernorm(b, k, dst, src, signal=None):
                for r in range(R):
                    link(nc.vector.bn_stats(stat[:, k, r, :], src[:, r, :]), r == R - 1)
                for r in range(R):
                    ins = nc.vector.bn_aggr(mv[:, k, r, :], stat[:, k, r, :])
                    if r < R - 1:
                        link(ins, False)
                ins.then_inc(var_ready, 1)
                dve.wait_ge(rstd_ready, LNS * b + k + 1)
                for r in range(R):
                    ins = TS(dst[:, r, :], src[:, r, :], mv[:, k, r, 0:1], rstd[:, k, r:r + 1], ALU.subtract, ALU.mult)
                    if r < R - 1:
                        link(ins, False)
                if signal is not None:
                    ins.then_inc(signal, 1)
                else:
                    link(ins)

            def front(b):
                dve.wait_ge(ld_x, 16 * (b + 1))
                layernorm(b, 0, xn, x_in, xn_ready)
                dve.wait_ge(xz_ps, 2 * b + 1)
                dve.wait_ge(ld_cols, 16)
                for c in range(CH):
                    link(TS(cv[:, c, :], M[:, 0, c * T:(c + 1) * T], col("conv_w", c * KC + KC - 1), col("conv_b", c),
                            ALU.mult, ALU.add), c == CH - 1)
                for j in range(1, KC):
                    for c in range(CH):
                        ins = STT(out=cv[:, c, j:T], in0=M[:, 0, c * T:(c + 1) * T - j],
                                  scalar=col("conv_w", c * KC + KC - 1 - j), in1=cv[:, c, j:T], op0=ALU.mult, op1=ALU.add)
                        if c == CH - 1 and j == KC - 1:
                            ins.then_inc(conv_ready, 1)
                        else:
                            link(ins, c == CH - 1)
                dve.wait_ge(bc_hi, b + 1)
                link(TTN(bc_r[:, :], M[0:96, 1, 0:T], parts[:, :], ALU.subtract))
                link(nc.vector.tensor_copy(bc_m[:, :], bc_r[:, :]))
                link(TTN(bc_r[:, :], bc_r[:, :], bc_m[:, :], ALU.subtract), False)
                link(nc.vector.tensor_copy(parts[32:64, :], bc_m[32:64, :]))
                nc.vector.tensor_copy(parts[64:96, :], bc_r[64:96, :]).then_inc(parts_ready, 1)
                dve.wait_ge(sp_ready, b + 1)
                link(TS(sp_q[:, :, :], sp_a[:, :, :], 2.0, None, ALU.add))
                link(nc.vector.reciprocal(sp_q[:, :, :], sp_q[:, :, :]))
                link(TTN(sp_r[:, :, :], sp_a[:, :, :], sp_q[:, :, :], ALU.mult))
                dve.sem_inc(sq_in, 1)
                dve.wait_ge(sq_out, b + 1)
                link(TS(sp_a[:, :, :], sp_q[:, :, :], C1[5], None, ALU.mult))
                for j in range(4, 0, -1):
                    link(STT(out=sp_a[:, :, :], in0=sp_a[:, :, :], scalar=C1[j], in1=sp_q[:, :, :], op0=ALU.add, op1=ALU.mult))
                link(STT(out=sp_a[:, :, :], in0=sp_a[:, :, :], scalar=C1[0], in1=sp_r[:, :, :], op0=ALU.add, op1=ALU.mult))
                link(TTN(dt_[:, :, :], sp_a[:, :, :], sp_p[:, :, :], ALU.add))
                dve.sem_inc(dt_ready, 1)
                dve.wait_ge(xc_ready, b + 1)
                link(TTN(ux[:, :, :], dt_[:, :, :], xc[:, :, :], ALU.mult))
                for u in range(NU):
                    half_b, half_c = (S[:, i * 1024:(i + 1) * 1024].rearrange("p (n t) -> p n t", n=UN) for i in range(2))
                    dve.wait_ge(bc_ps, 2 * (NU * b + u) + 1)
                    for c in range(CH):
                        if u >= 2:
                            dve.wait_ge(y_sum, CH * (NU * b + u - 2) + c + 1)
                        link(TTN(hst[:, u % 2, c, :, :], ux[:, c, :].unsqueeze(1).to_broadcast([P, UN, T]), half_b, ALU.mult),
                             c == CH - 1)
                    dve.sem_inc(b_used, 1)
                    for c in range(CH):
                        dve.wait_ge(abar_ready, CH * (NU * b + u) + c + 1)
                        hf = hst[:, u % 2, c, :, :].rearrange("p n t -> p (n t)")
                        nc.vector.tensor_tensor_scan(hf, abar[:, u % 2, c, :, :].rearrange("p n t -> p (n t)"), hf, 0.0,
                                                     ALU.mult, ALU.add).then_inc(scan_done, 1)
                    dve.wait_ge(bc_ps, 2 * (NU * b + u) + 2)
                    for c in range(CH):
                        dve.wait_ge(scan_done, CH * (NU * b + u) + c + 1)
                        ins = TTN(hst[:, u % 2, c, :, :], hst[:, u % 2, c, :, :], half_c, ALU.mult)
                        ins.then_inc(hc_ready, 1)
                    dve.wait_ge(hc_ready, CH * (NU * b + u + 1))
                    dve.sem_inc(c_used, 1)
                dve.wait_ge(y_sum, CH * NU * (b + 1))
                dve.wait_ge(sz_ready, b + 1)
                for c in range(CH):
                    link(STT(out=yv[:, c, :], in0=xc[:, c, :], scalar=col("d_param", c), in1=M[:, c, 0:T], op0=ALU.mult,
                             op1=ALU.add), c == CH - 1)
                link(TTN(yv[:, :, :], yv[:, :, :], sz[:, :, :], ALU.mult))
                dve.sem_inc(yv_ready, 1)
                dve.wait_ge(op_ps, b + 1)
                link(STT(out=res[:, :, :], in0=x_in[:, :, :], scalar=2.0,
                         in1=M[:, 0, T:2 * T].rearrange("p (r d) -> p r d", r=R), op0=ALU.mult, op1=ALU.add))
                dve.sem_inc(x_used, 1)
                layernorm(b, 1, x1, res)
                dve.sem_inc(x1_ready, 1)

            def largest(k):
                link(nc.vector.max(top[:, k, 0:8], cand[:, :, :].rearrange("p n e -> p (n e)")))
                src = cand[:, :, :].rearrange("p n e -> p (n e)")
                for j in range(1, 4):
                    link(nc.vector.match_replace(cand2[:, :], top[:, k, 8 * j - 8:8 * j], src, LOWEST))
                    src = cand2[:, :]
                    link(nc.vector.max(top[:, k, 8 * j:8 * j + 8], src))

            def exact(k):
                src = s[:, k, :]
                for j in range(4):
                    nc.vector.max(top[:, k, 8 * j:8 * j + 8], src)
                    dve.drain()
                    nc.vector.match_replace(scratch[:, :], top[:, k, 8 * j:8 * j + 8], src, LOWEST)
                    dve.drain()
                    src = scratch[:, :]
                TTN(scratch[:, :], scratch[:, :], s[:, k, :], ALU.is_equal)
                dve.drain()
                STT(out=s[:, k, :], in0=scratch[:, :], scalar=-PENALTY / 4, in1=s[:, k, :], op0=ALU.mult, op1=ALU.add)
                dve.drain()

            def attention(b):
                for r in range(R):
                    t = R * b + r
                    for k in range(NH):
                        dve.wait_ge(s_ready, 2 * (NH * t + k) + 2)
                        for g in range(NSEG):
                            hi = G if g == NSEG - 1 else (g + 1) * SEG
                            link(nc.vector.max(cand[:, g, :], s[:, k, g * SEG:hi]), g == NSEG - 1)
                        largest(k)
                        link(nc.vector.tensor_reduce(seg8[:, k:k + 1], cand[:, :, 7], AX, ALU.max), False)
                        link(TS(above[:, :], cand[:, :, :].rearrange("p n e -> p (n e)"), top[:, k, TOPK - 1:TOPK], 0.0,
                                ALU.is_ge, ALU.add, accum_out=nabove[:, k:k + 1]))
                    link(TTN(seg8[:, :], seg8[:, :], top[:, :, TOPK - 1], ALU.is_ge), False)
                    link(TS(nabove[:, :], nabove[:, :], TOPK + 0.5, None, ALU.is_ge))
                    TTN(flag[:, :], seg8[:, :], nabove[:, :], ALU.add).then_inc(flags_ready, 1)
                    dve.wait_ge(flags_sum, t + 1)
                    link(nc.vector.tensor_reduce(anyf[:, :], M[0:1, 1, 0:NH], AX, ALU.add))
                    link(nc.vector.tensor_copy(anyi[:, :], anyf[:, :]))
                    found = dve.value_load(anyi[0:1, 0:1], min_val=0, max_val=8 * P)
                    with dve.If(found > 0):
                        for k in range(NH):
                            exact(k)
                    link(TS(ngmax[:, :], top[:, :, 0], 4.0, -0.25, ALU.mult, ALU.mult))
                    dve.sem_inc(top_ready, 1)
                    dve.wait_ge(esum_ready, t + 1)
                    link(TTN(ebias[:, :], ngmax[:, :], lnsum[:, :], ALU.subtract))
                    dve.sem_inc(ebias_ready, 1)
                    for k in range(NH):
                        dve.wait_ge(prob_ready, NH * t + k + 1)
                        STT(out=prob[:, k, :], in0=s[:, k, :], scalar=top[:, k, TOPK - 1:TOPK], in1=prob[:, k, :],
                            op0=ALU.is_ge, op1=ALU.mult).then_inc(masked_ready, 1)

            def rowb(name):
                return row(name).unsqueeze(1).to_broadcast([P, R, D])

            def tail(b):
                layernorm(b, 2, n2, x1)
                link(TTN(n2[:, :, :], n2[:, :, :], rowb("in_g"), ALU.mult))
                link(TTN(n2[:, :, :], n2[:, :, :], rowb("in_b"), ALU.add), False)
                dve.wait_ge(film_ps, b + 1)
                for dst, j, name in ((fi, 0, "film_in_b"), (fo, 1, "film_out_b")):
                    for r in range(R):
                        link(STT(out=dst[:, r, :], in0=TT[:, j, r * T:(r + 1) * T], scalar=tmask[:, b, r:r + 1], in1=row(name),
                                 op0=ALU.mult, op1=ALU.add), r == 1 and j == 1)
                link(TTN(n2[:, :, :], n2[:, :, :], fi[:, :, 0:D], ALU.mult))
                link(TTN(n2[:, :, :], n2[:, :, :], fi[:, :, D:2 * D], ALU.add))
                dve.sem_inc(xs_ready, 1)
                dve.wait_ge(xf_ps, b + 1)
                xre = TT[:, 0, 0:2 * D].rearrange("p (q d) -> p q d", q=2)
                xim = TT[:, 0, 2 * D:4 * D].rearrange("p (q d) -> p q d", q=2)
                for lo, ka, kb, op in ((0, 0, 1, ALU.subtract), (2, 1, 2, ALU.add)):
                    link(TTN(xf_a[:, :, :], xre, kf[:, ka, :, :], ALU.mult), False)
                    link(TTN(xf_b[:, :, :], xim, kf[:, kb, :, :], ALU.mult))
                    link(TTN(Y[:, lo:lo + 2, :], xf_a[:, :, :], xf_b[:, :, :], op))
                dve.sem_inc(Y_ready, 1)
                dve.wait_ge(y_ps, b + 1)
                link(TTN(xt[:, :, :], TT[:, 1, 0:T].rearrange("p (r d) -> p r d", r=R), fo[:, :, 0:D], ALU.mult))
                link(TTN(xt[:, :, :], xt[:, :, :], fo[:, :, D:2 * D], ALU.add))
                link(TTN(xt[:, :, :], xt[:, :, :], x1[:, :, :], ALU.add))
                layernorm(b, 3, n2, xt, n3_ready)
                dve.wait_ge(n3_ready, b + 1)
                link(TTN(xt[:, :, :], xt[:, :, :], rowb("ffn_b2"), ALU.add))
                dve.wait_ge(h2_ps, b + 1)
                link(TTN(xt[:, :, :], TT[:, 1, 0:T].rearrange("p (r d) -> p r d", r=R), xt[:, :, :], ALU.add))
                layernorm(b, 4, n2, xt)
                link(TTN(n2[:, :, :], n2[:, :, :], rowb("out_g"), ALU.mult))
                link(TTN(n2[:, :, :], n2[:, :, :], rowb("out_b"), ALU.add))
                link(TTN(n2[:, :, :], n2[:, :, :], x1[:, :, :], ALU.add))
                layernorm(b, 5, x2, n2)
                dve.sem_inc(x2_ready, 1)
                dve.wait_ge(lg_ps, b + 1)
                link(TTN(lg[:, :, :], TT[:, 1, 0:R * NE].rearrange("p (r e) -> p r e", r=R),
                         row("router_b").unsqueeze(1).to_broadcast([P, R, NE]), ALU.add))
                for r in range(R):
                    link(nc.vector.max(lmax[:, r, :], lg[:, r, :]), r == R - 1)
                for r in range(R):
                    link(nc.vector.max_index(lidx[:, r, :], lmax[:, r, :], lg[:, r, :]), r == R - 1)
                link(nc.vector.tensor_copy(lidf[:, :, :], lidx[:, :, 0:2]), False)
                link(TTN(wtop[:, :, 0], lmax[:, :, 1], lmax[:, :, 0], ALU.subtract))
                dve.sem_inc(wexp_in, 1)
                dve.wait_ge(wexp_out, b + 1)
                link(TS(wtop[:, :, 2], wtop[:, :, 1], 1.0, None, ALU.add))
                link(nc.vector.reciprocal(wtop[:, :, 2], wtop[:, :, 2]))
                link(TTN(wtop[:, :, 3], wtop[:, :, 1], wtop[:, :, 2], ALU.mult))
                for r in range(R):
                    link(TS(oh[:, r, 0, :], iota8[:, :], lidf[:, r, 0:1], wtop[:, r, 2:3], ALU.is_equal, ALU.mult), False)
                    link(TS(oh[:, r, 1, :], iota8[:, :], lidf[:, r, 1:2], wtop[:, r, 3:4], ALU.is_equal, ALU.mult), r == 1)
                link(TTN(wd[:, :, :], oh[:, :, 0, :], oh[:, :, 1, :], ALU.add))
                dve.sem_inc(wd_ready, 1)
                dve.wait_ge(mb_ps, b + 1)
                link(TTN(acc[:, :, :], M[:, 0, 0:T].rearrange("p (r d) -> p r d", r=R), x2[:, :, :], ALU.add))
                dve.sem_inc(acc_set, 1)
                for e in range(NE):
                    dve.wait_ge(eo_ps, NE * b + e + 1)
                    for r in range(R):
                        link(STT(out=acc[:, r, :], in0=M[:, e % 2, r * D:(r + 1) * D], scalar=wd[:, r, e:e + 1],
                                 in1=acc[:, r, :], op0=ALU.mult, op1=ALU.add), r == 1)
                    dve.sem_inc(eo_used, 1)
                if b >= 1:
                    dve.wait_ge(out_stored, 16 * b)
                layernorm(b, 6, outt, acc, out_ready)

            for b in range(B):
                front(b)
                attention(b)
                tail(b)


def dft_tables():
    t = np.arange(T)[:, None].astype(np.float64)
    k = np.arange(T)[None, :].astype(np.float64)
    ang = 2 * np.pi * t * k / NFFT
    re, im = np.cos(ang), -np.sin(ang)
    last = np.where(np.arange(T) % 2 == 0, 1.0, -1.0)
    im_last, re_last = im.copy(), re.copy()
    im_last[:, 0] = last
    re_last[:, 0] = last
    fwd = np.stack([re[:, :P], re[:, P:], im_last[:, :P], im[:, P:], im[:, :P], re_last[:, :P]], 1)
    fwd = fwd.reshape(R, P, 6, P).transpose(1, 0, 2, 3)
    w = np.full(T, 2.0)
    w[0] = 1.0
    ire, iim = (re * w).T / NFFT, (im * w).T / NFFT
    iim[0, :] = last / NFFT
    inv = np.concatenate([ire, iim], 0).reshape(4, P, T).transpose(1, 0, 2)
    return np.ascontiguousarray(fwd, np.float32), np.ascontiguousarray(inv, np.float32)


def layout(i):
    tiles = lambda v, n: v.reshape(n, P, -1).transpose(1, 0, 2).reshape(P, -1)
    cols = {"ln_g": i["L0_attn_ln_gamma"][:, None], "ln_b": i["L0_attn_ln_beta"][:, None],
            "conv_w": tiles(i["L0_attn_conv_w"], CH), "conv_b": tiles(i["L0_attn_conv_b"], CH),
            "w_dt": tiles(i["L0_attn_w_dt"], CH), "b_dt": tiles(i["L0_attn_b_dt"], CH),
            "d_param": tiles(i["L0_attn_D_param"], CH), "a_log": tiles(i["L0_attn_A_log"], CH),
            "ffn_g": i["L0_xattn_g_ffn"][:, None], "ffn_b": i["L0_xattn_b_ffn"][:, None],
            "ffn_b1": tiles(i["L0_xattn_b1"], FT), "moe_b1": tiles(i["L0_ffn_b1"].reshape(-1), NE * FT)}
    rows = {"in_g": i["L0_xattn_g_norm_in"], "in_b": i["L0_xattn_b_norm_in"], "out_g": i["L0_xattn_g_norm_out"],
            "out_b": i["L0_xattn_b_norm_out"], "ffn_b2": i["L0_xattn_b2"], "film_in_b": i["L0_xattn_b_film_in"],
            "film_out_b": i["L0_xattn_b_film_out"], "router_b": i["L0_ffn_router_b"],
            "gate": i["L0_xattn_mod_gate"].reshape(1), "log_dt": i["L0_xattn_log_dt"]}
    wx = i["L0_attn_W_x"]
    wts = {"w_in": i["L0_attn_W_in"].T, "wx_bc": tiles(np.concatenate([wx[1:]] * 3, 0).T, CH),
           "wx_raw": tiles(np.repeat(wx[0:1], P, 0).T, CH), "w_out": tiles(i["L0_attn_W_out"].T, CH),
           "wq": i["L0_xattn_Wq"], "film_in": i["L0_xattn_W_film_in"], "film_out": i["L0_xattn_W_film_out"],
           "w1": i["L0_xattn_W1"], "w2": tiles(i["L0_xattn_W2"], FT), "router": i["L0_ffn_router_w"].T}
    fwd, inv = dft_tables()
    sel = (np.arange(96)[:, None] % 32 == np.arange(32)[None, :]).astype(np.float32)
    twice = lambda v: np.concatenate([v.T, v.T], 0)
    c_re, c_im = i["L0_xattn_C_re"].T, i["L0_xattn_C_im"].T
    return {
        "x": i["x"], "ctxT": i["ctx_768"].transpose(0, 2, 1), "gmask": i["mask_BxS2_bf1"],
        "tmask": i["mask_BxS_bf1"].reshape(B * R, P).T,
        "cols": np.concatenate([cols[n] for n in COLS], 1), "rows": np.concatenate([rows[n] for n in ROWS])[None, :],
        "wts": np.concatenate([wts[n] for n in WTS], 1),
        "wkv": np.concatenate([i["L0_xattn_Wk"], i["L0_xattn_Wv"]], 1), "ident": np.eye(P, dtype=np.float32),
        "sel": sel, "dft": fwd, "idft": inv, "iota8": np.arange(NE, dtype=np.float32)[None, :],
        "moe_w1": i["L0_ffn_w1"].transpose(2, 0, 1).reshape(P, NE, FT, P),
        "moe_w2": i["L0_ffn_w2"].reshape(NE, D, FT, P).transpose(3, 0, 2, 1), "moe_b2": i["L0_ffn_b2"],
        "a_re": twice(i["L0_xattn_A_re"]), "a_im": twice(i["L0_xattn_A_im"]),
        "c_1": np.concatenate([c_re, c_im], 0), "c_2": np.concatenate([c_im, c_re], 0),
        "dskip": i["L0_xattn_D_skip"][None, :],
        "steps": np.concatenate([np.arange(L16), L16 * np.arange(L16)]).astype(np.float32)[None, :],
    }


def kernel(**inputs):
    import concourse.bacc as bacc
    from concourse.bass_utils import run_bass_kernel_spmd

    nc = bacc.Bacc("TRN2", target_bir_lowering=False, num_devices=1)
    arrays, args = {}, {}
    for name, v in layout({k: np.asarray(x) for k, x in inputs.items()}).items():
        v = np.ascontiguousarray(v)
        if v.dtype == np.bool_:
            v = v.view(np.uint8)
        arrays[f"in_{name}"] = v
        args[name] = nc.dram_tensor(f"in_{name}", v.shape, mybir.dt.from_np(v.dtype), kind="ExternalInput").ap()
    args["out"] = nc.dram_tensor("out_x", (B, T, D), F32, kind="ExternalOutput").ap()
    build(nc, args)
    r = run_bass_kernel_spmd(nc, [arrays], core_ids=[0])
    return r.results[0]["out_x"]
```

```python
from contextlib import ExitStack

import numpy as np

import concourse.bass as bass
from concourse import mybir

ALU = mybir.AluOpType
ACT = mybir.ActivationFunctionType
F32 = mybir.dt.float32
BF16 = mybir.dt.bfloat16
I32 = mybir.dt.int32
U32 = mybir.dt.uint32
U8 = mybir.dt.uint8
AX = mybir.AxisListType.X

P = 128
B, T, D = 4, 256, 128
R = T // P
CH = 2
NS = 16
NU = 4
UN = NS // NU
KC = 4
G, DV = 1601, 96
GC = (G + P - 1) // P
GL = G - (GC - 1) * P
NH, DH = 4, 32
SEG = 64
NSEG = G // SEG
TOPK = 32
FT = 4
NE = 8
NST = 64
L16 = 16
NFFT = 2 * T
EPS = 1e-5
SCALE = float(np.float32(1.0) / np.sqrt(np.float32(DH)))
PENALTY = 1.0e38
COUNTED = G - 2 * (TOPK - 1) - 1
LOWEST = -3.4e38


def log1p_coefficients():
    n = 64
    q = (np.cos(np.pi * (np.arange(n) + 0.5) / n) + 1) / 2 / 9
    s = np.sqrt(q)
    return [float(v) for v in np.polynomial.polynomial.polyfit(q, 2 * np.arctanh(s) / s, 5)]


def column_layout():
    at, n = {}, 0
    for name, width in (("ln_g", 1), ("ln_b", 1), ("conv_w", CH * KC), ("conv_b", CH), ("w_dt", CH), ("b_dt", CH),
                        ("d_param", CH), ("a_log", CH * NS), ("ffn_g", 1), ("ffn_b", 1), ("ffn_b1", FT),
                        ("moe_b1", NE * FT)):
        at[name] = (n, n + width)
        n += width
    return at, n


def row_layout():
    at, n = {}, 0
    for name, width in (("in_g", D), ("in_b", D), ("out_g", D), ("out_b", D), ("ffn_b2", D), ("film_in_b", 2 * D),
                        ("film_out_b", 2 * D), ("router_b", NE), ("gate", 1), ("log_dt", D)):
        at[name] = (n, n + width)
        n += width
    return at, n


def weight_layout():
    at, n = {}, 0
    for name, width in (("w_in", 4 * P), ("wx_bc", CH * 96), ("wx_raw", CH * P), ("w_out", CH * D), ("wq", D),
                        ("film_in", 2 * D), ("film_out", 2 * D), ("w1", FT * P), ("w2", FT * D), ("router", NE)):
        at[name] = (n, n + width)
        n += width
    return at, n


COLS, NCOLS = column_layout()
ROWS, NROWS = row_layout()
WTS, NWTS = weight_layout()
LD = L16 * D
TILES = B * R * NH
LNS = 7


def build(nc, a):
    ctx = ExitStack()
    with ctx:
        def sb(name, shape, dt=F32):
            return ctx.enter_context(nc.sbuf_tensor(name, shape, dt))

        def sem(name):
            return ctx.enter_context(nc.semaphore(name))

        cols = sb("cols", [P, NCOLS])
        rows = sb("rows", [P, NROWS])
        wts = sb("wts", [P, NWTS])
        wkv = sb("wkv", [DV, 2 * D])
        ident = sb("ident", [P, P])
        sel_c = sb("sel_c", [96, 32])
        sel = sb("sel", [96, 32], BF16)
        dft = sb("dft", [P, R, 6, P])
        idft = sb("idft", [P, 4, T])
        moe_w = sb("moe_w", [P, 2 * NE * FT * P])
        moe_w1, moe_w2 = (moe_w[:, i * NE * FT * P:(i + 1) * NE * FT * P].rearrange("p (e f m) -> p e f m", e=NE, f=FT)
                          for i in range(2))
        moe_b2 = sb("moe_b2", [NE, D])
        tmask8 = sb("tmask8", [P, B * R], U8)
        tmask = sb("tmask", [P, B, R])
        half = sb("half", [P, R])
        onesb = sb("onesb", [P, P], BF16)
        iota8 = sb("iota8", [P, NE])
        a_neg = sb("a_neg", [P, CH * NS])
        kf = sb("kf", [P, 3, 2, D])

        xs_ = sb("xs_", [P, B, R, D])
        stat = sb("stat", [P, LNS, R, 6])
        mv = sb("mv", [P, LNS, R, 2])
        rstd = sb("rstd", [P, LNS, R])
        shared = sb("shared", [P, 2 * FT * T])
        sp_a, sp_p, sp_r, sp_q = (shared[:, i * CH * T:(i + 1) * CH * T].rearrange("p (c t) -> p c t", c=CH) for i in range(4))
        gT = shared[:, 1024:1024 + FT * T].rearrange("p (f t) -> p f t", f=FT)
        gm = shared[:, :].rearrange("p (e f t) -> p e f t", e=2, f=FT)
        mixed = sb("mixed", [P, 1024])
        yv = mixed[:, 0:512].rearrange("p (c t) -> p c t", c=CH)
        xn = mixed[:, 512:768].rearrange("p (r d) -> p r d", r=R)
        xnT = mixed[:, 768:1024]
        xf_a = mixed[:, 0:256].rearrange("p (q d) -> p q d", q=2)
        xf_b = mixed[:, 256:512].rearrange("p (q d) -> p q d", q=2)
        Y = mixed[:, 512:1024].rearrange("p (q d) -> p q d", q=4)
        big = sb("big", [P, 2 * NH * G])
        at = [0]

        def take(n):
            at[0] += n
            assert at[0] <= 2 * NH * G
            return big[:, at[0] - n:at[0]]

        abar, hst = (take(2 * CH * UN * T).rearrange("p (u c n t) -> p u c n t", u=2, c=CH, n=UN) for i in range(2))
        cv = take(CH * T).rearrange("p (c t) -> p c t", c=CH)
        xc, sz, dt_, ux = (take(2 * CH * T).rearrange("p (u c t) -> p u c t", u=2, c=CH) for i in range(4))
        early = sb("early", [P, (G + 1) // 2])
        parts = early[0:96, 0:T].bitcast(BF16).rearrange("p (u t) -> p u t", u=2)
        bc_r = early[0:96, T:2 * T]
        bc_m = early[0:96, 2 * T:2 * T + T // 2].bitcast(BF16)
        junk = early[:, :].bitcast(BF16)[:, 0:G]

        ctxT = sb("ctxT", [DV, G])
        gmask8 = sb("gmask8", [P, G], U8)
        pen0 = sb("pen0", [P, G], BF16)
        pen = (pen0[:, :], wts[:, 0:(G + 1) // 2].bitcast(BF16)[:, 0:G])
        KT = sb("KT", [P, G])
        V = sb("V", [P, GC, D])
        x1T = sb("x1T", [P, T])
        QT = sb("QT", [P, T])
        s = big[:, :].rearrange("p (u k g) -> p u k g", u=2, k=NH)
        att = sb("att", [P, 3 * LD])
        prob = att[:, 0:2 * G].rearrange("p (u g) -> p u g", u=2)
        aT = att[:, 2 * G:2 * G + GC * P].rearrange("p (g t) -> p g t", g=GC)
        scratch = prob[:, 0, :]
        avg = sb("avg", [P, G])
        cand = sb("cand", [P, 2, NSEG, 8])
        cand2 = sb("cand2", [P, NSEG * 8])
        top = sb("top", [P, 2, NH, TOPK])
        etop = sb("etop", [P, NH, TOPK])
        ngmax = sb("ngmax", [P, NH])
        ssum = sb("ssum", [P, NH])
        lnsum = sb("lnsum", [P, NH])
        ebias = sb("ebias", [P, NH])
        counts = sb("counts", [P, NH])
        tie = sb("tie", [P, NH])
        flag = sb("flag", [P, NH])
        flagrow = sb("flagrow", [1, P * NH])
        headf = sb("headf", [1, NH])
        anyf = sb("anyf", [1, 1])
        anyi = sb("anyi", [1, 1], I32)
        headi = sb("headi", [1, NH], I32)
        cT = sb("cT", [P, T])

        n2 = sb("n2", [P, R, D])
        xt = sb("xt", [P, R, D])
        hT = sb("hT", [P, T])
        x2 = sb("x2", [P, R, D])
        x2T = sb("x2T", [P, T])
        lg = sb("lg", [P, R, NE])
        lmax = sb("lmax", [P, R, 8])
        lidx = sb("lidx", [P, R, 8], U32)
        lidf = sb("lidf", [P, R, 2])
        wtop = sb("wtop", [P, R, 4])
        oh = sb("oh", [P, R, 2, NE])
        wd = sb("wd", [P, R, NE])
        wdT = sb("wdT", [NE, T])
        acc = sb("acc", [P, R, D])
        outt = sb("outt", [P, R, D])

        u_ph, u_ph2, u_exp, w_rnd = (moe_w[:, i * LD:(i + 1) * LD].rearrange("p (l d) -> p l d", l=L16) for i in range(4))
        w_ph, w_exp = (att[:, i * LD:(i + 1) * LD].rearrange("p (l d) -> p l d", l=L16) for i in range(2))
        a_re, a_im, c_1, c_2, *sv = [att[:, 2 * LD + i * D:2 * LD + (i + 1) * D] for i in range(16)]
        k16 = att[0:L16, 2 * LD:3 * LD].rearrange("p (l d) -> p l d", l=L16)
        kT = x1T[:, :].rearrange("p (r d) -> p r d", r=R)
        dskip = sb("dskip", [1, D])
        steps = sb("steps", [P, 2, L16])
        ki = sb("ki", [P, D], I32)
        phase = sb("phase", [P, 2])

        S = ctx.enter_context(nc.psum_tensor("S", [P, 4 * 512], F32))
        M = ctx.enter_context(nc.psum_tensor("M", [P, 2, 512], F32))
        TT = ctx.enter_context(nc.psum_tensor("TT", [P, 2, 512], F32))

        def col(name, i=0):
            return cols[:, COLS[name][0] + i:COLS[name][0] + i + 1]

        def row(name):
            return rows[:, ROWS[name][0]:ROWS[name][1]]

        def wt(name, i, n):
            return wts[:, WTS[name][0] + i * n:WTS[name][0] + (i + 1) * n]

        ld_x = sem("ld_x"); ld_ctx = sem("ld_ctx"); ld_cols = sem("ld_cols"); ld_rows = sem("ld_rows")
        ld_w = sem("ld_w"); ld_small = sem("ld_small"); ld_s4 = sem("ld_s4"); ld_dft = sem("ld_dft")
        ld_moe = sem("ld_moe"); k16_moved = sem("k16_moved"); out_stored = sem("out_stored")
        pool_step = sem("pool_step"); dve_step = sem("dve_step"); act_step = sem("act_step")
        consts_set = sem("consts_set"); a_exp = sem("a_exp"); params_ready = sem("params_ready")
        s4_small = sem("s4_small"); s4_sin_in = sem("s4_sin_in"); s4_sin = sem("s4_sin")
        s4_th_in = sem("s4_th_in"); s4_gain = sem("s4_gain")
        s4_arg = sem("s4_arg"); s4_fun = sem("s4_fun"); s4_mats = sem("s4_mats"); k16_ps = sem("k16_ps")
        k16_sb = sem("k16_sb"); kT_ready = sem("kT_ready"); kf_ps = sem("kf_ps"); kf_ready = sem("kf_ready")
        var_ready = sem("var_ready"); rstd_ready = sem("rstd_ready")
        xn_ready = sem("xn_ready"); xnT_ps = sem("xnT_ps"); xnT_ready = sem("xnT_ready"); xz_ps = sem("xz_ps")
        conv_ready = sem("conv_ready"); xc_ready = sem("xc_ready"); sz_ready = sem("sz_ready"); ssm_ps = sem("ssm_ps")
        bc_hi = sem("bc_hi"); sp_ready = sem("sp_ready"); sq_in = sem("sq_in"); sq_out = sem("sq_out")
        parts_ready = sem("parts_ready"); dt_ready = sem("dt_ready"); abar_ready = sem("abar_ready")
        bc_ps = sem("bc_ps"); b_used = sem("b_used"); c_used = sem("c_used"); scan_done = sem("scan_done"); hc_ready = sem("hc_ready"); y_sum = sem("y_sum")
        yv_ready = sem("yv_ready"); op_ps = sem("op_ps"); x1_ready = sem("x1_ready"); res_ready = sem("res_ready")
        added = sem("added");
        pen_ready = sem("pen_ready"); k_ps = sem("k_ps"); k_ready = sem("k_ready"); v_ps = sem("v_ps")
        v_ready = sem("v_ready"); x1T_ps = sem("x1T_ps"); x1T_ready = sem("x1T_ready"); q_ps = sem("q_ps")
        q_ready = sem("q_ready"); s_ps = sem("s_ps"); s_ready = sem("s_ready"); flags_ready = sem("flags_ready")
        top_found = sem("top_found"); counted = sem("counted"); ties_ready = sem("ties_ready")
        flags_moved = sem("flags_moved"); top_ready = sem("top_ready"); etop_ready = sem("etop_ready"); ssum_ready = sem("ssum_ready"); lnsum_ready = sem("lnsum_ready")
        ebias_ready = sem("ebias_ready"); prob_ready = sem("prob_ready"); masked_ready = sem("masked_ready")
        aT_ps = sem("aT_ps"); aT_ready = sem("aT_ready"); c_ps = sem("c_ps")
        c_ready = sem("c_ready")
        film_ps = sem("film_ps"); xs_ready = sem("xs_ready"); xf_ps = sem("xf_ps"); Y_ready = sem("Y_ready")
        y_ps = sem("y_ps"); n3_ready = sem("n3_ready"); n3T_ps = sem("n3T_ps"); hT_ready = sem("hT_ready")
        h1_ps = sem("h1_ps"); gT_ready = sem("gT_ready"); h2_ps = sem("h2_ps"); x2_ready = sem("x2_ready")
        x2T_ps = sem("x2T_ps"); x2T_ready = sem("x2T_ready"); lg_ps = sem("lg_ps"); wd_ready = sem("wd_ready")
        wdT_ps = sem("wdT_ps"); wdT_ready = sem("wdT_ready"); mb_ps = sem("mb_ps");
        eh_ps = sem("eh_ps"); eg_ready = sem("eg_ready"); eo_ps = sem("eo_ps"); wexp_in = sem("wexp_in"); wexp_out = sem("wexp_out"); eo_used = sem("eo_used")
        out_ready = sem("out_ready")

        block = ctx.enter_context(nc.Block())
        C1 = log1p_coefficients()
        MAGIC = 1.5 * 2.0 ** 23
        TWO_PI = float(2 * np.pi)

        def tails_at(g):
            steps_ = [(b, g - NH * R * (b + 1) - NH + (b == B - 1)) for b in range(B)]
            return [(b, i) for b, i in steps_ if FIRST <= i <= LAST]

        def mean_at(g):
            t, k = divmod(g, NH)
            return t - 2 if k == 0 and 2 <= t <= B * R else None

        def values_at(g):
            return g == 1 or NH * R < g < TILES and g % (NH * R) == NH

        AHEAD = 2
        FIRST, LAST = -1, 8
        HIDDEN = {4: (0, 1), 5: (2,), 6: (3, 4), 7: (5, 6, 7)}
        OUTPUTS = {5: (0, 1), 6: (2, 3), 7: (4, 5), 8: (6, 7)}
        def queries_at(g):
            return g + AHEAD + 1 < TILES and (g + AHEAD + 1) % (NH * R) == 0

        END = NH * R * B + NH + LAST

        @block.sync
        def _(sp):
            sp.dma_start(cols[:, :], a["cols"]).then_inc(ld_cols, 16)
            sp.dma_start(xs_[:, :, :, :].rearrange("p b r d -> p (b r) d"),
                         a["x"].rearrange("b (r p) d -> p (b r) d", p=P)).then_inc(ld_x, 16)
            sp.dma_start(ident[:, :], a["ident"]).then_inc(ld_small, 16)
            sp.dma_start(sel_c[:, :], a["sel"]).then_inc(ld_small, 16)
            sp.dma_start(wts[:, :], a["wts"]).then_inc(ld_w, 16)
            sp.dma_start(rows[:, :], a["rows"].to_broadcast([P, NROWS])).then_inc(ld_rows, 16)
            for dst, name in ((a_re, "a_re"), (a_im, "a_im"), (c_1, "c_1"), (c_2, "c_2"), (dskip, "dskip")):
                sp.dma_start(dst[:, :], a[name]).then_inc(ld_s4, 16)
            sp.dma_start(steps[:, :, :].rearrange("p a b -> p (a b)"), a["steps"].to_broadcast([P, 2 * L16])).then_inc(ld_s4, 16)
            sp.dma_start(wkv[:, :], a["wkv"]).then_inc(ld_small, 16)
            sp.dma_start(tmask8[:, :], a["tmask"]).then_inc(ld_small, 16)
            sp.dma_start(iota8[:, :], a["iota8"].to_broadcast([P, NE])).then_inc(ld_small, 16)
            sp.dma_start(ctxT[:, :], a["ctxT"][0]).then_inc(ld_ctx, 16)
            sp.dma_start(gmask8[:, :], a["gmask"][0:1, :].to_broadcast([P, G])).then_inc(ld_ctx, 16)
            sp.dma_start(dft[:, :, :, :], a["dft"]).then_inc(ld_dft, 16)
            sp.dma_start(idft[:, :, :], a["idft"]).then_inc(ld_dft, 16)
            sp.wait_ge(k16_sb, 2)
            for r in range(R):
                sp.dma_start(kT[:, r, :], k16[r * 8:(r + 1) * 8, :, :]).then_inc(k16_moved, 16)
            sp.dma_start(moe_w1[:, :, :, :], a["moe_w1"]).then_inc(ld_moe, 16)
            sp.dma_start(moe_w2[:, :, :, :], a["moe_w2"]).then_inc(ld_moe, 16)
            sp.dma_start(moe_b2[:, :], a["moe_b2"]).then_inc(ld_moe, 16)
            for g in range(END):
                t, k = divmod(g, NH)
                if k == 0 and 1 <= t <= B * R:
                    sp.wait_ge(flags_ready, t)
                    sp.dma_start(flagrow[:, :].rearrange("o (p k) -> o p k", k=NH), flag[:, :]).then_inc(flags_moved, 16)
                b = g // (NH * R)
                if values_at(g) and b + 1 < B:
                    sp.wait_ge(k_ps, b + 1)
                    sp.wait_ge(v_ps, 4 * (b + 1))
                    sp.wait_ge(pen_ready, b + 1)
                    sp.dma_start(ctxT[:, :], a["ctxT"][b + 1]).then_inc(ld_ctx, 16)
                    sp.dma_start(gmask8[:, :], a["gmask"][b + 1:b + 2, :].to_broadcast([P, G])).then_inc(ld_ctx, 16)
                for b, i in tails_at(g):
                    if i == LAST:
                        sp.wait_ge(out_ready, b + 1)
                        sp.dma_start(a["out"][b].rearrange("(r p) d -> p r d", p=P), outt[:, :, :]).then_inc(out_stored, 16)
            sp.wait_ge(out_stored, 16 * B)

        @block.gpsimd
        def _(pool):
            n = [0]
            nln = [0]

            def link(ins):
                n[0] += 1
                ins.then_inc(pool_step, 1)
                pool.wait_ge(pool_step, n[0])

            def layernorm(k):
                nln[0] += 1
                pool.wait_ge(var_ready, nln[0])
                link(pool.tensor_scalar(rstd[:, k, :], mv[:, k, :, 1], EPS, None, ALU.add))
                pool.tensor_tensor(rstd[:, k, :], rstd[:, k, :], half[:, :], ALU.pow).then_inc(rstd_ready, 1)

            link(pool.memset(half[:, :], -0.5))
            layernorm(0)
            link(pool.memset(onesb[:, :], 1.0))
            link(pool.memset(phase[0:64, 0:1], 0.25))
            link(pool.memset(phase[64:128, 0:1], 0.5))
            link(pool.tensor_copy(phase[:, 1:2], phase[:, 0:1]))
            link(pool.memset(abar[:, :, :, :, 0:1].rearrange("p u c n t -> p (u c n) t"), 0.0))
            pool.sem_inc(consts_set, 1)
            pool.wait_ge(s4_small, 1)
            turn, are = sv[0], sv[1]
            bc = lambda v: v.unsqueeze(1).to_broadcast([P, L16, D])
            st = lambda i: steps[:, i, :].unsqueeze(2).to_broadcast([P, L16, D])
            link(pool.tensor_tensor(w_exp, bc(are), st(0), ALU.mult))
            link(pool.tensor_tensor(w_ph, bc(turn), st(0), ALU.mult))
            pool.sem_inc(s4_arg, 1)
            layernorm(0)
            link(pool.tensor_tensor(u_exp, bc(are), st(1), ALU.mult))
            link(pool.tensor_tensor(u_ph, bc(turn), st(1), ALU.mult))
            pool.sem_inc(s4_arg, 1)
            layernorm(1)
            layernorm(0)
            pool.wait_ge(s4_fun, 5)
            pool.wait_ge(s4_gain, 1)
            link(pool.tensor_tensor(w_ph, w_exp, w_ph, ALU.mult))
            layernorm(1)
            layernorm(0)
            link(pool.tensor_tensor(u_ph, u_ph, bc(sv[10]), ALU.mult))
            link(pool.tensor_tensor(u_ph2, u_ph2, bc(sv[11]), ALU.mult))
            link(pool.tensor_tensor(u_ph, u_ph, u_ph2, ALU.add))
            link(pool.tensor_tensor(u_ph, u_ph, u_exp, ALU.mult))
            pool.sem_inc(s4_mats, 1)
            layernorm(1)

            def penalty(b):
                pool.wait_ge(ld_ctx, 32 * (b + 1))
                if b == 1:
                    pool.wait_ge(k_ps, 1)
                elif b >= 2:
                    pool.wait_ge(s_ps, 4 * R * NH * (b - 1))
                pool.tensor_scalar(pen[b % 2], gmask8[:, :], PENALTY, -PENALTY, ALU.mult, ALU.add).then_inc(pen_ready, 1)

            penalty(0)
            layernorm(1)

            for g in range(END):
                t, k = divmod(g, NH)
                if 1 <= t <= B * R and k == 0:
                    pool.wait_ge(ties_ready, t)
                    pool.wait_ge(counted, NH * t)
                    if t >= 2:
                        pool.wait_ge(flags_moved, 16 * (t - 1))
                    pool.tensor_tensor(flag[:, :], counts[:, :], tie[:, :], ALU.add).then_inc(flags_ready, 1)
                if 1 <= t <= B * R and k == 1:
                    pool.wait_ge(lnsum_ready, t)
                    pool.tensor_tensor(ebias[:, :], ngmax[:, :], lnsum[:, :], ALU.subtract).then_inc(ebias_ready, 1)
                if 1 <= t <= B * R and k == 2:
                    su = s[:, (t - 1) % 2]
                    pool.wait_ge(masked_ready, NH * (t - 1) + 2)
                    if t >= 2:
                        pool.wait_ge(aT_ps, 4 * (t - 1))
                    pool.tensor_tensor(avg[:, :], su[:, 0, :], su[:, 1, :], ALU.add).then_inc(added, 1)
                if 1 <= t <= B * R and k == 3:
                    pool.wait_ge(masked_ready, NH * t)
                    pool.tensor_tensor(su[:, 2, :], su[:, 2, :], su[:, 3, :], ALU.add).then_inc(added, 1)
                    pool.wait_ge(added, 3 * (t - 1) + 2)
                    pool.tensor_tensor(avg[:, :], avg[:, :], su[:, 2, :], ALU.add).then_inc(added, 1)
                if k == 1 and t % R == 1 and t // R + 1 < B:
                    penalty(t // R + 1)
                for b, i in tails_at(g):
                    for q in {-1: (2,), 2: (3,), 3: (4, 5), 8: (6,)}.get(i, ()):
                        layernorm(q)

        @block.scalar
        def _(act):
            A = nc.scalar.activation
            n = [0]

            def link(ins):
                n[0] += 1
                ins.then_inc(act_step, 1)
                act.wait_ge(act_step, n[0])

            def normed(b):
                act.wait_ge(xnT_ps, b + 1)
                A(xnT, TT[:, 0, 0:T], ACT.Identity, scale=col("ln_g"), bias=col("ln_b")).then_inc(xnT_ready, 1)

            def silus(b):
                act.wait_ge(conv_ready, b + 1)
                A(xc[:, b % 2], cv, ACT.Silu).then_inc(xc_ready, 1)
                act.wait_ge(xz_ps, 2 * b + 2)
                A(sz[:, b % 2], TT[:, 1, :].rearrange("p (c t) -> p c t", c=CH), ACT.Silu).then_inc(sz_ready, 1)

            def softplus(b):
                act.wait_ge(ssm_ps, 2 * b + 1)
                for c in range(CH):
                    A(sp_a[:, c, :], TT[:, 0, T:2 * T], ACT.Abs, scale=col("w_dt", c), bias=col("b_dt", c))
                    link(A(sp_p[:, c, :], TT[:, 0, T:2 * T], ACT.Relu, scale=col("w_dt", c), bias=col("b_dt", c)))
                A(sp_a, sp_a, ACT.Exp, scale=-1.0).then_inc(sp_ready, 1)
                act.wait_ge(ssm_ps, 2 * b + 2)
                A(parts[:, b % 2, :], TT[0:96, 1, 0:T], ACT.Copy).then_inc(bc_hi, 1)

            def square(b):
                act.wait_ge(sq_in, b + 1)
                A(sp_q, sp_r, ACT.Square).then_inc(sq_out, 1)

            def decays(b, u):
                if u == 0:
                    act.wait_ge(dt_ready, b + 1)
                for c in range(CH):
                    if NU * b + u >= 2:
                        act.wait_ge(scan_done, CH * (NU * b + u - 2) + c + 1)
                    for j in range(UN):
                        i = UN * u + j
                        ins = A(abar[:, u % 2, c, j, 1:T], dt_[:, b % 2, c, 1:T], ACT.Exp,
                                scale=a_neg[:, c * NS + i:c * NS + i + 1])
                    ins.then_inc(abar_ready, 1)

            def kernel(h):
                act.wait_ge(k16_ps, h + 1)
                A(k16[:, :, h * D // 2:(h + 1) * D // 2], TT[0:L16, :, :].rearrange("p a (d j) -> p j (a d)", j=L16),
                  ACT.Copy).then_inc(k16_sb, 1)

            def keys(b):
                act.wait_ge(k_ps, b + 1)
                A(KT[:, :], S[:, 0:G], ACT.Copy).then_inc(k_ready, 1)

            def queries(b):
                at_ = TT if b == 0 else M
                act.wait_ge(x1T_ps, b + 1)
                A(x1T[:, :], at_[:, 0, 0:T], ACT.Copy).then_inc(x1T_ready, 1)
                act.wait_ge(q_ps, b + 1)
                A(QT[:, :], at_[:, 1, 0:T], ACT.Copy, scale=SCALE).then_inc(q_ready, 1)

            act.wait_ge(ld_cols, 16)
            A(a_neg[:, :], cols[:, COLS["a_log"][0]:COLS["a_log"][1]], ACT.Exp).then_inc(a_exp, 1)
            normed(0)
            silus(0)
            softplus(0)
            act.wait_ge(ld_small, 32)
            A(sel[:, :], sel_c[:, :], ACT.Copy).then_inc(params_ready, 1)
            square(0)
            act.wait_ge(consts_set, 1)
            for b in range(B):
                decays(b, 0)
                if b + 1 < B:
                    normed(b + 1)
                else:
                    kernel(0)
                decays(b, 1)
                if b + 1 == B:
                    kernel(1)
                if b == 0:
                    act.wait_ge(s4_sin_in, 1)
                    A(sv[4], sv[4], ACT.Sin, scale=TWO_PI)
                    A(sv[5], sv[5], ACT.Sin, scale=TWO_PI)
                    A(sv[6], sv[6], ACT.Sin, scale=TWO_PI / 2)
                    A(sv[7], sv[1], ACT.Tanh, scale=0.5).then_inc(s4_sin, 1)
                if b + 1 < B:
                    silus(b + 1)
                decays(b, 2)
                if b + 1 < B:
                    softplus(b + 1)
                decays(b, 3)
                if b == 0:
                    act.wait_ge(s4_arg, 2)
                    A(w_exp, w_exp, ACT.Exp).then_inc(s4_fun, 1)
                    A(u_exp, u_exp, ACT.Exp).then_inc(s4_fun, 1)
                if b + 1 < B:
                    square(b + 1)
                if b == 1:
                    act.wait_ge(s4_th_in, 2)
                    A(w_ph, w_ph, ACT.Sin, scale=TWO_PI).then_inc(s4_fun, 1)
                    A(u_ph, u_ph, ACT.Sin, scale=TWO_PI).then_inc(s4_fun, 1)
                    A(u_ph2, u_ph2, ACT.Sin, scale=TWO_PI).then_inc(s4_fun, 1)

            def evacuate(g):
                t, k = divmod(g, NH)
                if t >= 2:
                    act.wait_ge(added, 3 * (t - 2) + (1 if k < 2 else 3))
                act.wait_ge(s_ps, 4 * g + 2)
                A(s[:, t % 2, k, 0:1024], S[:, 0:1024], ACT.Copy).then_inc(s_ready, 1)
                act.wait_ge(s_ps, 4 * g + 4)
                A(s[:, t % 2, k, 1024:G], S[:, 1024:G], ACT.Copy).then_inc(s_ready, 1)

            def count(g):
                t, k = divmod(g, NH)
                act.wait_ge(top_found, g + 1)
                if t:
                    act.wait_ge(flags_ready, t)
                if g:
                    act.wait_ge(counted, g)
                A(junk, s[:, t % 2, k, :], ACT.Sign, scale=-1.0, bias=top[:, t % 2, k, TOPK - 1:TOPK],
                  accum_out=counts[:, k:k + 1]).then_inc(counted, 1)

            def exp_top(t):
                act.wait_ge(top_ready, t + 1)
                A(etop[:, :, :], etop[:, :, :], ACT.Exp).then_inc(etop_ready, 1)

            def log_sums(t):
                act.wait_ge(ssum_ready, t + 1)
                A(lnsum[:, :], ssum[:, :], ACT.Ln, scale=float(NH)).then_inc(lnsum_ready, 1)

            def exponents(t, k):
                act.wait_ge(ebias_ready, t + 1)
                if NH * t + k >= 2:
                    act.wait_ge(masked_ready, NH * t + k - 1)
                A(prob[:, k % 2, :], s[:, t % 2, k, :], ACT.Exp, bias=ebias[:, k:k + 1]).then_inc(prob_ready, 1)

            def turned(t):
                if t >= 1:
                    act.wait_ge(c_ps, t)
                for g in range(4):
                    act.wait_ge(aT_ps, 4 * t + g + 1)
                    w = min(4, GC - 4 * g)
                    rows_ = P if w == 4 else GL
                    A(aT[0:rows_, 4 * g:4 * g + w, :], M[0:rows_, g % 2, 0:w * P].rearrange("p (g d) -> p g d", d=P),
                      ACT.Copy).then_inc(aT_ready, 1)

            def context(t):
                act.wait_ge(c_ps, t + 1)
                if t >= 2 and t % R == 0:
                    act.wait_ge(film_ps, t // R)
                A(cT[:, t % R * P:(t % R + 1) * P], M[:, 0, 0:P], ACT.Copy).then_inc(c_ready, 1)

            def tail(b, i):
                if i == 3:
                    act.wait_ge(n3T_ps, b + 1)
                    A(hT[:, :], TT[:, 0, 0:T], ACT.Identity, scale=col("ffn_g"), bias=col("ffn_b")).then_inc(hT_ready, 1)
                    for f in range(FT):
                        act.wait_ge(h1_ps, FT // 2 * b + f // 2 + 1)
                        A(gT[:, f, :], TT[:, 1 - f // 2, (f % 2) * T:(f % 2 + 1) * T], ACT.Gelu,
                          bias=col("ffn_b1", f)).then_inc(gT_ready, 1)
                if i == 4:
                    act.wait_ge(x2T_ps, b + 1)
                    A(x2T[:, :], TT[:, 0, 0:T], ACT.Copy).then_inc(x2T_ready, 1)
                for e in HIDDEN.get(i, ()):
                    if e >= 2:
                        act.wait_ge(eo_ps, NE * b + e - 1)
                    for f in range(FT):
                        act.wait_ge(eh_ps, FT // 2 * (NE * b + e) + f // 2 + 1)
                        A(gm[:, e % 2, f, :], TT[:, f // 2, (f % 2) * T:(f % 2 + 1) * T], ACT.Gelu,
                          bias=col("moe_b1", FT * e + f)).then_inc(eg_ready, 1)
                if i == 6:
                    act.wait_ge(wdT_ps, b + 1)
                    A(wdT[:, :], M[0:NE, 1, 0:T], ACT.Copy).then_inc(wdT_ready, 1)

            keys(0)
            queries(0)
            act.wait_ge(hc_ready, CH * NU * B)
            evacuate(0)
            act.wait_ge(yv_ready, B)
            evacuate(1)
            for g in range(END):
                t, k = divmod(g, NH)
                if g + AHEAD < TILES and (g + AHEAD) % (NH * R) == 0:
                    keys((g + AHEAD) // (NH * R))
                if k == 0 and 1 <= t <= B * R:
                    count(g - 1)
                if k == 1 and 1 <= t <= B * R:
                    exp_top(t - 1)
                for b, i in tails_at(g):
                    if i == 5:
                        act.wait_ge(wexp_in, b + 1)
                        A(wtop[:, :, 1], wtop[:, :, 0], ACT.Exp).then_inc(wexp_out, 1)
                if g + AHEAD < TILES and k != 2:
                    evacuate(g + AHEAD)
                if queries_at(g):
                    queries(t // R + 1)
                if k == 1 and 1 <= t <= B * R:
                    log_sums(t - 1)
                if 1 <= t <= B * R:
                    if k == 1:
                        exponents(t - 1, 0)
                        exponents(t - 1, 1)
                    if k == 2:
                        exponents(t - 1, 2)
                        exponents(t - 1, 3)
                if g + AHEAD < TILES and k == 2:
                    evacuate(g + AHEAD)
                if mean_at(g) is not None:
                    turned(mean_at(g))
                    context(mean_at(g))
                for b, i in tails_at(g):
                    if (b, i) == (B - 1, 0):
                        turned(B * R - 1)
                        context(B * R - 1)
                    tail(b, i)
                if values_at(g):
                    for q in range(4):
                        act.wait_ge(v_ps, 4 * (t // R) + q + 1)
                        w = min(4, GC - 4 * q)
                        rows_ = P if w == 4 else GL
                        A(V[0:rows_, 4 * q:4 * q + w, :], M[0:rows_, q % 2, 0:w * D].rearrange("p (g d) -> p g d", d=D),
                          ACT.Copy).then_inc(v_ready, 1)
                if k and g <= TILES:
                    count(g - 1)

        @block.tensor
        def _(pe):
            mm = nc.tensor.matmul

            def normed(b):
                pe.wait_ge(xn_ready, b + 1)
                if b >= 1:
                    pe.wait_ge(sp_ready, b)
                for r in range(R):
                    ins = nc.tensor.transpose(TT[:, 0, r * P:(r + 1) * P], xn[:, r, :], ident[:, :])
                ins.then_inc(xnT_ps, 1)
                pe.wait_ge(xnT_ready, b + 1)
                if b >= 1:
                    pe.wait_ge(parts_ready, b)
                for j in range(4):
                    ins = mm(TT[:, j // 2, (j % 2) * T:(j % 2 + 1) * T], wt("w_in", j, P), xnT, start=True, stop=True)
                    if j % 2:
                        ins.then_inc(xz_ps, 1)

            def projected(b):
                pe.wait_ge(xc_ready, b + 1)
                for c in range(CH):
                    ins = mm(TT[:, 0, T:2 * T], wt("wx_raw", c, P), xc[:, b % 2, c, :], start=(c == 0), stop=(c == CH - 1))
                ins.then_inc(ssm_ps, 1)
                pe.wait_ge(sz_ready, b + 1)
                for c in range(CH):
                    ins = mm(TT[0:96, 1, 0:T], wt("wx_bc", c, 96), xc[:, b % 2, c, :], start=(c == 0), stop=(c == CH - 1))
                ins.then_inc(ssm_ps, 1)

            def spread(b, u):
                if u == 0:
                    pe.wait_ge(parts_ready, b + 1)
                for which, used in ((0, b_used), (1, c_used)):
                    if NU * b + u >= 1:
                        pe.wait_ge(used, NU * b + u)
                    for j in range(UN):
                        i = which * NS + UN * u + j
                        ins = mm(S[:, which * 1024 + j * T:which * 1024 + (j + 1) * T], sel[:, i:i + 1].to_broadcast([96, P]),
                                 parts[:, b % 2, :], start=True, stop=True)
                    ins.then_inc(bc_ps, 1)

            def state_sum(b, u):
                if u == 0 and b >= 1:
                    pe.wait_ge(res_ready, b)
                for c in range(CH):
                    pe.wait_ge(hc_ready, CH * (NU * b + u) + c + 1)
                    for j in range(UN):
                        ins = mm(M[:, c, 0:T], ident[:, :], hst[:, u % 2, c, j, :], start=(u + j == 0),
                                 stop=(u == NU - 1 and j == UN - 1))
                    ins.then_inc(y_sum, 1)

            def out_projected(b):
                pe.wait_ge(yv_ready, b + 1)
                for r in range(R):
                    for c in range(CH):
                        ins = mm(M[:, 0, T + r * D:T + (r + 1) * D], yv[:, c, r * P:(r + 1) * P], wt("w_out", c, D),
                                 start=(c == 0), stop=(c == CH - 1))
                ins.then_inc(op_ps, 1)

            def s4_kernel(h):
                if h == 0:
                    pe.wait_ge(s4_mats, 1)
                    pe.wait_ge(sp_ready, B)
                    pe.wait_ge(parts_ready, B)
                    pe.wait_ge(conv_ready, B)
                    pe.wait_ge(sz_ready, B)
                else:
                    pe.wait_ge(k16_sb, 1)
                for d in range(h * D // 2, (h + 1) * D // 2):
                    at_ = (d - h * D // 2) * L16
                    ins = mm(TT[0:L16, at_ // 512, at_ % 512:at_ % 512 + L16], u_ph[:, :, d], w_ph[:, :, d], start=True, stop=True)
                ins.then_inc(k16_ps, 1)

            def s4_spectrum():
                pe.wait_ge(k16_sb, 2)
                pe.wait_ge(kT_ready, 1)
                pe.wait_ge(ld_dft, 32)
                for j, cols_ in enumerate(((0, 1), (4, 3), (5, 1))):
                    for q in range(2):
                        for r in range(R):
                            ins = mm(TT[:, j // 2, (j % 2) * 256 + q * D:(j % 2) * 256 + (q + 1) * D],
                                     dft[:, r, cols_[q], :], kT[:, r, :], start=(r == 0), stop=(r == R - 1))
                ins.then_inc(kf_ps, 1)

            def queries(b):
                at_ = TT if b == 0 else M
                if b == 0:
                    pe.wait_ge(kf_ready, 1)
                pe.wait_ge(x1_ready, b + 1)
                if outs[0]:
                    pe.wait_ge(eo_used, outs[0])
                for q in range(R):
                    ins = nc.tensor.transpose(at_[:, 0, q * P:(q + 1) * P], xs_[:, b, q, :], ident[:, :])
                ins.then_inc(x1T_ps, 1)
                pe.wait_ge(x1T_ready, b + 1)
                mm(at_[:, 1, 0:T], wt("wq", 0, D), x1T[:, :], start=True, stop=True).then_inc(q_ps, 1)
                pe.wait_ge(q_ready, b + 1)

            def keys(b):
                pe.wait_ge(ld_ctx, 32 * (b + 1))
                if b:
                    pe.wait_ge(s_ready, 2 * R * NH * b)
                else:
                    pe.wait_ge(c_used, NU * B)
                for q in range(4):
                    w = min(512, G - 512 * q)
                    ins = mm(S[:, 512 * q:512 * q + w], wkv[:, 0:D], ctxT[:, 512 * q:512 * q + w], start=True, stop=True)
                ins.then_inc(k_ps, 1)

            def scores(g):
                t, k = divmod(g, NH)
                b, r = divmod(t, R)
                if k == 0 and r == 0:
                    pe.wait_ge(q_ready, b + 1)
                    pe.wait_ge(k_ready, b + 1)
                    pe.wait_ge(pen_ready, b + 1)
                for q in range(4):
                    w = min(512, G - 512 * q)
                    if g:
                        pe.wait_ge(s_ready, 2 * g - (1 if q < 2 else 0))
                    mm(S[:, 512 * q:512 * q + w], onesb[k * DH:k * DH + 1, :], pen[b % 2][k * DH:k * DH + 1, 512 * q:512 * q + w],
                       start=True, stop=False)
                    mm(S[:, 512 * q:512 * q + w], QT[k * DH:(k + 1) * DH, r * P:(r + 1) * P],
                       KT[k * DH:(k + 1) * DH, 512 * q:512 * q + w], start=False, stop=True).then_inc(s_ps, 1)

            outs = [0]
            pe.wait_ge(ld_small, 32)
            pe.wait_ge(ld_w, 16)
            normed(0)
            projected(0)
            pe.wait_ge(params_ready, 1)
            spread(0, 0)
            for b in range(B):
                for u in range(NU):
                    if u == 2 and b + 1 < B:
                        projected(b + 1)
                    if u + 1 < NU:
                        spread(b, u + 1)
                    elif b + 1 < B:
                        spread(b + 1, 0)
                    if u == 0 and b + 1 < B:
                        normed(b + 1)
                    if b == B - 1:
                        if u == 0:
                            s4_kernel(1)
                        if u == 2:
                            s4_spectrum()
                    state_sum(b, u)
                    if b == B - 2 and u == NU - 1:
                        s4_kernel(0)
                if b == B - 1:
                    keys(0)
                    queries(0)
                    scores(0)
                out_projected(b)
            scores(1)

            def values(b):
                if b == 0:
                    pe.wait_ge(res_ready, B)
                if outs[0]:
                    pe.wait_ge(eo_used, outs[0])
                for g in range(4):
                    if g >= 2:
                        pe.wait_ge(v_ready, 4 * b + g - 1)
                    for i in range(4 * g, min(4 * g + 4, GC)):
                        w = P if i < GC - 1 else GL
                        ins = mm(M[0:w, g % 2, (i % 4) * D:(i % 4 + 1) * D], ctxT[:, i * P:i * P + w], wkv[:, D:2 * D],
                                 start=True, stop=True)
                    ins.then_inc(v_ps, 1)
                pe.wait_ge(v_ready, 4 * b + 4)

            def mean_turned(t):
                if outs[0]:
                    pe.wait_ge(eo_used, outs[0])
                pe.wait_ge(added, 3 * (t + 1))
                for g in range(4):
                    if g >= 2:
                        pe.wait_ge(aT_ready, 4 * t + g - 1)
                    for i in range(4 * g, min(4 * g + 4, GC)):
                        w = P if i < GC - 1 else GL
                        ins = nc.tensor.transpose(M[0:w, g % 2, (i % 4) * P:(i % 4 + 1) * P],
                                                  avg[:, i * P:i * P + w], ident[:, :])
                    ins.then_inc(aT_ps, 1)
                pe.wait_ge(aT_ready, 4 * (t + 1))
                for i in range(GC):
                    w = P if i < GC - 1 else GL
                    ins = mm(M[:, 0, 0:P], V[0:w, i, :], aT[0:w, i, :], start=(i == 0), stop=(i == GC - 1))
                ins.then_inc(c_ps, 1)
                pe.wait_ge(c_ready, t + 1)

            def tail(b, i):
                if i == 0:
                    if b == 0:
                        pe.wait_ge(kf_ready, 1)
                        pe.wait_ge(params_ready, 2)
                    if b >= 1:
                        pe.wait_ge(eg_ready, FT * NE * b)
                    for j, name in enumerate(("film_in", "film_out")):
                        for r in range(R):
                            ins = mm(TT[:, j, r * T:(r + 1) * T], cT[:, r * P:(r + 1) * P], wt(name, 0, 2 * D), start=True, stop=True)
                    ins.then_inc(film_ps, 1)
                if i == 1:
                    pe.wait_ge(xs_ready, b + 1)
                    for q in range(4):
                        for r in range(R):
                            ins = mm(TT[:, 0, q * D:(q + 1) * D], dft[:, r, q, :], n2[:, r, :], start=(r == 0), stop=(r == R - 1))
                    ins.then_inc(xf_ps, 1)
                if i == 2:
                    pe.wait_ge(Y_ready, b + 1)
                    for r in range(R):
                        for q in range(4):
                            ins = mm(TT[:, 1, r * D:(r + 1) * D], idft[:, q, r * P:(r + 1) * P], Y[:, q, :],
                                     start=(q == 0), stop=(q == 3))
                    ins.then_inc(y_ps, 1)
                if i == 3:
                    pe.wait_ge(n3_ready, b + 1)
                    for r in range(R):
                        ins = nc.tensor.transpose(TT[:, 0, r * P:(r + 1) * P], n2[:, r, :], ident[:, :])
                    ins.then_inc(n3T_ps, 1)
                    pe.wait_ge(hT_ready, b + 1)
                    for f in range(FT):
                        ins = mm(TT[:, 1 - f // 2, (f % 2) * T:(f % 2 + 1) * T], wt("w1", f, P), hT[:, :], start=True, stop=True)
                        if f % 2:
                            ins.then_inc(h1_ps, 1)
                    pe.wait_ge(gT_ready, FT * (b + 1))
                    for r in range(R):
                        for f in range(FT):
                            ins = mm(TT[:, 1, r * D:(r + 1) * D], gT[:, f, r * P:(r + 1) * P], wt("w2", f, D),
                                     start=(f == 0), stop=(f == FT - 1))
                    ins.then_inc(h2_ps, 1)
                if i == 4:
                    pe.wait_ge(x2_ready, b + 1)
                    for r in range(R):
                        ins = nc.tensor.transpose(TT[:, 0, r * P:(r + 1) * P], x2[:, r, :], ident[:, :])
                    ins.then_inc(x2T_ps, 1)
                    pe.wait_ge(x2T_ready, b + 1)
                    for r in range(R):
                        ins = mm(M[:, 1, r * NE:(r + 1) * NE], x2T[:, r * P:(r + 1) * P], wt("router", 0, NE), start=True, stop=True)
                    ins.then_inc(lg_ps, 1)
                    if b == 0:
                        pe.wait_ge(ld_moe, 48)
                if i == 7:
                    pe.wait_ge(wdT_ready, b + 1)
                    for r in range(R):
                        ins = mm(M[:, 1, r * D:(r + 1) * D], wdT[:, r * P:(r + 1) * P], moe_b2[:, :], start=True, stop=True)
                    ins.then_inc(mb_ps, 1)
                hidden, outputs = list(HIDDEN.get(i, ())), list(OUTPUTS.get(i, ()))
                while hidden or outputs:
                    if hidden:
                        expert_hidden(b, hidden.pop(0))
                    if outputs:
                        expert_out(b, outputs.pop(0))
                if i == 6:
                    pe.wait_ge(wd_ready, b + 1)
                    for r in range(R):
                        ins = nc.tensor.transpose(M[0:NE, 1, r * P:(r + 1) * P], wd[:, r, :], ident[:, :])
                    ins.then_inc(wdT_ps, 1)

            def expert_hidden(b, e):
                for f in range(FT):
                    if e >= 1 and f % 2 == 0:
                        pe.wait_ge(eg_ready, FT * (NE * b + e - 1) + f + 2)
                    ins = mm(TT[:, f // 2, (f % 2) * T:(f % 2 + 1) * T], moe_w1[:, e, f, :], x2T[:, :],
                             start=True, stop=True)
                    if f % 2:
                        ins.then_inc(eh_ps, 1)

            def expert_out(b, e):
                pe.wait_ge(eg_ready, FT * NE * b + FT * (e + 1))
                if outs[0] and e % 2 == 0:
                    pe.wait_ge(eo_used, outs[0])
                for r in range(R):
                    for f in range(FT):
                        ins = mm(M[:, 0, (R * (e % 2) + r) * D:(R * (e % 2) + r + 1) * D], gm[:, e % 2, f, r * P:(r + 1) * P],
                                 moe_w2[:, e, f, :], start=(f == 0), stop=(f == FT - 1))
                ins.then_inc(eo_ps, 1)
                outs[0] += 1

            for g in range(END):
                t, k = divmod(g, NH)
                if g + AHEAD < TILES:
                    if (g + AHEAD) % (NH * R) == 0:
                        keys((g + AHEAD) // (NH * R))
                    scores(g + AHEAD)
                if mean_at(g) is not None:
                    mean_turned(mean_at(g))
                if queries_at(g):
                    queries(t // R + 1)
                for b, i in tails_at(g):
                    if (b, i) == (B - 1, 0):
                        mean_turned(B * R - 1)
                    tail(b, i)
                if values_at(g):
                    values(t // R)

        @block.vector
        def _(dve):
            n = [0]
            nln = [0]

            def link(ins, wait=True, meanwhile=None):
                n[0] += 1
                here = n[0]
                ins.then_inc(dve_step, 1)
                if meanwhile is not None:
                    meanwhile()
                if wait:
                    dve.wait_ge(dve_step, here)

            TS, TTN, STT = nc.vector.tensor_scalar, nc.vector.tensor_tensor, nc.vector.scalar_tensor_tensor

            def variance(k, src):
                for r in range(R):
                    link(nc.vector.bn_stats(stat[:, k, r, :], src[:, r, :]), r == R - 1)
                for r in range(R):
                    ins = nc.vector.bn_aggr(mv[:, k, r, :], stat[:, k, r, :])
                    if r < R - 1:
                        link(ins, False)
                ins.then_inc(var_ready, 1)

            def normalise(k, dst, src):
                nln[0] += 1
                dve.wait_ge(rstd_ready, nln[0])
                for r in range(R):
                    link(TS(dst[:, r, :], src[:, r, :], mv[:, k, r, 0:1], rstd[:, k, r:r + 1], ALU.subtract, ALU.mult), r == R - 1)

            def layernorm(k, dst, src):
                variance(k, src)
                normalise(k, dst, src)

            def normed(b):
                normalise(0, xn, xs_[:, b])
                dve.sem_inc(xn_ready, 1)

            def conv(b):
                dve.wait_ge(xz_ps, 2 * b + 1)
                for c in range(CH):
                    link(TS(cv[:, c, :], TT[:, 0, c * T:(c + 1) * T], col("conv_w", c * KC + KC - 1), col("conv_b", c),
                            ALU.mult, ALU.add), c == CH - 1)
                for j in range(1, KC):
                    for c in range(CH):
                        ins = STT(out=cv[:, c, j:T], in0=TT[:, 0, c * T:(c + 1) * T - j],
                                  scalar=col("conv_w", c * KC + KC - 1 - j), in1=cv[:, c, j:T], op0=ALU.mult, op1=ALU.add)
                        if c == CH - 1 and j == KC - 1:
                            ins.then_inc(conv_ready, 1)
                        else:
                            link(ins, c == CH - 1)

            def bc_parts(b):
                p_ = parts[:, b % 2, :]
                dve.wait_ge(bc_hi, b + 1)
                link(TTN(bc_r[:, :], TT[0:96, 1, 0:T], p_, ALU.subtract))
                link(nc.vector.tensor_copy(bc_m[:, :], bc_r[:, :]))
                link(TTN(bc_r[:, :], bc_r[:, :], bc_m[:, :], ALU.subtract), False)
                link(nc.vector.tensor_copy(p_[32:64, :], bc_m[32:64, :]))
                nc.vector.tensor_copy(p_[64:96, :], bc_r[64:96, :]).then_inc(parts_ready, 1)

            def softplus_w(b):
                dve.wait_ge(sp_ready, b + 1)
                link(TS(sp_q, sp_a, 2.0, None, ALU.add))
                link(nc.vector.reciprocal(sp_q, sp_q))
                link(TTN(sp_r, sp_a, sp_q, ALU.mult))
                dve.sem_inc(sq_in, 1)

            def softplus(b):
                dve.wait_ge(sq_out, b + 1)
                link(TS(sp_a, sp_q, C1[5], None, ALU.mult))
                for j in range(4, 0, -1):
                    link(STT(out=sp_a, in0=sp_a, scalar=C1[j], in1=sp_q, op0=ALU.add, op1=ALU.mult))
                link(STT(out=sp_a, in0=sp_a, scalar=C1[0], in1=sp_r, op0=ALU.add, op1=ALU.mult))
                link(TTN(dt_[:, b % 2], sp_a, sp_p, ALU.add))
                dve.sem_inc(dt_ready, 1)
                link(TTN(ux[:, b % 2], dt_[:, b % 2], xc[:, b % 2], ALU.mult))

            def unit(b, u):
                half_b, half_c = (S[:, i * 1024:(i + 1) * 1024].rearrange("p (n t) -> p n t", n=UN) for i in range(2))
                gu = NU * b + u
                dve.wait_ge(bc_ps, 2 * gu + 1)
                for c in range(CH):
                    if gu >= 2:
                        dve.wait_ge(y_sum, CH * (gu - 2) + c + 1)
                    link(TTN(hst[:, u % 2, c, :, :], ux[:, b % 2, c, :].unsqueeze(1).to_broadcast([P, UN, T]), half_b, ALU.mult),
                         c == CH - 1)
                dve.sem_inc(b_used, 1)
                for c in range(CH):
                    dve.wait_ge(abar_ready, CH * gu + c + 1)
                    hf = hst[:, u % 2, c, :, :].rearrange("p n t -> p (n t)")
                    nc.vector.tensor_tensor_scan(hf, abar[:, u % 2, c, :, :].rearrange("p n t -> p (n t)"), hf, 0.0,
                                                 ALU.mult, ALU.add).then_inc(scan_done, 1)
                dve.wait_ge(bc_ps, 2 * gu + 2)
                for c in range(CH):
                    dve.wait_ge(scan_done, CH * gu + c + 1)
                    TTN(hst[:, u % 2, c, :, :], hst[:, u % 2, c, :, :], half_c, ALU.mult).then_inc(hc_ready, 1)
                dve.wait_ge(hc_ready, CH * (gu + 1))
                dve.sem_inc(c_used, 1)

            def gated(b):
                dve.wait_ge(y_sum, CH * NU * (b + 1))
                dve.wait_ge(sz_ready, b + 1)
                for c in range(CH):
                    link(STT(out=yv[:, c, :], in0=xc[:, b % 2, c, :], scalar=col("d_param", c), in1=M[:, c, 0:T],
                             op0=ALU.mult, op1=ALU.add), c == CH - 1)
                link(TTN(yv, yv, sz[:, b % 2], ALU.mult))
                dve.sem_inc(yv_ready, 1)

            def residual(b):
                dve.wait_ge(op_ps, b + 1)
                link(STT(out=xs_[:, b], in0=xs_[:, b], scalar=2.0, in1=M[:, 0, T:2 * T].rearrange("p (r d) -> p r d", r=R),
                         op0=ALU.mult, op1=ALU.add))
                dve.sem_inc(res_ready, 1)
                variance(1, xs_[:, b])

            def residual_done(b):
                normalise(1, xs_[:, b], xs_[:, b])
                dve.sem_inc(x1_ready, 1)

            dve.wait_ge(ld_cols, 16)
            dve.wait_ge(ld_x, 16)
            variance(0, xs_[:, 0])
            normed(0)
            dve.wait_ge(a_exp, 1)
            link(TS(a_neg[:, :], a_neg[:, :], -1.0, None, ALU.mult), False)

            turn, are, dts, r_, sinb, cosb, sinh, th, k_, g_, gx, gy = sv
            LN2H = float(np.float32(0.693359375))
            LN2L = float(np.float32(np.log(2.0) - 0.693359375))

            def less_whole(dst, src, tmp, add=None):
                if add is not None:
                    link(TS(dst, src, add, None, ALU.add))
                    src = dst
                link(TS(tmp, src, MAGIC, None, ALU.add))
                link(TS(tmp, tmp, MAGIC, None, ALU.subtract))
                link(TTN(dst, src, tmp, ALU.subtract))

            def s4_steps():
                ldt = row("log_dt")
                dve.wait_ge(ld_rows, 16)
                dve.wait_ge(ld_s4, 96)
                link(TS(k_, ldt, float(np.log2(np.e)), MAGIC, ALU.mult, ALU.add))
                link(TS(k_, k_, MAGIC, None, ALU.subtract))
                link(STT(out=r_, in0=k_, scalar=-LN2H, in1=ldt, op0=ALU.mult, op1=ALU.add))
                link(STT(out=r_, in0=k_, scalar=-LN2L, in1=r_, op0=ALU.mult, op1=ALU.add))
                fact = [1.0 / 5040, 1.0 / 720, 1.0 / 120, 1.0 / 24, 1.0 / 6, 0.5, 1.0]
                link(TS(g_, r_, fact[0], None, ALU.mult))
                for c_ in fact[1:]:
                    link(STT(out=g_, in0=g_, scalar=c_, in1=r_, op0=ALU.add, op1=ALU.mult))
                link(TS(g_, g_, 1.0, None, ALU.add))
                link(TS(k_, k_, 127.0, 0.0, ALU.add, ALU.max))
                link(TS(ki[:, :], k_, 254.0, 2.0 ** 23, ALU.min, ALU.mult))
                link(TTN(dts, g_, ki[:, :].bitcast(F32), ALU.mult))
                link(TTN(are, dts, a_re, ALU.mult), False)
                link(TTN(turn, dts, a_im, ALU.mult))
                link(TS(turn, turn, float(1.0 / (2 * np.pi)), None, ALU.mult))
                less_whole(turn, turn, k_)
                dve.sem_inc(s4_small, 1)
                link(nc.vector.tensor_copy(sinb, turn), False)
                link(nc.vector.tensor_copy(sinh, turn), False)
                less_whole(cosb, turn, k_, 0.25)
                dve.sem_inc(s4_sin_in, 1)
                link(TS(c_2[64:128, :], c_2[64:128, :], -1.0, None, ALU.mult), False)

            def s4_gains():
                dve.wait_ge(s4_sin, 1)
                link(TS(k_, th, -1.0, 1.0, ALU.mult, ALU.add))
                link(nc.vector.reciprocal(k_, k_))
                link(STT(out=th, in0=th, scalar=2.0, in1=k_, op0=ALU.mult, op1=ALU.mult))
                link(TTN(cosb, th, cosb, ALU.mult), False)
                link(TTN(sinh, sinh, sinh, ALU.mult))
                link(STT(out=gx, in0=sinh, scalar=-2.0, in1=cosb, op0=ALU.mult, op1=ALU.add))
                link(STT(out=gy, in0=th, scalar=1.0, in1=sinb, op0=ALU.add, op1=ALU.mult))
                link(TTN(k_, a_re, a_re, ALU.mult), False)
                link(TTN(dts, a_im, a_im, ALU.mult))
                link(TTN(k_, k_, dts, ALU.add))
                link(nc.vector.reciprocal(k_, k_))
                link(TTN(r_, gx, a_re, ALU.mult), False)
                link(TTN(dts, gy, a_im, ALU.mult))
                link(TTN(r_, r_, dts, ALU.add))
                link(STT(out=r_, in0=r_, scalar=2.0, in1=k_, op0=ALU.mult, op1=ALU.mult))
                link(TTN(g_, gy, a_re, ALU.mult), False)
                link(TTN(dts, gx, a_im, ALU.mult))
                link(TTN(g_, g_, dts, ALU.subtract))
                link(STT(out=g_, in0=g_, scalar=2.0, in1=k_, op0=ALU.mult, op1=ALU.mult))
                link(TTN(gx, c_1, r_, ALU.mult), False)
                link(TTN(dts, c_2, g_, ALU.mult))
                link(TTN(gx, gx, dts, ALU.subtract))
                link(TTN(gy, c_1, g_, ALU.mult), False)
                link(TTN(dts, c_2, r_, ALU.mult))
                link(TTN(gy, gy, dts, ALU.add))
                dve.sem_inc(s4_gain, 1)

            def s4_angles():
                dve.wait_ge(s4_arg, 2)
                dve.wait_ge(consts_set, 1)
                link(TS(w_ph, w_ph, phase[:, 0:1], None, ALU.add), False)
                link(TS(u_ph2, u_ph, 0.5, None, ALU.add), False)
                link(TS(u_ph, u_ph, 0.25, None, ALU.add))
                for ph in (w_ph, u_ph, u_ph2):
                    link(TS(w_rnd, ph, MAGIC, None, ALU.add))
                    link(TS(w_rnd, w_rnd, MAGIC, None, ALU.subtract))
                    link(TTN(ph, ph, w_rnd, ALU.subtract))
                dve.sem_inc(s4_th_in, 2)

            conv(0)
            s4_steps()
            bc_parts(0)
            softplus_w(0)
            softplus(0)
            for b in range(B):
                unit(b, 0)
                if b >= 1:
                    residual(b - 1)
                if b + 1 < B:
                    variance(0, xs_[:, b + 1])
                if b >= 1:
                    residual_done(b - 1)
                if b + 1 < B:
                    normed(b + 1)
                unit(b, 1)
                if b == 0:
                    s4_gains()
                if b + 1 < B:
                    conv(b + 1)
                unit(b, 2)
                if b == 1:
                    s4_angles()
                if b + 1 < B:
                    softplus_w(b + 1)
                    bc_parts(b + 1)
                else:
                    dve.wait_ge(k16_moved, 32)
                    link(TTN(kT[0:1, 0, :], kT[0:1, 0, :], dskip[:, :], ALU.add))
                    dve.sem_inc(kT_ready, 1)
                unit(b, 3)
                if b + 1 < B:
                    softplus(b + 1)
                else:
                    dve.wait_ge(kf_ps, 1)
                    for j in range(3):
                        link(nc.vector.tensor_copy(kf[:, j, :, :], TT[:, j // 2, (j % 2) * 256:(j % 2) * 256 + 256]
                                                   .rearrange("p (q d) -> p q d", q=2)))
                    dve.sem_inc(kf_ready, 1)
                gated(b)

            def film_params():
                dve.wait_ge(ld_small, 80)
                gate = row("gate")
                for name in ("film_in", "film_out"):
                    link(TS(wt(name, 0, 2 * D), wt(name, 0, 2 * D), gate, None, ALU.mult), False)
                    rb = row(name + "_b")
                    link(TS(rb, rb, gate, None, ALU.mult))
                    link(TS(rb[:, 0:D], rb[:, 0:D], 1.0, None, ALU.add), False)
                link(nc.vector.tensor_copy(tmask[:, :, :].rearrange("p b r -> p (b r)"), tmask8[:, :]))
                dve.sem_inc(params_ready, 1)

            def flat(c_):
                return c_.rearrange("p n e -> p (n e)")

            def segment_max(g, lo, hi):
                t, k = divmod(g, NH)
                for q in range(lo, min(hi, NSEG)):
                    if q in (0, 1024 // SEG):
                        dve.wait_ge(s_ready, 2 * g + (1 if q == 0 else 2))
                    end = G if q == NSEG - 1 else (q + 1) * SEG
                    link(nc.vector.max(cand[:, g % 2, q, :], s[:, t % 2, k, q * SEG:end]), q == NSEG - 1)

            def largest(g):
                t, k = divmod(g, NH)
                tk = top[:, t % 2, k, :]
                chunk = [0]

                def next_chunk():
                    if g + 1 < TILES:
                        segment_max(g + 1, 4 * chunk[0], 4 * chunk[0] + 4)
                        chunk[0] += 1

                src = flat(cand[:, g % 2])
                link(nc.vector.max(tk[:, 0:8], src), True, next_chunk)
                for j in range(1, 4):
                    link(nc.vector.match_replace(cand2[:, :], tk[:, 8 * j - 8:8 * j], src, LOWEST), True, next_chunk)
                    if j == 2 and k == 1 and t >= 1:
                        summed(t - 1)
                    src = cand2[:, :]
                    link(nc.vector.max(tk[:, 8 * j:8 * j + 8], src), True, next_chunk)
                assert 4 * chunk[0] >= NSEG or g + 1 == TILES
                dve.sem_inc(top_found, 1)

            def summed(t):
                dve.wait_ge(etop_ready, t + 1)
                nc.vector.tensor_reduce(ssum[:, :], etop[:, :, :], AX, ALU.add).then_inc(ssum_ready, 1)

            def ties(t):
                if t:
                    dve.wait_ge(flags_ready, t)
                link(TTN(tie[:, :], top[:, t % 2, :, TOPK - 2], top[:, t % 2, :, TOPK - 1], ALU.subtract))
                TS(tie[:, :], tie[:, :], 0.0, -4.0 * G, ALU.is_equal, ALU.mult).then_inc(ties_ready, 1)

            def exact(t, k):
                sk = s[:, t % 2, k, :]
                src = sk
                for j in range(4):
                    nc.vector.max(top[:, t % 2, k, 8 * j:8 * j + 8], src)
                    dve.drain()
                    nc.vector.match_replace(scratch, top[:, t % 2, k, 8 * j:8 * j + 8], src, LOWEST)
                    dve.drain()
                    src = scratch
                TTN(scratch, scratch, sk, ALU.is_equal)
                dve.drain()
                STT(out=sk, in0=scratch, scalar=-PENALTY, in1=sk, op0=ALU.mult, op1=ALU.add)
                dve.drain()

            def checked(t):
                dve.wait_ge(flags_moved, 16 * (t + 1))
                link(nc.vector.tensor_reduce(headf[:, :], flagrow[:, :].rearrange("o (p k) -> o k p", k=NH), AX, ALU.min))
                link(TS(headf[:, :], headf[:, :], COUNTED - 0.5, None, ALU.is_lt))
                link(nc.vector.tensor_copy(headi[:, :], headf[:, :]), False)
                link(nc.vector.tensor_reduce(anyf[:, :], headf[:, :], AX, ALU.add))
                link(nc.vector.tensor_copy(anyi[:, :], anyf[:, :]))
                found = dve.value_load(anyi[0:1, 0:1], min_val=0, max_val=NH)
                with dve.If(found > 0):
                    for k in range(NH):
                        in_head = dve.value_load(headi[0:1, k:k + 1], min_val=0, max_val=1)
                        with dve.If(in_head > 0):
                            exact(t, k)
                if t >= 1:
                    dve.wait_ge(ssum_ready, t)
                    dve.wait_ge(ebias_ready, t)
                link(TS(ngmax[:, :], top[:, t % 2, :, 0], 4.0, -0.25, ALU.mult, ALU.mult))
                link(TTN(etop[:, :, :], top[:, t % 2], ngmax[:, :].unsqueeze(2).to_broadcast([P, NH, TOPK]), ALU.add))
                dve.sem_inc(top_ready, 1)

            def masked(t, k):
                dve.wait_ge(prob_ready, NH * t + k + 1)
                sk = s[:, t % 2, k, :]
                STT(out=sk, in0=sk, scalar=top[:, t % 2, k, TOPK - 1:TOPK], in1=prob[:, k % 2, :],
                    op0=ALU.is_ge, op1=ALU.mult).then_inc(masked_ready, 1)

            def rowb(name):
                return row(name).unsqueeze(1).to_broadcast([P, R, D])

            def film(b):
                src = big if b == B - 1 else shared
                return [src[:, i * 512:(i + 1) * 512].rearrange("p (r d) -> p r d", r=R) for i in range(2)]

            def tail(b, i):
                x1 = xs_[:, b]
                if i == -1:
                    layernorm(2, n2, x1)
                    link(TTN(n2[:, :, :], n2[:, :, :], rowb("in_g"), ALU.mult))
                    link(TTN(n2[:, :, :], n2[:, :, :], rowb("in_b"), ALU.add), False)
                if i == 0:
                    dve.wait_ge(film_ps, b + 1)
                    fi, fo = film(b)
                    for dst, j, name in ((fi, 0, "film_in_b"), (fo, 1, "film_out_b")):
                        for r in range(R):
                            link(STT(out=dst[:, r, :], in0=TT[:, j, r * T:(r + 1) * T], scalar=tmask[:, b, r:r + 1],
                                     in1=row(name), op0=ALU.mult, op1=ALU.add), r == 1 and j == 1)
                    link(TTN(n2[:, :, :], n2[:, :, :], fi[:, :, 0:D], ALU.mult))
                    link(TTN(n2[:, :, :], n2[:, :, :], fi[:, :, D:2 * D], ALU.add))
                    dve.sem_inc(xs_ready, 1)
                if i == 1:
                    dve.wait_ge(xf_ps, b + 1)
                    xre = TT[:, 0, 0:2 * D].rearrange("p (q d) -> p q d", q=2)
                    xim = TT[:, 0, 2 * D:4 * D].rearrange("p (q d) -> p q d", q=2)
                    for lo, ka, kb, op in ((0, 0, 1, ALU.subtract), (2, 1, 2, ALU.add)):
                        link(TTN(xf_a, xre, kf[:, ka, :, :], ALU.mult), False)
                        link(TTN(xf_b, xim, kf[:, kb, :, :], ALU.mult))
                        link(TTN(Y[:, lo:lo + 2, :], xf_a, xf_b, op))
                    dve.sem_inc(Y_ready, 1)
                if i == 2:
                    dve.wait_ge(y_ps, b + 1)
                    fo = film(b)[1]
                    link(TTN(xt[:, :, :], TT[:, 1, 0:T].rearrange("p (r d) -> p r d", r=R), fo[:, :, 0:D], ALU.mult))
                    link(TTN(xt[:, :, :], xt[:, :, :], fo[:, :, D:2 * D], ALU.add))
                    link(TTN(xt[:, :, :], xt[:, :, :], x1, ALU.add))
                    layernorm(3, n2, xt)
                    dve.sem_inc(n3_ready, 1)
                    link(TTN(xt[:, :, :], xt[:, :, :], rowb("ffn_b2"), ALU.add))
                if i == 3:
                    dve.wait_ge(h2_ps, b + 1)
                    link(TTN(xt[:, :, :], TT[:, 1, 0:T].rearrange("p (r d) -> p r d", r=R), xt[:, :, :], ALU.add))
                    layernorm(4, n2, xt)
                    link(TTN(n2[:, :, :], n2[:, :, :], rowb("out_g"), ALU.mult))
                    link(TTN(n2[:, :, :], n2[:, :, :], rowb("out_b"), ALU.add))
                    link(TTN(n2[:, :, :], n2[:, :, :], x1, ALU.add))
                    layernorm(5, x2, n2)
                    dve.sem_inc(x2_ready, 1)
                if i == 4:
                    dve.wait_ge(lg_ps, b + 1)
                    link(TTN(lg[:, :, :], M[:, 1, 0:R * NE].rearrange("p (r e) -> p r e", r=R),
                             row("router_b").unsqueeze(1).to_broadcast([P, R, NE]), ALU.add))
                    for r in range(R):
                        link(nc.vector.max(lmax[:, r, :], lg[:, r, :]), r == R - 1)
                    for r in range(R):
                        link(nc.vector.max_index(lidx[:, r, :], lmax[:, r, :], lg[:, r, :]), r == R - 1)
                    link(nc.vector.tensor_copy(lidf[:, :, :], lidx[:, :, 0:2]), False)
                    link(TTN(wtop[:, :, 0], lmax[:, :, 1], lmax[:, :, 0], ALU.subtract))
                    dve.sem_inc(wexp_in, 1)
                if i == 5:
                    dve.wait_ge(wexp_out, b + 1)
                    link(TS(wtop[:, :, 2], wtop[:, :, 1], 1.0, None, ALU.add))
                    link(nc.vector.reciprocal(wtop[:, :, 2], wtop[:, :, 2]))
                    link(TTN(wtop[:, :, 3], wtop[:, :, 1], wtop[:, :, 2], ALU.mult))
                    for r in range(R):
                        link(TS(oh[:, r, 0, :], iota8[:, :], lidf[:, r, 0:1], wtop[:, r, 2:3], ALU.is_equal, ALU.mult), False)
                        link(TS(oh[:, r, 1, :], iota8[:, :], lidf[:, r, 1:2], wtop[:, r, 3:4], ALU.is_equal, ALU.mult), r == 1)
                    link(TTN(wd[:, :, :], oh[:, :, 0, :], oh[:, :, 1, :], ALU.add))
                    dve.sem_inc(wd_ready, 1)
                if i == 7:
                    dve.wait_ge(mb_ps, b + 1)
                    link(TTN(acc[:, :, :], M[:, 1, 0:T].rearrange("p (r d) -> p r d", r=R), acc[:, :, :], ALU.add))
                if i in OUTPUTS:
                    experts_added(b, OUTPUTS[i])
                if i == LAST:
                    if b >= 1:
                        dve.wait_ge(out_stored, 16 * b)
                    layernorm(6, outt, acc)
                    dve.sem_inc(out_ready, 1)

            def experts_added(b, pair):
                dve.wait_ge(eo_ps, NE * b + pair[-1] + 1)
                for e in pair:
                    for r in range(R):
                        link(STT(out=acc[:, r, :], in0=M[:, 0, (R * (e % 2) + r) * D:(R * (e % 2) + r + 1) * D],
                                 scalar=wd[:, r, e:e + 1], in1=x2[:, r, :] if e == 0 else acc[:, r, :],
                                 op0=ALU.mult, op1=ALU.add), r == 1)
                    dve.sem_inc(eo_used, 1)

            segment_max(0, 0, NSEG)
            for g in range(END):
                t, k = divmod(g, NH)
                if g < TILES:
                    largest(g)
                    if k == NH - 1:
                        ties(t)
                    if g == 0:
                        residual(B - 1)
                        film_params()
                        residual_done(B - 1)
                if 1 <= t <= B * R:
                    if k == 0:
                        checked(t - 1)
                    if k == 1:
                        if g >= TILES:
                            summed(t - 1)
                        masked(t - 1, 0)
                        masked(t - 1, 1)
                    if k == 2:
                        masked(t - 1, 2)
                        masked(t - 1, 3)
                for b, i in tails_at(g):
                    tail(b, i)


def dft_tables():
    t = np.arange(T)[:, None].astype(np.float64)
    k = np.arange(T)[None, :].astype(np.float64)
    ang = 2 * np.pi * t * k / NFFT
    re, im = np.cos(ang), -np.sin(ang)
    last = np.where(np.arange(T) % 2 == 0, 1.0, -1.0)
    im_last, re_last = im.copy(), re.copy()
    im_last[:, 0] = last
    re_last[:, 0] = last
    fwd = np.stack([re[:, :P], re[:, P:], im_last[:, :P], im[:, P:], im[:, :P], re_last[:, :P]], 1)
    fwd = fwd.reshape(R, P, 6, P).transpose(1, 0, 2, 3)
    w = np.full(T, 2.0)
    w[0] = 1.0
    ire, iim = (re * w).T / NFFT, (im * w).T / NFFT
    iim[0, :] = last / NFFT
    inv = np.concatenate([ire, iim], 0).reshape(4, P, T).transpose(1, 0, 2)
    return np.ascontiguousarray(fwd, np.float32), np.ascontiguousarray(inv, np.float32)


def layout(i):
    tiles = lambda v, n: v.reshape(n, P, -1).transpose(1, 0, 2).reshape(P, -1)
    cols = {"ln_g": i["L0_attn_ln_gamma"][:, None], "ln_b": i["L0_attn_ln_beta"][:, None],
            "conv_w": tiles(i["L0_attn_conv_w"], CH), "conv_b": tiles(i["L0_attn_conv_b"], CH),
            "w_dt": tiles(i["L0_attn_w_dt"], CH), "b_dt": tiles(i["L0_attn_b_dt"], CH),
            "d_param": tiles(i["L0_attn_D_param"], CH), "a_log": tiles(i["L0_attn_A_log"], CH),
            "ffn_g": i["L0_xattn_g_ffn"][:, None], "ffn_b": i["L0_xattn_b_ffn"][:, None],
            "ffn_b1": tiles(i["L0_xattn_b1"], FT), "moe_b1": tiles(i["L0_ffn_b1"].reshape(-1), NE * FT)}
    rows = {"in_g": i["L0_xattn_g_norm_in"], "in_b": i["L0_xattn_b_norm_in"], "out_g": i["L0_xattn_g_norm_out"],
            "out_b": i["L0_xattn_b_norm_out"], "ffn_b2": i["L0_xattn_b2"], "film_in_b": i["L0_xattn_b_film_in"],
            "film_out_b": i["L0_xattn_b_film_out"], "router_b": i["L0_ffn_router_b"],
            "gate": i["L0_xattn_mod_gate"].reshape(1), "log_dt": i["L0_xattn_log_dt"]}
    wx = i["L0_attn_W_x"]
    wts = {"w_in": i["L0_attn_W_in"].T, "wx_bc": tiles(np.concatenate([wx[1:]] * 3, 0).T, CH),
           "wx_raw": tiles(np.repeat(wx[0:1], P, 0).T, CH), "w_out": tiles(i["L0_attn_W_out"].T, CH),
           "wq": i["L0_xattn_Wq"], "film_in": i["L0_xattn_W_film_in"], "film_out": i["L0_xattn_W_film_out"],
           "w1": i["L0_xattn_W1"], "w2": tiles(i["L0_xattn_W2"], FT), "router": i["L0_ffn_router_w"].T}
    fwd, inv = dft_tables()
    sel = (np.arange(96)[:, None] % 32 == np.arange(32)[None, :]).astype(np.float32)
    twice = lambda v: np.concatenate([v.T, v.T], 0)
    c_re, c_im = i["L0_xattn_C_re"].T, i["L0_xattn_C_im"].T
    return {
        "x": i["x"], "ctxT": i["ctx_768"].transpose(0, 2, 1), "gmask": i["mask_BxS2_bf1"],
        "tmask": i["mask_BxS_bf1"].reshape(B * R, P).T,
        "cols": np.concatenate([cols[n] for n in COLS], 1), "rows": np.concatenate([rows[n] for n in ROWS])[None, :],
        "wts": np.concatenate([wts[n] for n in WTS], 1),
        "wkv": np.concatenate([i["L0_xattn_Wk"], i["L0_xattn_Wv"]], 1), "ident": np.eye(P, dtype=np.float32),
        "sel": sel, "dft": fwd, "idft": inv, "iota8": np.arange(NE, dtype=np.float32)[None, :],
        "moe_w1": i["L0_ffn_w1"].transpose(2, 0, 1).reshape(P, NE, FT, P),
        "moe_w2": i["L0_ffn_w2"].reshape(NE, D, FT, P).transpose(3, 0, 2, 1), "moe_b2": i["L0_ffn_b2"],
        "a_re": twice(i["L0_xattn_A_re"]), "a_im": twice(i["L0_xattn_A_im"]),
        "c_1": np.concatenate([c_re, c_im], 0), "c_2": np.concatenate([c_im, c_re], 0),
        "dskip": i["L0_xattn_D_skip"][None, :],
        "steps": np.concatenate([np.arange(L16), L16 * np.arange(L16)]).astype(np.float32)[None, :],
    }


def kernel(**inputs):
    import concourse.bacc as bacc
    from concourse.bass_utils import run_bass_kernel_spmd

    nc = bacc.Bacc("TRN2", target_bir_lowering=False, num_devices=1)
    arrays, args = {}, {}
    for name, v in layout({k: np.asarray(x) for k, x in inputs.items()}).items():
        v = np.ascontiguousarray(v)
        if v.dtype == np.bool_:
            v = v.view(np.uint8)
        arrays[f"in_{name}"] = v
        args[name] = nc.dram_tensor(f"in_{name}", v.shape, mybir.dt.from_np(v.dtype), kind="ExternalInput").ap()
    args["out"] = nc.dram_tensor("out_x", (B, T, D), F32, kind="ExternalOutput").ap()
    build(nc, args)
    r = run_bass_kernel_spmd(nc, [arrays], core_ids=[0])
    return r.results[0]["out_x"]
```

```python
from contextlib import ExitStack

import numpy as np

import concourse.bass as bass
from concourse import mybir

ALU = mybir.AluOpType
ACT = mybir.ActivationFunctionType
F32 = mybir.dt.float32
BF16 = mybir.dt.bfloat16
I32 = mybir.dt.int32
U32 = mybir.dt.uint32
U8 = mybir.dt.uint8
AX = mybir.AxisListType.X

P = 128
B, T, D = 4, 256, 128
R = T // P
CH = 2
NS = 16
NU = 4
UN = NS // NU
KC = 4
G, DV = 1601, 96
GC = (G + P - 1) // P
GL = G - (GC - 1) * P
NH, DH = 4, 32
SEG = 57
NSEG = G // SEG
TOPK = 32
FT = 4
NE = 8
L16 = 16
NFFT = 2 * T
EPS = 1e-5
SCALE = float(np.float32(1.0) / np.sqrt(np.float32(DH)))
PENALTY = 1.0e38
COUNTED = G - 2 * (TOPK - 1) - 1
LOWEST = -3.4e38


def log1p_coefficients():
    n = 64
    u = (np.cos(np.pi * (np.arange(n) + 0.5) / n) + 1) / 2
    return [float(v) for v in np.polynomial.polynomial.polyfit(u, np.log1p(u) / u, 8)]


def column_layout():
    at, n = {}, 0
    for name, width in (("ln_g", 1), ("ln_b", 1), ("conv_b", CH), ("w_dt", CH), ("b_dt", CH),
                        ("d_param", CH), ("a_log", CH * NS), ("ffn_g", 1), ("ffn_b", 1), ("ffn_b1", FT),
                        ("moe_b1", NE * FT)):
        at[name] = (n, n + width)
        n += width
    return at, n


def row_layout():
    at, n = {}, 0
    for name, width in (("in_g", D), ("in_b", D), ("out_g", D), ("out_b", D), ("ffn_b2", D), ("film_in_b", 2 * D),
                        ("film_out_b", 2 * D), ("router_b", NE), ("gate", 1), ("log_dt", D)):
        at[name] = (n, n + width)
        n += width
    return at, n


def weight_layout():
    at, n = {}, 0
    for name, width in (("w_in", 4 * P), ("wx_bc", CH * 96), ("wx_raw", CH * P), ("w_out", CH * D), ("wq", D),
                        ("film_in", 2 * D), ("film_out", 2 * D), ("w1", FT * P), ("w2", FT * D), ("router", NE)):
        at[name] = (n, n + width)
        n += width
    return at, n


COLS, NCOLS = column_layout()
ROWS, NROWS = row_layout()
WTS, NWTS = weight_layout()
LD = L16 * D
TILES = B * R * NH
LNS = 7


def build(nc, a):
    ctx = ExitStack()
    with ctx:
        def sb(name, shape, dt=F32):
            return ctx.enter_context(nc.sbuf_tensor(name, shape, dt))

        def sem(name):
            return ctx.enter_context(nc.semaphore(name))

        cols = sb("cols", [P, NCOLS])
        rows = sb("rows", [P, NROWS])
        wts = sb("wts", [P, NWTS])
        wv = sb("wv", [DV, D])
        ident = sb("ident", [P, P])
        sel_c = sb("sel_c", [96, 32])
        sel = sb("sel", [96, 32], BF16)
        dft = sb("dft", [P, R, 6, P])
        idft = sb("idft", [P, 4, T])
        moe_w = sb("moe_w", [P, 2 * NE * FT * P])
        moe_w1, moe_w2 = (moe_w[:, i * NE * FT * P:(i + 1) * NE * FT * P].rearrange("p (e f m) -> p e f m", e=NE, f=FT)
                          for i in range(2))
        moe_b2 = sb("moe_b2", [NE, D])
        tmask8 = sb("tmask8", [P, B * R], U8)
        tmask = sb("tmask", [P, B, R])
        half = sb("half", [P, R])
        iota8 = sb("iota8", [P, NE])
        a_neg = sb("a_neg", [P, CH * NS])
        kf = sb("kf", [P, 3, 2, D])

        xs_ = sb("xs_", [P, B, R, D])
        stat = sb("stat", [P, LNS, R, 6])
        mv = sb("mv", [P, LNS, R, 2])
        rstd = sb("rstd", [P, LNS, R])
        shared = sb("shared", [P, 2 * FT * T])
        sp_a, sp_p, sp_q = (shared[:, i * CH * T:(i + 1) * CH * T].rearrange("p (c t) -> p c t", c=CH) for i in range(3))
        gT = shared[:, 1024:1024 + FT * T].rearrange("p (f t) -> p f t", f=FT)
        gm = shared[:, :].rearrange("p (e f t) -> p e f t", e=2, f=FT)
        mixed = sb("mixed", [P, 1024])
        yv = mixed[:, 0:512].rearrange("p (c t) -> p c t", c=CH)
        xn = mixed[:, 512:768].rearrange("p (r d) -> p r d", r=R)
        xnT = mixed[:, 768:1024]
        xf_a = mixed[:, 0:256].rearrange("p (q d) -> p q d", q=2)
        xf_b = mixed[:, 256:512].rearrange("p (q d) -> p q d", q=2)
        Y = mixed[:, 512:1024].rearrange("p (q d) -> p q d", q=4)
        big = sb("big", [P, 2 * NH * G])
        at = [0]

        def take(n):
            at[0] += n
            assert at[0] <= 2 * NH * G
            return big[:, at[0] - n:at[0]]

        abar, hst = (take(2 * CH * UN * T).rearrange("p (u c n t) -> p u c n t", u=2, c=CH, n=UN) for i in range(2))
        xc, sz, dt_, ux = (take(2 * CH * T).rearrange("p (u c t) -> p u c t", u=2, c=CH) for i in range(4))
        early = sb("early", [P, (G + 1) // 2])
        parts = early[0:96, 0:T].bitcast(BF16).rearrange("p (u t) -> p u t", u=2)
        bc_r = early[0:96, T:2 * T]
        bc_m = early[0:96, 2 * T:2 * T + T // 2].bitcast(BF16)
        junk = early[:, :].bitcast(BF16)[:, 0:G]

        ctxT = sb("ctxT", [DV + 1, 2, G])
        gmask8 = sb("gmask8", [P, G], U8)
        V = sb("V", [P, GC, D])
        x1T = sb("x1T", [P, T])
        QT = sb("QT", [DV + 1, NH, T])
        wqk = wts[:, 0:NH * DV].rearrange("p (h e) -> p h e", h=NH)
        wconv = V[:, 0:KC * CH, :].rearrange("p (j c) m -> p j c m", j=KC)
        s = big[:, :].rearrange("p (u k g) -> p u k g", u=2, k=NH)
        att = sb("att", [P, 3 * LD])
        prob = att[:, 0:2 * G].rearrange("p (u g) -> p u g", u=2)
        aT = att[:, 2 * G:2 * G + GC * P].rearrange("p (g t) -> p g t", g=GC)
        scratch = prob[:, 0, :]
        avg = sb("avg", [P, G])
        wkb = avg[:, 0:NH * DV]
        cand = sb("cand", [P, 2, NSEG, 8])
        cand2 = sb("cand2", [P, NSEG * 8])
        top = sb("top", [P, 2, NH, TOPK])
        etop = sb("etop", [P, NH, TOPK])
        ngmax = sb("ngmax", [P, NH])
        ssum = sb("ssum", [P, NH])
        lnsum = sb("lnsum", [P, NH])
        ebias = sb("ebias", [P, NH])
        counts = sb("counts", [P, NH])
        tie = sb("tie", [P, NH])
        flag = sb("flag", [P, NH])
        flagrow = sb("flagrow", [1, P * NH])
        headf = sb("headf", [1, NH])
        anyf = sb("anyf", [1, 1])
        anyi = sb("anyi", [1, 1], I32)
        headi = sb("headi", [1, NH], I32)
        cT = sb("cT", [P, T])

        n2 = sb("n2", [P, R, D])
        xt = sb("xt", [P, R, D])
        hT = sb("hT", [P, T])
        x2 = sb("x2", [P, R, D])
        x2T = sb("x2T", [P, T])
        lg = sb("lg", [P, R, NE])
        lmax = sb("lmax", [P, R, 8])
        lidx = sb("lidx", [P, R, 8], U32)
        lidf = sb("lidf", [P, R, 2])
        wtop = sb("wtop", [P, R, 4])
        oh = sb("oh", [P, R, 2, NE])
        wd = sb("wd", [P, R, NE])
        wdT = sb("wdT", [NE, T])
        acc = sb("acc", [P, R, D])
        outt = sb("outt", [P, R, D])

        u_ph, u_ph2, u_exp, w_rnd = (moe_w[:, i * LD:(i + 1) * LD].rearrange("p (l d) -> p l d", l=L16) for i in range(4))
        w_ph, w_exp = (att[:, i * LD:(i + 1) * LD].rearrange("p (l d) -> p l d", l=L16) for i in range(2))
        a_re, a_im, c_1, c_2, *sv = [att[:, 2 * LD + i * D:2 * LD + (i + 1) * D] for i in range(16)]
        k16 = att[0:L16, 2 * LD:3 * LD].rearrange("p (l d) -> p l d", l=L16)
        kT = x1T[:, :].rearrange("p (r d) -> p r d", r=R)
        dskip = sb("dskip", [1, D])
        steps = sb("steps", [P, 2, L16])
        ki = sb("ki", [P, D], I32)
        phase = sb("phase", [P, 2])

        S = ctx.enter_context(nc.psum_tensor("S", [P, 4 * 512], F32))
        M = ctx.enter_context(nc.psum_tensor("M", [P, 2, 512], F32))
        TT = ctx.enter_context(nc.psum_tensor("TT", [P, 2, 512], F32))

        def col(name, i=0):
            return cols[:, COLS[name][0] + i:COLS[name][0] + i + 1]

        def row(name):
            return rows[:, ROWS[name][0]:ROWS[name][1]]

        def wt(name, i, n):
            return wts[:, WTS[name][0] + i * n:WTS[name][0] + (i + 1) * n]

        ld_x = sem("ld_x"); ld_ctx = sem("ld_ctx"); ld_cols = sem("ld_cols"); ld_rows = sem("ld_rows")
        ld_w = sem("ld_w"); ld_ident = sem("ld_ident"); ld_small = sem("ld_small"); ld_s4 = sem("ld_s4")
        ld_dft = sem("ld_dft"); ld_moe = sem("ld_moe"); k16_moved = sem("k16_moved"); out_stored = sem("out_stored")
        pool_step = sem("pool_step"); dve_step = sem("dve_step"); act_step = sem("act_step")
        consts_set = sem("consts_set"); a_exp = sem("a_exp"); params_ready = sem("params_ready")
        s4_small = sem("s4_small"); s4_sin_in = sem("s4_sin_in"); s4_sin = sem("s4_sin"); s4_th_in = sem("s4_th_in")
        s4_gain = sem("s4_gain"); s4_arg = sem("s4_arg"); s4_fun = sem("s4_fun"); s4_mats = sem("s4_mats")
        k16_ps = sem("k16_ps"); k16_sb = sem("k16_sb"); kT_ready = sem("kT_ready"); kf_ps = sem("kf_ps")
        kf_ready = sem("kf_ready")
        var_ready = sem("var_ready"); rstd_ready = sem("rstd_ready")
        xn_ready = sem("xn_ready"); xnT_ps = sem("xnT_ps"); xnT_ready = sem("xnT_ready"); xz_ps = sem("xz_ps")
        wconv_ready = sem("wconv_ready"); ld_conv = sem("ld_conv"); xc_ready = sem("xc_ready")
        sz_ready = sem("sz_ready"); ssm_ps = sem("ssm_ps"); bc_hi = sem("bc_hi"); sp_ready = sem("sp_ready")
        parts_ready = sem("parts_ready"); dt_ready = sem("dt_ready"); abar_ready = sem("abar_ready")
        bc_ps = sem("bc_ps"); b_used = sem("b_used"); c_used = sem("c_used"); scan_done = sem("scan_done")
        hc_ready = sem("hc_ready"); y_sum = sem("y_sum"); yv_ready = sem("yv_ready"); op_ps = sem("op_ps")
        x1_ready = sem("x1_ready"); res_ready = sem("res_ready"); added = sem("added")
        pen_ready = sem("pen_ready"); wqk_ps = sem("wqk_ps"); wqk_ready = sem("wqk_ready"); v_ps = sem("v_ps")
        v_ready = sem("v_ready"); x1T_ps = sem("x1T_ps"); x1T_ready = sem("x1T_ready"); q_ps = sem("q_ps")
        q_ready = sem("q_ready"); s_ps = sem("s_ps"); s_ready = sem("s_ready"); flags_ready = sem("flags_ready")
        top_found = sem("top_found"); counted = sem("counted"); ties_ready = sem("ties_ready")
        flags_moved = sem("flags_moved"); top_ready = sem("top_ready"); etop_ready = sem("etop_ready")
        ssum_ready = sem("ssum_ready"); lnsum_ready = sem("lnsum_ready"); ebias_ready = sem("ebias_ready")
        prob_ready = sem("prob_ready"); masked_ready = sem("masked_ready"); aT_ps = sem("aT_ps")
        aT_ready = sem("aT_ready"); c_ps = sem("c_ps"); c_ready = sem("c_ready")
        film_ps = sem("film_ps"); xs_ready = sem("xs_ready"); xf_ps = sem("xf_ps"); Y_ready = sem("Y_ready")
        y_ps = sem("y_ps"); n3_ready = sem("n3_ready"); n3T_ps = sem("n3T_ps"); hT_ready = sem("hT_ready")
        h1_ps = sem("h1_ps"); gT_ready = sem("gT_ready"); h2_ps = sem("h2_ps"); x2_ready = sem("x2_ready")
        x2T_ps = sem("x2T_ps"); x2T_ready = sem("x2T_ready"); lg_ps = sem("lg_ps"); wd_ready = sem("wd_ready")
        wdT_ps = sem("wdT_ps"); wdT_ready = sem("wdT_ready"); mb_ps = sem("mb_ps"); eh_ps = sem("eh_ps")
        eg_ready = sem("eg_ready"); eo_ps = sem("eo_ps"); wexp_in = sem("wexp_in"); wexp_out = sem("wexp_out")
        eo_used = sem("eo_used"); out_ready = sem("out_ready")

        block = ctx.enter_context(nc.Block())
        C1 = log1p_coefficients()
        MAGIC = 1.5 * 2.0 ** 23
        TWO_PI = float(2 * np.pi)

        def tails_at(g):
            steps_ = [(b, g - NH * R * (b + 1) - NH + (b == B - 1)) for b in range(B)]
            if g >= TILES + NH:
                steps_ = steps_[::-1]
            return [(b, i) for b, i in steps_ if FIRST <= i <= LAST]

        def mean_at(g):
            t, k = divmod(g, NH)
            return t - 2 if k == 0 and 2 <= t <= B * R else None

        def values_at(g):
            return g == 1 or NH * R < g < TILES and g % (NH * R) == NH

        AHEAD = 2
        FIRST, LAST = -1, 8
        HIDDEN = {4: (0, 1), 5: (2,), 6: (3, 4), 7: (5, 6, 7)}
        OUTPUTS = {5: (0, 1), 6: (2, 3), 7: (4, 5), 8: (6, 7)}

        def queries_at(g):
            return g + AHEAD + 1 < TILES and (g + AHEAD + 1) % (NH * R) == 0

        END = NH * R * B + NH + LAST

        @block.sync
        def _(sp):
            sp.dma_start(cols[:, :], a["cols"]).then_inc(ld_cols, 16)
            sp.dma_start(xs_[:, :, :, :].rearrange("p b r d -> p (b r) d"),
                         a["x"].rearrange("b (r p) d -> p (b r) d", p=P)).then_inc(ld_x, 16)
            sp.dma_start(ident[:, :], a["ident"]).then_inc(ld_ident, 16)
            sp.dma_start(sel_c[:, :], a["sel"]).then_inc(ld_ident, 16)
            sp.dma_start(wts[:, :], a["wts"]).then_inc(ld_w, 16)
            sp.dma_start(wconv, a["conv"].to_broadcast([P, KC * CH * P])
                         .rearrange("p (j c m) -> p j c m", j=KC, c=CH)).then_inc(ld_conv, 16)
            sp.dma_start(rows[:, :], a["rows"].to_broadcast([P, NROWS])).then_inc(ld_rows, 16)
            for dst, name in ((a_re, "a_re"), (a_im, "a_im"), (c_1, "c_1"), (c_2, "c_2"), (dskip, "dskip")):
                sp.dma_start(dst[:, :], a[name]).then_inc(ld_s4, 16)
            sp.dma_start(steps[:, :, :].rearrange("p a b -> p (a b)"), a["steps"].to_broadcast([P, 2 * L16])).then_inc(ld_s4, 16)
            sp.dma_start(wv[:, :], a["wv"]).then_inc(ld_small, 16)
            sp.dma_start(wkb, a["wkb"]).then_inc(ld_small, 16)
            sp.dma_start(tmask8[:, :], a["tmask"]).then_inc(ld_small, 16)
            sp.dma_start(iota8[:, :], a["iota8"].to_broadcast([P, NE])).then_inc(ld_small, 16)
            sp.dma_start(ctxT[0:DV, 0, :], a["ctxT"][0]).then_inc(ld_ctx, 16)
            sp.dma_start(gmask8[DV:DV + 1, :], a["gmask"][0:1, :]).then_inc(ld_ctx, 16)
            sp.dma_start(dft[:, :, :, :], a["dft"]).then_inc(ld_dft, 16)
            sp.dma_start(idft[:, :, :], a["idft"]).then_inc(ld_dft, 16)
            sp.wait_ge(k16_sb, 2)
            for r in range(R):
                sp.dma_start(kT[:, r, :], k16[r * 8:(r + 1) * 8, :, :]).then_inc(k16_moved, 16)
            sp.dma_start(moe_w1[:, :, :, :], a["moe_w1"]).then_inc(ld_moe, 16)
            sp.dma_start(moe_w2[:, :, :, :], a["moe_w2"]).then_inc(ld_moe, 16)
            sp.dma_start(moe_b2[:, :], a["moe_b2"]).then_inc(ld_moe, 16)
            for g in range(END):
                t, k = divmod(g, NH)
                if k == 0 and 1 <= t <= B * R:
                    sp.wait_ge(flags_ready, t)
                    sp.dma_start(flagrow[:, :].rearrange("o (p k) -> o p k", k=NH), flag[:, :]).then_inc(flags_moved, 16)
                b = g // (NH * R)
                if values_at(g) and b + 1 < B:
                    if b >= 1:
                        sp.wait_ge(s_ps, 4 * R * NH * b)
                        sp.wait_ge(v_ps, 4 * b)
                    sp.wait_ge(pen_ready, b + 1)
                    sp.dma_start(ctxT[0:DV, (b + 1) % 2, :], a["ctxT"][b + 1]).then_inc(ld_ctx, 16)
                    sp.dma_start(gmask8[DV:DV + 1, :], a["gmask"][b + 1:b + 2, :]).then_inc(ld_ctx, 16)
                for b, i in tails_at(g):
                    if i == LAST:
                        sp.wait_ge(out_ready, b + 1)
                        sp.dma_start(a["out"][b].rearrange("(r p) d -> p r d", p=P), outt[:, :, :]).then_inc(out_stored, 16)
            sp.wait_ge(out_stored, 16 * B)

        @block.gpsimd
        def _(pool):
            n = [0]
            nln = [0]

            def link(ins):
                n[0] += 1
                ins.then_inc(pool_step, 1)
                pool.wait_ge(pool_step, n[0])

            def layernorm(k):
                nln[0] += 1
                pool.wait_ge(var_ready, nln[0])
                link(pool.tensor_scalar(rstd[:, k, :], mv[:, k, :, 1], EPS, None, ALU.add))
                pool.tensor_tensor(rstd[:, k, :], rstd[:, k, :], half[:, :], ALU.pow).then_inc(rstd_ready, 1)

            def less_whole(ph):
                link(pool.tensor_scalar(w_rnd, ph, MAGIC, MAGIC, ALU.add, ALU.subtract))
                link(pool.tensor_tensor(ph, ph, w_rnd, ALU.subtract))

            link(pool.memset(half[:, :], -0.5))
            layernorm(0)
            link(pool.memset(phase[0:64, 0:1], 0.25))
            link(pool.memset(phase[64:128, 0:1], 0.5))
            link(pool.tensor_copy(phase[:, 1:2], phase[:, 0:1]))
            link(pool.memset(abar[:, :, :, :, 0:1].rearrange("p u c n t -> p (u c n) t"), 0.0))
            pool.sem_inc(consts_set, 1)
            pool.wait_ge(s4_small, 1)
            turn, are = sv[0], sv[1]
            bc = lambda v: v.unsqueeze(1).to_broadcast([P, L16, D])
            st = lambda i: steps[:, i, :].unsqueeze(2).to_broadcast([P, L16, D])
            link(pool.tensor_tensor(w_exp, bc(are), st(0), ALU.mult))
            link(pool.tensor_tensor(w_ph, bc(turn), st(0), ALU.mult))
            pool.sem_inc(s4_arg, 1)
            layernorm(0)
            link(pool.tensor_tensor(u_exp, bc(are), st(1), ALU.mult))
            link(pool.tensor_tensor(u_ph, bc(turn), st(1), ALU.mult))
            pool.sem_inc(s4_arg, 1)
            link(pool.tensor_scalar(u_ph2, u_ph, 0.5, None, ALU.add))
            link(pool.tensor_scalar(u_ph, u_ph, 0.25, None, ALU.add))
            less_whole(u_ph)
            link(pool.tensor_scalar(w_ph, w_ph, phase[:, 0:1], None, ALU.add))
            layernorm(1)
            layernorm(0)
            less_whole(u_ph2)
            less_whole(w_ph)
            pool.sem_inc(s4_th_in, 2)
            pool.wait_ge(s4_fun, 5)
            pool.wait_ge(s4_gain, 1)
            link(pool.tensor_tensor(w_ph, w_exp, w_ph, ALU.mult))
            layernorm(1)
            layernorm(0)
            link(pool.tensor_tensor(u_ph, u_ph, bc(sv[10]), ALU.mult))
            link(pool.tensor_tensor(u_ph2, u_ph2, bc(sv[11]), ALU.mult))
            link(pool.tensor_tensor(u_ph, u_ph, u_ph2, ALU.add))
            link(pool.tensor_tensor(u_ph, u_ph, u_exp, ALU.mult))
            pool.sem_inc(s4_mats, 1)
            layernorm(1)

            def penalty(b):
                pool.wait_ge(ld_ctx, 32 * (b + 1))
                if b >= 2:
                    pool.wait_ge(s_ps, 4 * R * NH * (b - 1))
                pool.wait_ge(rstd_ready, nln[0])
                if b >= 2:
                    pool.wait_ge(added, 3 * (R * b - 2))
                if b:
                    pool.wait_ge(flags_ready, R * b - 1)
                    pool.wait_ge(ebias_ready, R * b - 1)
                pool.tensor_scalar(ctxT[DV:DV + 1, b % 2, :], gmask8[DV:DV + 1, :], PENALTY, -PENALTY, ALU.mult, ALU.add).then_inc(pen_ready, 1)
                pool.wait_ge(pen_ready, b + 1)

            penalty(0)
            layernorm(1)

            for g in range(END):
                t, k = divmod(g, NH)
                if 1 <= t <= B * R and k == 0:
                    pool.wait_ge(ties_ready, t)
                    pool.wait_ge(counted, NH * t)
                    if t >= 2:
                        pool.wait_ge(flags_moved, 16 * (t - 1))
                    pool.tensor_tensor(flag[:, :], counts[:, :], tie[:, :], ALU.add).then_inc(flags_ready, 1)
                if 1 <= t <= B * R and k == 1:
                    pool.wait_ge(lnsum_ready, t)
                    pool.tensor_tensor(ebias[:, :], ngmax[:, :], lnsum[:, :], ALU.subtract).then_inc(ebias_ready, 1)
                if 1 <= t <= B * R and k == 2:
                    su = s[:, (t - 1) % 2]
                    pool.wait_ge(masked_ready, NH * (t - 1) + 2)
                    if t >= 2:
                        pool.wait_ge(aT_ps, 4 * (t - 1))
                    pool.tensor_tensor(avg[:, :], su[:, 0, :], su[:, 1, :], ALU.add).then_inc(added, 1)
                if 1 <= t < B * R and k == 3:
                    pool.wait_ge(masked_ready, NH * t)
                    pool.tensor_tensor(su[:, 2, :], su[:, 2, :], su[:, 3, :], ALU.add).then_inc(added, 1)
                    pool.wait_ge(added, 3 * (t - 1) + 2)
                    pool.tensor_tensor(avg[:, :], avg[:, :], su[:, 2, :], ALU.add).then_inc(added, 1)
                if k == 1 and t % R == 1 and t // R + 1 < B:
                    penalty(t // R + 1)
                for b, i in tails_at(g):
                    for q in {-1: (2,), 2: (3,), 3: (4, 5), 8: (6,)}.get(i, ()):
                        layernorm(q)

        @block.scalar
        def _(act):
            A = nc.scalar.activation
            n = [0]

            def link(ins):
                n[0] += 1
                ins.then_inc(act_step, 1)
                act.wait_ge(act_step, n[0])

            def normed(b):
                act.wait_ge(xnT_ps, b + 1)
                A(xnT, TT[:, 0, 0:T], ACT.Identity, scale=col("ln_g"), bias=col("ln_b")).then_inc(xnT_ready, 1)

            def silus(b):
                act.wait_ge(xz_ps, 2 * b + 1)
                for c in range(CH):
                    ins = A(xc[:, b % 2, c, :], TT[:, 0, c * T:(c + 1) * T], ACT.Silu, bias=col("conv_b", c))
                ins.then_inc(xc_ready, 1)
                act.wait_ge(xz_ps, 2 * b + 2)
                A(sz[:, b % 2], TT[:, 1, :].rearrange("p (c t) -> p c t", c=CH), ACT.Silu).then_inc(sz_ready, 1)

            def softplus(b):
                act.wait_ge(ssm_ps, 2 * b + 1)
                for c in range(CH):
                    A(sp_a[:, c, :], TT[:, 0, T:2 * T], ACT.Abs, scale=col("w_dt", c), bias=col("b_dt", c))
                    link(A(sp_p[:, c, :], TT[:, 0, T:2 * T], ACT.Relu, scale=col("w_dt", c), bias=col("b_dt", c)))
                A(sp_a, sp_a, ACT.Exp, scale=-1.0).then_inc(sp_ready, 1)
                act.wait_ge(ssm_ps, 2 * b + 2)
                A(parts[:, b % 2, :], TT[0:96, 1, 0:T], ACT.Copy).then_inc(bc_hi, 1)

            def decays(b, u):
                if u == 0:
                    act.wait_ge(dt_ready, b + 1)
                for c in range(CH):
                    if NU * b + u >= 2:
                        act.wait_ge(scan_done, CH * (NU * b + u - 2) + c + 1)
                    for j in range(UN):
                        i = UN * u + j
                        ins = A(abar[:, u % 2, c, j, 1:T], dt_[:, b % 2, c, 1:T], ACT.Exp,
                                scale=a_neg[:, c * NS + i:c * NS + i + 1])
                    ins.then_inc(abar_ready, 1)

            def kernel(h):
                act.wait_ge(k16_ps, h + 1)
                A(k16[:, :, h * D // 2:(h + 1) * D // 2], TT[0:L16, :, :].rearrange("p a (d j) -> p j (a d)", j=L16),
                  ACT.Copy).then_inc(k16_sb, 1)

            def queries(b):
                at_ = TT if b == 0 else M
                act.wait_ge(x1T_ps, b + 1)
                A(x1T[:, :], at_[:, 0, 0:T], ACT.Copy).then_inc(x1T_ready, 1)
                act.wait_ge(q_ps, b + 1)
                A(QT[0:DV, :, :], at_[0:DV, :, :].rearrange("p a (h t) -> p (a h) t", t=T), ACT.Copy,
                  scale=SCALE).then_inc(q_ready, 1)

            act.wait_ge(ld_cols, 16)
            A(a_neg[:, :], cols[:, COLS["a_log"][0]:COLS["a_log"][1]], ACT.Exp).then_inc(a_exp, 1)
            normed(0)
            silus(0)
            softplus(0)
            act.wait_ge(ld_ident, 32)
            A(sel[:, :], sel_c[:, :], ACT.Copy).then_inc(params_ready, 1)
            act.wait_ge(consts_set, 1)
            for b in range(B):
                decays(b, 0)
                decays(b, 1)
                if b + 1 < B:
                    normed(b + 1)
                else:
                    kernel(0)
                    kernel(1)
                    act.wait_ge(wqk_ps, 1)
                    A(wqk, TT[:, 0, 0:NH * DV].rearrange("p (h e) -> p h e", h=NH), ACT.Copy).then_inc(wqk_ready, 1)
                if b == 0:
                    act.wait_ge(s4_sin_in, 1)
                    A(sv[4], sv[4], ACT.Sin, scale=TWO_PI)
                    A(sv[5], sv[5], ACT.Sin, scale=TWO_PI)
                    A(sv[6], sv[6], ACT.Sin, scale=TWO_PI / 2)
                    A(sv[7], sv[1], ACT.Tanh, scale=0.5).then_inc(s4_sin, 1)
                if b + 1 < B:
                    silus(b + 1)
                decays(b, 2)
                if b + 1 < B:
                    softplus(b + 1)
                decays(b, 3)
                if b == 0:
                    act.wait_ge(s4_arg, 2)
                    A(w_exp, w_exp, ACT.Exp).then_inc(s4_fun, 1)
                    A(u_exp, u_exp, ACT.Exp).then_inc(s4_fun, 1)
                if b == 1:
                    act.wait_ge(s4_th_in, 2)
                    A(w_ph, w_ph, ACT.Sin, scale=TWO_PI).then_inc(s4_fun, 1)
                    A(u_ph, u_ph, ACT.Sin, scale=TWO_PI).then_inc(s4_fun, 1)
                    A(u_ph2, u_ph2, ACT.Sin, scale=TWO_PI).then_inc(s4_fun, 1)

            def evacuate(g):
                t, k = divmod(g, NH)
                if t >= 2:
                    act.wait_ge(added, 3 * (t - 2) + (1 if k < 2 else 3))
                act.wait_ge(s_ps, 4 * g + 2)
                A(s[:, t % 2, k, 0:1024], S[:, 0:1024], ACT.Copy).then_inc(s_ready, 1)
                act.wait_ge(s_ps, 4 * g + 4)
                A(s[:, t % 2, k, 1024:G], S[:, 1024:G], ACT.Copy).then_inc(s_ready, 1)

            def count(g):
                t, k = divmod(g, NH)
                act.wait_ge(top_found, g + 1)
                if t:
                    act.wait_ge(flags_ready, t)
                if g:
                    act.wait_ge(counted, g)
                A(junk, s[:, t % 2, k, :], ACT.Sign, scale=-1.0, bias=top[:, t % 2, k, TOPK - 1:TOPK],
                  accum_out=counts[:, k:k + 1]).then_inc(counted, 1)

            def exp_top(t):
                act.wait_ge(top_ready, t + 1)
                A(etop[:, :, :], etop[:, :, :], ACT.Exp).then_inc(etop_ready, 1)

            def log_sums(t):
                act.wait_ge(ssum_ready, t + 1)
                A(lnsum[:, :], ssum[:, :], ACT.Ln, scale=float(NH)).then_inc(lnsum_ready, 1)

            def exponents(t, k):
                act.wait_ge(ebias_ready, t + 1)
                if NH * t + k >= 2:
                    act.wait_ge(masked_ready, NH * t + k - 1)
                A(prob[:, k % 2, :], s[:, t % 2, k, :], ACT.Exp, bias=ebias[:, k:k + 1]).then_inc(prob_ready, 1)

            def turned(t):
                if t >= 1:
                    act.wait_ge(c_ps, t)
                for g in range(4):
                    act.wait_ge(aT_ps, 4 * t + g + 1)
                    w = min(4, GC - 4 * g)
                    rows_ = P if w == 4 else GL
                    A(aT[0:rows_, 4 * g:4 * g + w, :], M[0:rows_, g % 2, 0:w * P].rearrange("p (g d) -> p g d", d=P),
                      ACT.Copy).then_inc(aT_ready, 1)

            def context(t):
                act.wait_ge(c_ps, t + 1)
                if t >= 2 and t % R == 0:
                    act.wait_ge(film_ps, t // R)
                A(cT[:, t % R * P:(t % R + 1) * P], M[:, 0, 0:P], ACT.Copy).then_inc(c_ready, 1)

            def tail(b, i):
                if i == 3:
                    act.wait_ge(n3T_ps, b + 1)
                    A(hT[:, :], TT[:, 0, 0:T], ACT.Identity, scale=col("ffn_g"), bias=col("ffn_b")).then_inc(hT_ready, 1)
                    for f in range(FT):
                        act.wait_ge(h1_ps, FT // 2 * b + f // 2 + 1)
                        A(gT[:, f, :], TT[:, 1 - f // 2, (f % 2) * T:(f % 2 + 1) * T], ACT.Gelu,
                          bias=col("ffn_b1", f)).then_inc(gT_ready, 1)
                if i == 4:
                    act.wait_ge(x2T_ps, b + 1)
                    A(x2T[:, :], TT[:, 0, 0:T], ACT.Copy).then_inc(x2T_ready, 1)
                for e in HIDDEN.get(i, ()):
                    if e >= 2:
                        act.wait_ge(eo_ps, NE * b + e - 1)
                    for f in range(FT):
                        act.wait_ge(eh_ps, FT // 2 * (NE * b + e) + f // 2 + 1)
                        A(gm[:, e % 2, f, :], TT[:, f // 2, (f % 2) * T:(f % 2 + 1) * T], ACT.Gelu,
                          bias=col("moe_b1", FT * e + f)).then_inc(eg_ready, 1)
                if i == 6:
                    act.wait_ge(wdT_ps, b + 1)
                    A(wdT[:, :], M[0:NE, 1, 0:T], ACT.Copy).then_inc(wdT_ready, 1)

            queries(0)
            act.wait_ge(hc_ready, CH * NU * B)
            evacuate(0)
            act.wait_ge(yv_ready, B)
            evacuate(1)
            for g in range(END):
                t, k = divmod(g, NH)
                if k == 0 and 1 <= t <= B * R:
                    count(g - 1)
                if k == 1 and 1 <= t <= B * R:
                    exp_top(t - 1)
                for b, i in tails_at(g):
                    if i == 5:
                        act.wait_ge(wexp_in, b + 1)
                        A(wtop[:, :, 1], wtop[:, :, 0], ACT.Exp).then_inc(wexp_out, 1)
                if k == NH - 1 and g < TILES:
                    for h in (3, 2, 1):
                        count(g - h)
                if g + AHEAD < TILES and k != 2:
                    evacuate(g + AHEAD)
                if queries_at(g):
                    queries(t // R + 1)
                if k == 1 and 1 <= t <= B * R:
                    log_sums(t - 1)
                if 1 <= t <= B * R:
                    if k == 1:
                        exponents(t - 1, 0)
                        exponents(t - 1, 1)
                    if k == 2:
                        exponents(t - 1, 2)
                        exponents(t - 1, 3)
                if g + AHEAD < TILES and k == 2:
                    evacuate(g + AHEAD)
                if mean_at(g) is not None:
                    turned(mean_at(g))
                    context(mean_at(g))
                for b, i in tails_at(g):
                    if (b, i) == (B - 1, 0):
                        turned(B * R - 1)
                        context(B * R - 1)
                    tail(b, i)
                if values_at(g):
                    for q in range(4):
                        act.wait_ge(v_ps, 4 * (t // R) + q + 1)
                        w = min(4, GC - 4 * q)
                        rows_ = P if w == 4 else GL
                        A(V[0:rows_, 4 * q:4 * q + w, :], M[0:rows_, q % 2, 0:w * D].rearrange("p (g d) -> p g d", d=D),
                          ACT.Copy).then_inc(v_ready, 1)

        @block.tensor
        def _(pe):
            mm = nc.tensor.matmul

            def normed(b):
                pe.wait_ge(xn_ready, b + 1)
                if b >= 1:
                    pe.wait_ge(sp_ready, b)
                for r in range(R):
                    ins = nc.tensor.transpose(TT[:, 0, r * P:(r + 1) * P], xn[:, r, :], ident[:, :])
                ins.then_inc(xnT_ps, 1)
                pe.wait_ge(xnT_ready, b + 1)
                if b >= 1:
                    pe.wait_ge(parts_ready, b)
                for c in range(CH):
                    for j in range(KC):
                        ins = mm(TT[:, 0, c * T + j:(c + 1) * T], wconv[:, j, c, :], xnT[:, 0:T - j], start=(j == 0),
                                 stop=(j == KC - 1))
                ins.then_inc(xz_ps, 1)
                for c in range(CH):
                    ins = mm(TT[:, 1, c * T:(c + 1) * T], wt("w_in", CH + c, P), xnT, start=True, stop=True)
                ins.then_inc(xz_ps, 1)

            def projected(b):
                pe.wait_ge(xc_ready, b + 1)
                for c in range(CH):
                    ins = mm(TT[:, 0, T:2 * T], wt("wx_raw", c, P), xc[:, b % 2, c, :], start=(c == 0), stop=(c == CH - 1))
                ins.then_inc(ssm_ps, 1)
                pe.wait_ge(sz_ready, b + 1)
                for c in range(CH):
                    ins = mm(TT[0:96, 1, 0:T], wt("wx_bc", c, 96), xc[:, b % 2, c, :], start=(c == 0), stop=(c == CH - 1))
                ins.then_inc(ssm_ps, 1)

            def spread(b, u):
                if u == 0:
                    pe.wait_ge(parts_ready, b + 1)
                for which, used in ((0, b_used), (1, c_used)):
                    if NU * b + u >= 1:
                        pe.wait_ge(used, NU * b + u)
                    for j in range(UN):
                        i = which * NS + UN * u + j
                        ins = mm(S[:, which * 1024 + j * T:which * 1024 + (j + 1) * T], sel[:, i:i + 1].to_broadcast([96, P]),
                                 parts[:, b % 2, :], start=True, stop=True)
                    ins.then_inc(bc_ps, 1)

            def state_sum(b, u):
                if u == 0 and b >= 1:
                    pe.wait_ge(res_ready, b)
                for c in range(CH):
                    pe.wait_ge(hc_ready, CH * (NU * b + u) + c + 1)
                    for j in range(UN):
                        ins = mm(M[:, c, 0:T], ident[:, :], hst[:, u % 2, c, j, :], start=(u + j == 0),
                                 stop=(u == NU - 1 and j == UN - 1))
                    ins.then_inc(y_sum, 1)

            def out_projected(b):
                pe.wait_ge(yv_ready, b + 1)
                for r in range(R):
                    for c in range(CH):
                        ins = mm(M[:, 0, T + r * D:T + (r + 1) * D], yv[:, c, r * P:(r + 1) * P], wt("w_out", c, D),
                                 start=(c == 0), stop=(c == CH - 1))
                ins.then_inc(op_ps, 1)

            def s4_kernel(h):
                if h == 0:
                    pe.wait_ge(s4_mats, 1)
                    pe.wait_ge(sp_ready, B)
                    pe.wait_ge(parts_ready, B)
                    pe.wait_ge(xc_ready, B)
                    pe.wait_ge(sz_ready, B)
                else:
                    pe.wait_ge(k16_sb, 1)
                for d in range(h * D // 2, (h + 1) * D // 2):
                    at_ = (d - h * D // 2) * L16
                    ins = mm(TT[0:L16, at_ // 512, at_ % 512:at_ % 512 + L16], u_ph[:, :, d], w_ph[:, :, d], start=True, stop=True)
                ins.then_inc(k16_ps, 1)

            def s4_spectrum():
                pe.wait_ge(wqk_ready, 1)
                pe.wait_ge(kT_ready, 1)
                pe.wait_ge(ld_dft, 32)
                for j, cols_ in enumerate(((0, 1), (4, 3), (5, 1))):
                    for q in range(2):
                        for r in range(R):
                            ins = mm(TT[:, j // 2, (j % 2) * 256 + q * D:(j % 2) * 256 + (q + 1) * D],
                                     dft[:, r, cols_[q], :], kT[:, r, :], start=(r == 0), stop=(r == R - 1))
                ins.then_inc(kf_ps, 1)

            def queries(b):
                at_ = TT if b == 0 else M
                if b == 0:
                    pe.wait_ge(kf_ready, 1)
                pe.wait_ge(x1_ready, b + 1)
                if outs[0]:
                    pe.wait_ge(eo_used, outs[0])
                for q in range(R):
                    ins = nc.tensor.transpose(at_[:, 0, q * P:(q + 1) * P], xs_[:, b, q, :], ident[:, :])
                ins.then_inc(x1T_ps, 1)
                pe.wait_ge(x1T_ready, b + 1)
                for h in range(NH):
                    ins = mm(at_[0:DV, h // 2, h % 2 * T:(h % 2 + 1) * T], wqk[:, h, :], x1T[:, :], start=True, stop=True)
                ins.then_inc(q_ps, 1)
                pe.wait_ge(q_ready, b + 1)

            def scores(g):
                t, k = divmod(g, NH)
                b, r = divmod(t, R)
                if k == 0 and r == 0:
                    pe.wait_ge(q_ready, b + 1)
                    pe.wait_ge(pen_ready, b + 1)
                for q in range(4):
                    w = min(512, G - 512 * q)
                    if g:
                        pe.wait_ge(s_ready, 2 * g - (1 if q < 2 else 0))
                    mm(S[:, 512 * q:512 * q + w], QT[:, k, r * P:(r + 1) * P], ctxT[:, b % 2, 512 * q:512 * q + w],
                       start=True, stop=True).then_inc(s_ps, 1)

            outs = [0]
            pe.wait_ge(ld_ident, 32)
            pe.wait_ge(ld_w, 16)
            pe.wait_ge(wconv_ready, 1)
            normed(0)
            projected(0)
            pe.wait_ge(params_ready, 1)
            spread(0, 0)
            for b in range(B):
                for u in range(NU):
                    if u == 2 and b + 1 < B:
                        projected(b + 1)
                    if u + 1 < NU:
                        spread(b, u + 1)
                    elif b + 1 < B:
                        spread(b + 1, 0)
                    if b == B - 1:
                        if u == 0:
                            s4_kernel(1)
                        if u == 1:
                            pe.wait_ge(k16_sb, 2)
                            pe.wait_ge(ld_small, 64)
                            mm(TT[:, 0, 0:NH * DV], wt("wq", 0, D), wkb, start=True, stop=True).then_inc(wqk_ps, 1)
                        if u == 3:
                            queries(0)
                    state_sum(b, u)
                    if b == B - 1 and u == 1:
                        s4_spectrum()
                    if u == 0 and b + 1 < B:
                        normed(b + 1)
                    if b == B - 2 and u == NU - 1:
                        s4_kernel(0)
                if b == B - 1:
                    scores(0)
                out_projected(b)
            scores(1)

            def values(b):
                if b == 0:
                    pe.wait_ge(res_ready, B)
                if outs[0]:
                    pe.wait_ge(eo_used, outs[0])
                for g in range(4):
                    if g >= 2:
                        pe.wait_ge(v_ready, 4 * b + g - 1)
                    for i in range(4 * g, min(4 * g + 4, GC)):
                        w = P if i < GC - 1 else GL
                        ins = mm(M[0:w, g % 2, (i % 4) * D:(i % 4 + 1) * D], ctxT[0:DV, b % 2, i * P:i * P + w], wv[:, :],
                                 start=True, stop=True)
                    ins.then_inc(v_ps, 1)
                pe.wait_ge(v_ready, 4 * b + 4)

            def mean_turned(t):
                if outs[0]:
                    pe.wait_ge(eo_used, outs[0])
                pe.wait_ge(added, 3 * (t + 1))
                for g in range(4):
                    if g >= 2:
                        pe.wait_ge(aT_ready, 4 * t + g - 1)
                    for i in range(4 * g, min(4 * g + 4, GC)):
                        w = P if i < GC - 1 else GL
                        ins = nc.tensor.transpose(M[0:w, g % 2, (i % 4) * P:(i % 4 + 1) * P],
                                                  avg[:, i * P:i * P + w], ident[:, :])
                    ins.then_inc(aT_ps, 1)
                pe.wait_ge(aT_ready, 4 * (t + 1))
                for i in range(GC):
                    w = P if i < GC - 1 else GL
                    ins = mm(M[:, 0, 0:P], V[0:w, i, :], aT[0:w, i, :], start=(i == 0), stop=(i == GC - 1))
                ins.then_inc(c_ps, 1)
                pe.wait_ge(c_ready, t + 1)

            def tail(b, i):
                if i == 0:
                    if b == 0:
                        pe.wait_ge(kf_ready, 1)
                        pe.wait_ge(params_ready, 2)
                    if b >= 1:
                        pe.wait_ge(eg_ready, FT * NE * b)
                    for j, name in enumerate(("film_in", "film_out")):
                        for r in range(R):
                            ins = mm(TT[:, j, r * T:(r + 1) * T], cT[:, r * P:(r + 1) * P], wt(name, 0, 2 * D), start=True, stop=True)
                    ins.then_inc(film_ps, 1)
                if i == 1:
                    pe.wait_ge(xs_ready, b + 1)
                    for q in range(4):
                        for r in range(R):
                            ins = mm(TT[:, 0, q * D:(q + 1) * D], dft[:, r, q, :], n2[:, r, :], start=(r == 0), stop=(r == R - 1))
                    ins.then_inc(xf_ps, 1)
                if i == 2:
                    pe.wait_ge(Y_ready, b + 1)
                    for r in range(R):
                        for q in range(4):
                            ins = mm(TT[:, 1, r * D:(r + 1) * D], idft[:, q, r * P:(r + 1) * P], Y[:, q, :],
                                     start=(q == 0), stop=(q == 3))
                    ins.then_inc(y_ps, 1)
                if i == 3:
                    pe.wait_ge(n3_ready, b + 1)
                    for r in range(R):
                        ins = nc.tensor.transpose(TT[:, 0, r * P:(r + 1) * P], n2[:, r, :], ident[:, :])
                    ins.then_inc(n3T_ps, 1)
                    pe.wait_ge(hT_ready, b + 1)
                    for f in range(FT):
                        ins = mm(TT[:, 1 - f // 2, (f % 2) * T:(f % 2 + 1) * T], wt("w1", f, P), hT[:, :], start=True, stop=True)
                        if f % 2:
                            ins.then_inc(h1_ps, 1)
                    pe.wait_ge(gT_ready, FT * (b + 1))
                    for r in range(R):
                        for f in range(FT):
                            ins = mm(TT[:, 1, r * D:(r + 1) * D], gT[:, f, r * P:(r + 1) * P], wt("w2", f, D),
                                     start=(f == 0), stop=(f == FT - 1))
                    ins.then_inc(h2_ps, 1)
                if i == 4:
                    pe.wait_ge(x2_ready, b + 1)
                    for r in range(R):
                        ins = nc.tensor.transpose(TT[:, 0, r * P:(r + 1) * P], x2[:, r, :], ident[:, :])
                    ins.then_inc(x2T_ps, 1)
                    pe.wait_ge(x2T_ready, b + 1)
                    for r in range(R):
                        ins = mm(M[:, 1, r * NE:(r + 1) * NE], x2T[:, r * P:(r + 1) * P], wt("router", 0, NE), start=True, stop=True)
                    ins.then_inc(lg_ps, 1)
                    if b == 0:
                        pe.wait_ge(ld_moe, 48)
                if i == 7:
                    pe.wait_ge(wdT_ready, b + 1)
                    for r in range(R):
                        ins = mm(M[:, 1, r * D:(r + 1) * D], wdT[:, r * P:(r + 1) * P], moe_b2[:, :], start=True, stop=True)
                    ins.then_inc(mb_ps, 1)
                hidden, outputs = list(HIDDEN.get(i, ())), list(OUTPUTS.get(i, ()))
                while hidden or outputs:
                    if hidden:
                        expert_hidden(b, hidden.pop(0))
                    if outputs:
                        expert_out(b, outputs.pop(0))
                if i == 6:
                    pe.wait_ge(wd_ready, b + 1)
                    for r in range(R):
                        ins = nc.tensor.transpose(M[0:NE, 1, r * P:(r + 1) * P], wd[:, r, :], ident[:, :])
                    ins.then_inc(wdT_ps, 1)

            def expert_hidden(b, e):
                for f in range(FT):
                    if e >= 1 and f % 2 == 0:
                        pe.wait_ge(eg_ready, FT * (NE * b + e - 1) + f + 2)
                    ins = mm(TT[:, f // 2, (f % 2) * T:(f % 2 + 1) * T], moe_w1[:, e, f, :], x2T[:, :],
                             start=True, stop=True)
                    if f % 2:
                        ins.then_inc(eh_ps, 1)

            def expert_out(b, e):
                pe.wait_ge(eg_ready, FT * NE * b + FT * (e + 1))
                if outs[0] and e % 2 == 0:
                    pe.wait_ge(eo_used, outs[0])
                for r in range(R):
                    for f in range(FT):
                        ins = mm(M[:, 0, (R * (e % 2) + r) * D:(R * (e % 2) + r + 1) * D], gm[:, e % 2, f, r * P:(r + 1) * P],
                                 moe_w2[:, e, f, :], start=(f == 0), stop=(f == FT - 1))
                ins.then_inc(eo_ps, 1)
                outs[0] += 1

            for g in range(END):
                t, k = divmod(g, NH)
                if g + AHEAD < TILES:
                    scores(g + AHEAD)
                if mean_at(g) is not None:
                    mean_turned(mean_at(g))
                if queries_at(g):
                    queries(t // R + 1)
                for b, i in tails_at(g):
                    if (b, i) == (B - 1, 0):
                        mean_turned(B * R - 1)
                    tail(b, i)
                if values_at(g):
                    values(t // R)

        @block.vector
        def _(dve):
            n = [0]
            nln = [0]

            def link(ins, wait=True, meanwhile=None):
                n[0] += 1
                here = n[0]
                ins.then_inc(dve_step, 1)
                if meanwhile is not None:
                    meanwhile()
                if wait:
                    dve.wait_ge(dve_step, here)

            TS, TTN, STT = nc.vector.tensor_scalar, nc.vector.tensor_tensor, nc.vector.scalar_tensor_tensor

            def variance(k, src):
                for r in range(R):
                    link(nc.vector.bn_stats(stat[:, k, r, :], src[:, r, :]), r == R - 1)
                for r in range(R):
                    ins = nc.vector.bn_aggr(mv[:, k, r, :], stat[:, k, r, :])
                    if r < R - 1:
                        link(ins, False)
                ins.then_inc(var_ready, 1)

            def normalise(k, dst, src):
                nln[0] += 1
                dve.wait_ge(rstd_ready, nln[0])
                for r in range(R):
                    link(TS(dst[:, r, :], src[:, r, :], mv[:, k, r, 0:1], rstd[:, k, r:r + 1], ALU.subtract, ALU.mult), r == R - 1)

            def layernorm(k, dst, src):
                variance(k, src)
                if now[0] + 2 < TILES:
                    segment_max(now[0] + 2, min(8, 11 - segments[now[0] + 2]))
                normalise(k, dst, src)

            def normed(b):
                normalise(0, xn, xs_[:, b])
                dve.sem_inc(xn_ready, 1)

            def bc_parts(b):
                p_ = parts[:, b % 2, :]
                dve.wait_ge(bc_hi, b + 1)
                link(TTN(bc_r[:, :], TT[0:96, 1, 0:T], p_, ALU.subtract))
                link(nc.vector.tensor_copy(bc_m[:, :], bc_r[:, :]))
                link(TTN(bc_r[:, :], bc_r[:, :], bc_m[:, :], ALU.subtract), False)
                link(nc.vector.tensor_copy(p_[32:64, :], bc_m[32:64, :]))
                nc.vector.tensor_copy(p_[64:96, :], bc_r[64:96, :]).then_inc(parts_ready, 1)

            def softplus(b):
                dve.wait_ge(sp_ready, b + 1)
                link(TS(sp_q, sp_a, C1[-1], None, ALU.mult))
                for c_ in C1[-2::-1]:
                    link(STT(out=sp_q, in0=sp_q, scalar=c_, in1=sp_a, op0=ALU.add, op1=ALU.mult))
                link(TTN(dt_[:, b % 2], sp_q, sp_p, ALU.add))
                dve.sem_inc(dt_ready, 1)
                link(TTN(ux[:, b % 2], dt_[:, b % 2], xc[:, b % 2], ALU.mult))

            def unit(b, u):
                half_b, half_c = (S[:, i * 1024:(i + 1) * 1024].rearrange("p (n t) -> p n t", n=UN) for i in range(2))
                gu = NU * b + u
                dve.wait_ge(bc_ps, 2 * gu + 1)
                for c in range(CH):
                    if gu >= 2:
                        dve.wait_ge(y_sum, CH * (gu - 2) + c + 1)
                    link(TTN(hst[:, u % 2, c, :, :], ux[:, b % 2, c, :].unsqueeze(1).to_broadcast([P, UN, T]), half_b, ALU.mult),
                         c == CH - 1)
                dve.sem_inc(b_used, 1)
                for c in range(CH):
                    dve.wait_ge(abar_ready, CH * gu + c + 1)
                    hf = hst[:, u % 2, c, :, :].rearrange("p n t -> p (n t)")
                    nc.vector.tensor_tensor_scan(hf, abar[:, u % 2, c, :, :].rearrange("p n t -> p (n t)"), hf, 0.0,
                                                 ALU.mult, ALU.add).then_inc(scan_done, 1)
                dve.wait_ge(bc_ps, 2 * gu + 2)
                for c in range(CH):
                    dve.wait_ge(scan_done, CH * gu + c + 1)
                    TTN(hst[:, u % 2, c, :, :], hst[:, u % 2, c, :, :], half_c, ALU.mult).then_inc(hc_ready, 1)
                dve.wait_ge(hc_ready, CH * (gu + 1))
                dve.sem_inc(c_used, 1)

            def gated(b):
                dve.wait_ge(y_sum, CH * NU * (b + 1))
                dve.wait_ge(sz_ready, b + 1)
                for c in range(CH):
                    link(STT(out=yv[:, c, :], in0=xc[:, b % 2, c, :], scalar=col("d_param", c), in1=M[:, c, 0:T],
                             op0=ALU.mult, op1=ALU.add), c == CH - 1)
                link(TTN(yv, yv, sz[:, b % 2], ALU.mult))
                dve.sem_inc(yv_ready, 1)

            def residual(b):
                dve.wait_ge(op_ps, b + 1)
                link(STT(out=xs_[:, b], in0=xs_[:, b], scalar=2.0, in1=M[:, 0, T:2 * T].rearrange("p (r d) -> p r d", r=R),
                         op0=ALU.mult, op1=ALU.add))
                dve.sem_inc(res_ready, 1)
                variance(1, xs_[:, b])

            def residual_done(b):
                normalise(1, xs_[:, b], xs_[:, b])
                dve.sem_inc(x1_ready, 1)

            dve.wait_ge(ld_cols, 16)
            dve.wait_ge(ld_x, 16)
            variance(0, xs_[:, 0])
            normed(0)
            dve.wait_ge(ld_w, 16)
            dve.wait_ge(ld_conv, 16)
            link(TTN(wconv, wconv, wt("w_in", 0, CH * P).rearrange("p (c m) -> p c m", c=CH).unsqueeze(1)
                     .to_broadcast([P, KC, CH, P]), ALU.mult))
            dve.sem_inc(wconv_ready, 1)
            dve.wait_ge(a_exp, 1)
            link(TS(a_neg[:, :], a_neg[:, :], -1.0, None, ALU.mult), False)

            turn, are, dts, r_, sinb, cosb, sinh, th, k_, g_, gx, gy = sv
            LN2H = float(np.float32(0.693359375))
            LN2L = float(np.float32(np.log(2.0) - 0.693359375))

            def less_whole(dst, src, tmp, add=None):
                if add is not None:
                    link(TS(dst, src, add, None, ALU.add))
                    src = dst
                link(TS(tmp, src, MAGIC, MAGIC, ALU.add, ALU.subtract))
                link(TTN(dst, src, tmp, ALU.subtract))

            def s4_steps():
                ldt = row("log_dt")
                dve.wait_ge(ld_rows, 16)
                dve.wait_ge(ld_s4, 96)
                link(TS(k_, ldt, float(np.log2(np.e)), MAGIC, ALU.mult, ALU.add))
                link(TS(k_, k_, MAGIC, None, ALU.subtract))
                link(STT(out=r_, in0=k_, scalar=-LN2H, in1=ldt, op0=ALU.mult, op1=ALU.add))
                link(STT(out=r_, in0=k_, scalar=-LN2L, in1=r_, op0=ALU.mult, op1=ALU.add))
                fact = [1.0 / 5040, 1.0 / 720, 1.0 / 120, 1.0 / 24, 1.0 / 6, 0.5, 1.0]
                link(TS(g_, r_, fact[0], None, ALU.mult))
                for c_ in fact[1:]:
                    link(STT(out=g_, in0=g_, scalar=c_, in1=r_, op0=ALU.add, op1=ALU.mult))
                link(TS(g_, g_, 1.0, None, ALU.add))
                link(TS(k_, k_, 127.0, 0.0, ALU.add, ALU.max))
                link(TS(ki[:, :], k_, 254.0, 2.0 ** 23, ALU.min, ALU.mult))
                link(TTN(dts, g_, ki[:, :].bitcast(F32), ALU.mult))
                link(TTN(are, dts, a_re, ALU.mult), False)
                link(TTN(turn, dts, a_im, ALU.mult))
                link(TS(turn, turn, float(1.0 / (2 * np.pi)), None, ALU.mult))
                less_whole(turn, turn, k_)
                dve.sem_inc(s4_small, 1)
                link(nc.vector.tensor_copy(sinb, turn), False)
                link(nc.vector.tensor_copy(sinh, turn), False)
                less_whole(cosb, turn, k_, 0.25)
                dve.sem_inc(s4_sin_in, 1)
                link(TS(c_2[64:128, :], c_2[64:128, :], -1.0, None, ALU.mult), False)

            def s4_gains():
                dve.wait_ge(s4_sin, 1)
                link(TS(k_, th, -1.0, 1.0, ALU.mult, ALU.add))
                link(nc.vector.reciprocal(k_, k_))
                link(STT(out=th, in0=th, scalar=2.0, in1=k_, op0=ALU.mult, op1=ALU.mult))
                link(TTN(cosb, th, cosb, ALU.mult), False)
                link(TTN(sinh, sinh, sinh, ALU.mult))
                link(STT(out=gx, in0=sinh, scalar=-2.0, in1=cosb, op0=ALU.mult, op1=ALU.add))
                link(STT(out=gy, in0=th, scalar=1.0, in1=sinb, op0=ALU.add, op1=ALU.mult))
                link(TTN(k_, a_re, a_re, ALU.mult), False)
                link(TTN(dts, a_im, a_im, ALU.mult))
                link(TTN(k_, k_, dts, ALU.add))
                link(nc.vector.reciprocal(k_, k_))
                link(TTN(r_, gx, a_re, ALU.mult), False)
                link(TTN(dts, gy, a_im, ALU.mult))
                link(TTN(r_, r_, dts, ALU.add))
                link(STT(out=r_, in0=r_, scalar=2.0, in1=k_, op0=ALU.mult, op1=ALU.mult))
                link(TTN(g_, gy, a_re, ALU.mult), False)
                link(TTN(dts, gx, a_im, ALU.mult))
                link(TTN(g_, g_, dts, ALU.subtract))
                link(STT(out=g_, in0=g_, scalar=2.0, in1=k_, op0=ALU.mult, op1=ALU.mult))
                link(TTN(gx, c_1, r_, ALU.mult), False)
                link(TTN(dts, c_2, g_, ALU.mult))
                link(TTN(gx, gx, dts, ALU.subtract))
                link(TTN(gy, c_1, g_, ALU.mult), False)
                link(TTN(dts, c_2, r_, ALU.mult))
                link(TTN(gy, gy, dts, ALU.add))
                dve.sem_inc(s4_gain, 1)

            s4_steps()
            link(nc.vector.memset(QT[DV:DV + 1, :, :], 1.0), False)
            softplus(0)
            bc_parts(0)
            for b in range(B):
                unit(b, 0)
                if b >= 1:
                    residual(b - 1)
                if b + 1 < B:
                    variance(0, xs_[:, b + 1])
                if b >= 1:
                    residual_done(b - 1)
                if b + 1 < B:
                    normed(b + 1)
                unit(b, 1)
                if b == 0:
                    s4_gains()
                if b == B - 1:
                    dve.wait_ge(k16_moved, 32)
                    link(TTN(kT[0:1, 0, :], kT[0:1, 0, :], dskip[:, :], ALU.add))
                    dve.sem_inc(kT_ready, 1)
                unit(b, 2)
                if b + 1 < B:
                    bc_parts(b + 1)
                else:
                    dve.wait_ge(kf_ps, 1)
                    for j in range(3):
                        link(nc.vector.tensor_copy(kf[:, j, :, :], TT[:, j // 2, (j % 2) * 256:(j % 2) * 256 + 256]
                                                   .rearrange("p (q d) -> p q d", q=2)))
                    dve.sem_inc(kf_ready, 1)
                unit(b, 3)
                if b + 1 < B:
                    softplus(b + 1)
                gated(b)

            def film_params():
                dve.wait_ge(ld_small, 64)
                gate = row("gate")
                for name in ("film_in", "film_out"):
                    link(TS(wt(name, 0, 2 * D), wt(name, 0, 2 * D), gate, None, ALU.mult), False)
                    rb = row(name + "_b")
                    link(TS(rb, rb, gate, None, ALU.mult))
                    link(TS(rb[:, 0:D], rb[:, 0:D], 1.0, None, ALU.add), False)
                link(nc.vector.tensor_copy(tmask[:, :, :].rearrange("p b r -> p (b r)"), tmask8[:, :]))
                dve.sem_inc(params_ready, 1)

            def flat(c_):
                return c_.rearrange("p n e -> p (n e)")

            segments = [0] * (TILES + AHEAD)

            def segment_max(g, n):
                if g >= TILES:
                    return
                t, k = divmod(g, NH)
                lo = segments[g]
                segments[g] = min(lo + n, NSEG)
                for q in range(lo, segments[g]):
                    if q in (0, 1024 // SEG):
                        dve.wait_ge(s_ready, 2 * g + (1 if q == 0 else 2))
                    end = G if q == NSEG - 1 else (q + 1) * SEG
                    link(nc.vector.max(cand[:, g % 2, q, :], s[:, t % 2, k, q * SEG:end]), q == NSEG - 1)

            def largest(g):
                t, k = divmod(g, NH)
                tk = top[:, t % 2, k, :]
                holes = [7]

                def next_chunk():
                    segment_max(g + 1, -(-(NSEG - segments[g + 1]) // holes[0]))
                    holes[0] -= 1

                src = flat(cand[:, g % 2])
                link(nc.vector.max(tk[:, 0:8], src), True, next_chunk)
                for j in range(1, 4):
                    link(nc.vector.match_replace(cand2[:, :], tk[:, 8 * j - 8:8 * j], src, LOWEST), True, next_chunk)
                    if j == 1 and k == 1 and t >= 1:
                        summed(t - 1)
                    src = cand2[:, :]
                    link(nc.vector.max(tk[:, 8 * j:8 * j + 8], src), True, next_chunk)
                assert segments[g + 1] == NSEG or g + 1 == TILES
                dve.sem_inc(top_found, 1)

            def summed(t):
                dve.wait_ge(etop_ready, t + 1)
                nc.vector.tensor_reduce(ssum[:, :], etop[:, :, :], AX, ALU.add).then_inc(ssum_ready, 1)

            def ties(t):
                if t:
                    dve.wait_ge(flags_ready, t)
                link(TTN(tie[:, :], top[:, t % 2, :, TOPK - 2], top[:, t % 2, :, TOPK - 1], ALU.subtract))
                TS(tie[:, :], tie[:, :], 0.0, -4.0 * G, ALU.is_equal, ALU.mult).then_inc(ties_ready, 1)

            def exact(t, k):
                sk = s[:, t % 2, k, :]
                src = sk
                for j in range(4):
                    nc.vector.max(top[:, t % 2, k, 8 * j:8 * j + 8], src)
                    dve.drain()
                    nc.vector.match_replace(scratch, top[:, t % 2, k, 8 * j:8 * j + 8], src, LOWEST)
                    dve.drain()
                    src = scratch
                TTN(scratch, scratch, sk, ALU.is_equal)
                dve.drain()
                STT(out=sk, in0=scratch, scalar=-PENALTY, in1=sk, op0=ALU.mult, op1=ALU.add)
                dve.drain()

            def checked(t):
                dve.wait_ge(flags_moved, 16 * (t + 1))
                link(nc.vector.tensor_reduce(headf[:, :], flagrow[:, :].rearrange("o (p k) -> o k p", k=NH), AX, ALU.min))
                link(TS(headf[:, :], headf[:, :], COUNTED - 0.5, None, ALU.is_lt))
                link(nc.vector.tensor_copy(headi[:, :], headf[:, :]), False)
                link(nc.vector.tensor_reduce(anyf[:, :], headf[:, :], AX, ALU.add))
                link(nc.vector.tensor_copy(anyi[:, :], anyf[:, :]))
                found = dve.value_load(anyi[0:1, 0:1], min_val=0, max_val=NH)
                with dve.If(found > 0):
                    for k in range(NH):
                        in_head = dve.value_load(headi[0:1, k:k + 1], min_val=0, max_val=1)
                        with dve.If(in_head > 0):
                            exact(t, k)
                if t >= 1:
                    dve.wait_ge(ssum_ready, t)
                    dve.wait_ge(ebias_ready, t)
                link(TS(ngmax[:, :], top[:, t % 2, :, 0], 4.0, -0.25, ALU.mult, ALU.mult))
                link(TTN(etop[:, :, :], top[:, t % 2], ngmax[:, :].unsqueeze(2).to_broadcast([P, NH, TOPK]), ALU.add))
                dve.sem_inc(top_ready, 1)

            def masked(t, k):
                dve.wait_ge(prob_ready, NH * t + k + 1)
                sk = s[:, t % 2, k, :]
                STT(out=sk, in0=sk, scalar=top[:, t % 2, k, TOPK - 1:TOPK], in1=prob[:, k % 2, :],
                    op0=ALU.is_ge, op1=ALU.mult).then_inc(masked_ready, 1)

            now = [0]

            def rowb(name):
                return row(name).unsqueeze(1).to_broadcast([P, R, D])

            def film(b):
                src = big if b == B - 1 else shared
                return [src[:, i * 512:(i + 1) * 512].rearrange("p (r d) -> p r d", r=R) for i in range(2)]

            def tail(b, i):
                x1 = xs_[:, b]
                if i == -1:
                    layernorm(2, n2, x1)
                    link(TTN(n2[:, :, :], n2[:, :, :], rowb("in_g"), ALU.mult))
                    link(TTN(n2[:, :, :], n2[:, :, :], rowb("in_b"), ALU.add), False)
                if i == 0:
                    dve.wait_ge(film_ps, b + 1)
                    fi, fo = film(b)
                    for dst, j, name in ((fi, 0, "film_in_b"), (fo, 1, "film_out_b")):
                        for r in range(R):
                            link(STT(out=dst[:, r, :], in0=TT[:, j, r * T:(r + 1) * T], scalar=tmask[:, b, r:r + 1],
                                     in1=row(name), op0=ALU.mult, op1=ALU.add), r == 1 and j == 1)
                    link(TTN(n2[:, :, :], n2[:, :, :], fi[:, :, 0:D], ALU.mult))
                    link(TTN(n2[:, :, :], n2[:, :, :], fi[:, :, D:2 * D], ALU.add))
                    dve.sem_inc(xs_ready, 1)
                    link(TTN(xt[:, :, :], x1, fo[:, :, D:2 * D], ALU.add))
                if i == 1:
                    dve.wait_ge(xf_ps, b + 1)
                    xre = TT[:, 0, 0:2 * D].rearrange("p (q d) -> p q d", q=2)
                    xim = TT[:, 0, 2 * D:4 * D].rearrange("p (q d) -> p q d", q=2)
                    for lo, ka, kb, op in ((0, 0, 1, ALU.subtract), (2, 1, 2, ALU.add)):
                        link(TTN(xf_a, xre, kf[:, ka, :, :], ALU.mult), False)
                        link(TTN(xf_b, xim, kf[:, kb, :, :], ALU.mult))
                        link(TTN(Y[:, lo:lo + 2, :], xf_a, xf_b, op))
                    dve.sem_inc(Y_ready, 1)
                if i == 2:
                    dve.wait_ge(y_ps, b + 1)
                    fo = film(b)[1]
                    link(TTN(fo[:, :, 0:D], TT[:, 1, 0:T].rearrange("p (r d) -> p r d", r=R), fo[:, :, 0:D], ALU.mult))
                    link(TTN(xt[:, :, :], xt[:, :, :], fo[:, :, 0:D], ALU.add))
                    layernorm(3, n2, xt)
                    dve.sem_inc(n3_ready, 1)
                    link(TTN(xt[:, :, :], xt[:, :, :], rowb("ffn_b2"), ALU.add))
                    link(TTN(x1, x1, rowb("out_b"), ALU.add), False)
                if i == 3:
                    dve.wait_ge(h2_ps, b + 1)
                    link(TTN(xt[:, :, :], TT[:, 1, 0:T].rearrange("p (r d) -> p r d", r=R), xt[:, :, :], ALU.add))
                    layernorm(4, n2, xt)
                    link(TTN(n2[:, :, :], n2[:, :, :], rowb("out_g"), ALU.mult))
                    link(TTN(n2[:, :, :], n2[:, :, :], x1, ALU.add))
                    layernorm(5, x2, n2)
                    dve.sem_inc(x2_ready, 1)
                if i == 4:
                    dve.wait_ge(lg_ps, b + 1)
                    link(TTN(lg[:, :, :], M[:, 1, 0:R * NE].rearrange("p (r e) -> p r e", r=R),
                             row("router_b").unsqueeze(1).to_broadcast([P, R, NE]), ALU.add))
                    for r in range(R):
                        link(nc.vector.max(lmax[:, r, :], lg[:, r, :]), r == R - 1)
                    for r in range(R):
                        link(nc.vector.max_index(lidx[:, r, :], lmax[:, r, :], lg[:, r, :]), r == R - 1)
                    link(nc.vector.tensor_copy(lidf[:, :, :], lidx[:, :, 0:2]), False)
                    link(TTN(wtop[:, :, 0], lmax[:, :, 1], lmax[:, :, 0], ALU.subtract))
                    dve.sem_inc(wexp_in, 1)
                if i == 5:
                    dve.wait_ge(wexp_out, b + 1)
                    link(TS(wtop[:, :, 2], wtop[:, :, 1], 1.0, None, ALU.add))
                    link(nc.vector.reciprocal(wtop[:, :, 2], wtop[:, :, 2]))
                    link(TTN(wtop[:, :, 3], wtop[:, :, 1], wtop[:, :, 2], ALU.mult))
                    for r in range(R):
                        link(TS(oh[:, r, 0, :], iota8[:, :], lidf[:, r, 0:1], wtop[:, r, 2:3], ALU.is_equal, ALU.mult), False)
                        link(TS(oh[:, r, 1, :], iota8[:, :], lidf[:, r, 1:2], wtop[:, r, 3:4], ALU.is_equal, ALU.mult), r == 1)
                    link(TTN(wd[:, :, :], oh[:, :, 0, :], oh[:, :, 1, :], ALU.add))
                    dve.sem_inc(wd_ready, 1)
                if i == 7:
                    dve.wait_ge(mb_ps, b + 1)
                    link(TTN(acc[:, :, :], M[:, 1, 0:T].rearrange("p (r d) -> p r d", r=R), acc[:, :, :], ALU.add))
                if i in OUTPUTS:
                    experts_added(b, OUTPUTS[i])
                if i == LAST:
                    if b >= 1:
                        dve.wait_ge(out_stored, 16 * b)
                    layernorm(6, outt, acc)
                    dve.sem_inc(out_ready, 1)

            def experts_added(b, pair):
                dve.wait_ge(eo_ps, NE * b + pair[-1] + 1)
                for e in pair:
                    for r in range(R):
                        link(STT(out=acc[:, r, :], in0=M[:, 0, (R * (e % 2) + r) * D:(R * (e % 2) + r + 1) * D],
                                 scalar=wd[:, r, e:e + 1], in1=x2[:, r, :] if e == 0 else acc[:, r, :],
                                 op0=ALU.mult, op1=ALU.add), r == 1)
                    dve.sem_inc(eo_used, 1)

            segment_max(0, NSEG)
            for g in range(END):
                now[0] = g
                t, k = divmod(g, NH)
                if g < TILES:
                    largest(g)
                    if k == NH - 1:
                        ties(t)
                    if g == 0:
                        residual(B - 1)
                        film_params()
                        residual_done(B - 1)
                early = k in (1, 2) and t % R == 1
                if early:
                    for b, i in tails_at(g):
                        tail(b, i)
                if 1 <= t <= B * R:
                    if k == 0:
                        checked(t - 1)
                    if k == 1:
                        if g >= TILES:
                            summed(t - 1)
                        masked(t - 1, 0)
                        masked(t - 1, 1)
                    if k == 2:
                        masked(t - 1, 2)
                        masked(t - 1, 3)
                        if t == B * R:
                            for h in (2, 3):
                                dve.wait_ge(masked_ready, NH * (t - 1) + h + 1)
                                dve.wait_ge(added, 3 * (t - 1) + h - 1)
                                TTN(avg[:, :], avg[:, :], s[:, (t - 1) % 2, h, :], ALU.add).then_inc(added, 1)
                for b, i in () if early else tails_at(g):
                    tail(b, i)


def dft_tables():
    t = np.arange(T)[:, None].astype(np.float64)
    k = np.arange(T)[None, :].astype(np.float64)
    ang = 2 * np.pi * t * k / NFFT
    re, im = np.cos(ang), -np.sin(ang)
    last = np.where(np.arange(T) % 2 == 0, 1.0, -1.0)
    im_last, re_last = im.copy(), re.copy()
    im_last[:, 0] = last
    re_last[:, 0] = last
    fwd = np.stack([re[:, :P], re[:, P:], im_last[:, :P], im[:, P:], im[:, :P], re_last[:, :P]], 1)
    fwd = fwd.reshape(R, P, 6, P).transpose(1, 0, 2, 3)
    w = np.full(T, 2.0)
    w[0] = 1.0
    ire, iim = (re * w).T / NFFT, (im * w).T / NFFT
    iim[0, :] = last / NFFT
    inv = np.concatenate([ire, iim], 0).reshape(4, P, T).transpose(1, 0, 2)
    return np.ascontiguousarray(fwd, np.float32), np.ascontiguousarray(inv, np.float32)


def heads_apart(w):
    out = np.zeros((NH, DH, NH, DV), w.dtype)
    for h in range(NH):
        out[h, :, h, :] = w[:, h * DH:(h + 1) * DH].T
    return out.reshape(NH * DH, NH * DV)


def layout(i):
    tiles = lambda v, n: v.reshape(n, P, -1).transpose(1, 0, 2).reshape(P, -1)
    cols = {"ln_g": i["L0_attn_ln_gamma"][:, None], "ln_b": i["L0_attn_ln_beta"][:, None],
            "conv_b": tiles(i["L0_attn_conv_b"], CH),
            "w_dt": tiles(i["L0_attn_w_dt"], CH), "b_dt": tiles(i["L0_attn_b_dt"], CH),
            "d_param": tiles(i["L0_attn_D_param"], CH), "a_log": tiles(i["L0_attn_A_log"], CH),
            "ffn_g": i["L0_xattn_g_ffn"][:, None], "ffn_b": i["L0_xattn_b_ffn"][:, None],
            "ffn_b1": tiles(i["L0_xattn_b1"], FT), "moe_b1": tiles(i["L0_ffn_b1"].reshape(-1), NE * FT)}
    rows = {"in_g": i["L0_xattn_g_norm_in"], "in_b": i["L0_xattn_b_norm_in"], "out_g": i["L0_xattn_g_norm_out"],
            "out_b": i["L0_xattn_b_norm_out"], "ffn_b2": i["L0_xattn_b2"], "film_in_b": i["L0_xattn_b_film_in"],
            "film_out_b": i["L0_xattn_b_film_out"], "router_b": i["L0_ffn_router_b"],
            "gate": i["L0_xattn_mod_gate"].reshape(1), "log_dt": i["L0_xattn_log_dt"]}
    wx = i["L0_attn_W_x"]
    wts = {"w_in": i["L0_attn_W_in"].T, "wx_bc": tiles(np.concatenate([wx[1:]] * 3, 0).T, CH),
           "wx_raw": tiles(np.repeat(wx[0:1], P, 0).T, CH), "w_out": tiles(i["L0_attn_W_out"].T, CH),
           "wq": i["L0_xattn_Wq"].T, "film_in": i["L0_xattn_W_film_in"], "film_out": i["L0_xattn_W_film_out"],
           "w1": i["L0_xattn_W1"], "w2": tiles(i["L0_xattn_W2"], FT), "router": i["L0_ffn_router_w"].T}
    fwd, inv = dft_tables()
    sel = (np.arange(96)[:, None] % 32 == np.arange(32)[None, :]).astype(np.float32)
    twice = lambda v: np.concatenate([v.T, v.T], 0)
    c_re, c_im = i["L0_xattn_C_re"].T, i["L0_xattn_C_im"].T
    return {
        "x": i["x"], "ctxT": i["ctx_768"].transpose(0, 2, 1), "gmask": i["mask_BxS2_bf1"],
        "tmask": i["mask_BxS_bf1"].reshape(B * R, P).T,
        "cols": np.concatenate([cols[n] for n in COLS], 1), "rows": np.concatenate([rows[n] for n in ROWS])[None, :],
        "wts": np.concatenate([wts[n] for n in WTS], 1),
        "wv": i["L0_xattn_Wv"], "wkb": heads_apart(i["L0_xattn_Wk"]), "ident": np.eye(P, dtype=np.float32),
        "conv": i["L0_attn_conv_w"].reshape(CH * P, KC).T[::-1].reshape(1, -1), "sel": sel, "dft": fwd, "idft": inv,
        "iota8": np.arange(NE, dtype=np.float32)[None, :],
        "moe_w1": i["L0_ffn_w1"].transpose(2, 0, 1).reshape(P, NE, FT, P),
        "moe_w2": i["L0_ffn_w2"].reshape(NE, D, FT, P).transpose(3, 0, 2, 1), "moe_b2": i["L0_ffn_b2"],
        "a_re": twice(i["L0_xattn_A_re"]), "a_im": twice(i["L0_xattn_A_im"]),
        "c_1": np.concatenate([c_re, c_im], 0), "c_2": np.concatenate([c_im, c_re], 0),
        "dskip": i["L0_xattn_D_skip"][None, :],
        "steps": np.concatenate([np.arange(L16), L16 * np.arange(L16)]).astype(np.float32)[None, :],
    }


def kernel(**inputs):
    import concourse.bacc as bacc
    from concourse.bass_utils import run_bass_kernel_spmd

    nc = bacc.Bacc("TRN2", target_bir_lowering=False, num_devices=1)
    arrays, args = {}, {}
    for name, v in layout({k: np.asarray(x) for k, x in inputs.items()}).items():
        v = np.ascontiguousarray(v)
        if v.dtype == np.bool_:
            v = v.view(np.uint8)
        arrays[f"in_{name}"] = v
        args[name] = nc.dram_tensor(f"in_{name}", v.shape, mybir.dt.from_np(v.dtype), kind="ExternalInput").ap()
    args["out"] = nc.dram_tensor("out_x", (B, T, D), F32, kind="ExternalOutput").ap()
    build(nc, args)
    r = run_bass_kernel_spmd(nc, [arrays], core_ids=[0])
    return r.results[0]["out_x"]
```
